# Optimizing a Trainium2 kernel written in Bass

```python
import numpy as np
import jax
import jax.numpy as jnp

def _softmax(x, axis=-1):
    return jax.nn.softmax(x, axis=axis)

def _gelu(x):
    return jax.nn.gelu(x, approximate=True)

def _silu(x):
    return jax.nn.silu(x)

def _sigmoid(x):
    return jax.nn.sigmoid(x)

def _layernorm(x, axis=-1, eps=1e-05):
    m = jnp.mean(x, axis=axis, keepdims=True)
    v = jnp.var(x, axis=axis, keepdims=True)
    return (x - m) / jnp.sqrt(v + eps)

def _scatter_add(tgt, idx, src, axis=0):
    return tgt.at[idx].add(src)

def _segment_sum(src, seg, n):
    return jax.ops.segment_sum(src, seg, n)
kernel_name = 'mk_vit_tower_postln_d1_tok_img768_r4_7d75a7'

def setup_inputs(seed: int=0):
    np.random.seed(seed)
    _w = jnp.asarray

    def _rec_inputs():
        import jax
        import jax.numpy as jnp
        _rk = jax.random.key(seed)
        x = 7.57192e-06 + 1.00007 * jax.random.normal(jax.random.fold_in(_rk, 1), (64, 3, 224, 224), jnp.float32)
        return x
    x = _rec_inputs()

    def _L0_tok_setup():
        import jax, jax.numpy as jnp
        import numpy as np
        IMAGE_SIZE = 224
        NUM_CHANNELS = 3
        NUM_BINS = 16
        EMBED_DIM = 192
        FILTER_SIZE = 96
        CROP = 2 * FILTER_SIZE
        BIN_SIZE = CROP * CROP // NUM_BINS
        IN_FEATURES = NUM_CHANNELS * BIN_SIZE
        SEQ_LEN = NUM_BINS + 1

        def _sorted_radial_indices(H, W):
            y, x = np.meshgrid(np.arange(H), np.arange(W), indexing='ij')
            d = np.sqrt((x - W / 2.0) ** 2 + (y - H / 2.0) ** 2).reshape(-1)
            return jnp.asarray(np.argsort(d, kind='stable'))

        def _sinusoidal_pe(seq_len, d):
            pos = np.arange(seq_len)[:, None].astype(np.float32)
            div = np.exp(np.arange(0, d, 2).astype(np.float32) * (-np.log(10000.0) / d))
            pe = np.zeros((seq_len, d), dtype=np.float32)
            pe[:, 0::2] = np.sin(pos * div)
            pe[:, 1::2] = np.cos(pos * div)
            return jnp.asarray(pe)
        key = jax.random.key(seed)
        k1, k2, k3 = jax.random.split(key, 3)
        images = jax.random.normal(k1, (64, NUM_CHANNELS, IMAGE_SIZE, IMAGE_SIZE), dtype=jnp.float32)
        cls_token = jax.random.normal(k2, (1, 1, EMBED_DIM), dtype=jnp.float32)
        W = jax.random.normal(k3, (EMBED_DIM, IN_FEATURES), dtype=jnp.float32) * 0.02
        b = jnp.zeros((EMBED_DIM,), dtype=jnp.float32)
        return {'images': images, 'cls_token': cls_token, 'W': W, 'b': b}
    _L0_tok_all = _L0_tok_setup()
    _L0_tok_in = {k: v for k, v in _L0_tok_all.items() if k in ('cls_token', 'W', 'b')}
    del _L0_tok_all

    def _L0_attn_setup():
        import jax, jax.numpy as jnp
        import numpy as np
        B, S, D, H = (8, 256, 192, 12)
        HS = D // H
        key = jax.random.key(seed)
        k1, k2, k3 = jax.random.split(key, 3)
        x = jax.random.normal(k1, (B, S, D), dtype=jnp.float32)
        W_attn = jax.random.normal(k2, (D, 3 * H * HS), dtype=jnp.float32) * 0.02
        b_attn = jnp.zeros((3 * H * HS,), dtype=jnp.float32)
        W_proj = jax.random.normal(k3, (H * HS, D), dtype=jnp.float32) * 0.02
        b_proj = jnp.zeros((D,), dtype=jnp.float32)
        return {'x': x, 'W_attn': W_attn, 'b_attn': b_attn, 'W_proj': W_proj, 'b_proj': b_proj}
    _L0_attn_all = _L0_attn_setup()
    _L0_attn_in = {k: v for k, v in _L0_attn_all.items() if k in ('W_attn', 'b_attn', 'W_proj', 'b_proj')}
    del _L0_attn_all

    def _L0_ffn_setup():
        import jax, jax.numpy as jnp
        import numpy as np
        B, N, DIM, HEADS = (4, 256, 192, 12)
        HIDDEN, E, TOPK = (768, 8, 2)
        EPS = 1e-05

        def _layernorm(x, g, b):
            mu = jnp.mean(x, axis=-1, keepdims=True)
            var = jnp.var(x, axis=-1, keepdims=True)
            return (x - mu) * jax.lax.rsqrt(var + EPS) * g + b
        key = jax.random.key(seed)
        ks = jax.random.split(key, 10)
        s = 0.02
        return {'x': jax.random.normal(ks[0], (B, N, DIM), dtype=jnp.float32), 'ln1_g': jnp.ones((DIM,), jnp.float32), 'ln1_b': jnp.zeros((DIM,), jnp.float32), 'qkv_w': jax.random.normal(ks[1], (3 * DIM, DIM), jnp.float32) * s, 'proj_w': jax.random.normal(ks[2], (DIM, DIM), jnp.float32) * s, 'proj_b': jnp.zeros((DIM,), jnp.float32), 'ln2_g': jnp.ones((DIM,), jnp.float32), 'ln2_b': jnp.zeros((DIM,), jnp.float32), 'gate_w': jax.random.normal(ks[3], (E, DIM), jnp.float32) * s, 'gate_b': jnp.zeros((E,), jnp.float32), 'w1': jax.random.normal(ks[4], (E, HIDDEN, DIM), jnp.float32) * s, 'b1': jnp.zeros((E, HIDDEN), jnp.float32), 'w2': jax.random.normal(ks[5], (E, DIM, HIDDEN), jnp.float32) * s, 'b2': jnp.zeros((E, DIM), jnp.float32)}
    _L0_ffn_all = _L0_ffn_setup()
    _L0_ffn_in = {k: v for k, v in _L0_ffn_all.items() if k in ('ln1_g', 'ln1_b', 'qkv_w', 'proj_w', 'proj_b', 'ln2_g', 'ln2_b', 'gate_w', 'gate_b', 'w1', 'b1', 'w2', 'b2')}
    del _L0_ffn_all
    return {'x': x, 'L0_tok_cls_token': _L0_tok_in['cls_token'], 'L0_tok_W': _L0_tok_in['W'], 'L0_tok_b': _L0_tok_in['b'], 'L0_attn_W_attn': _L0_attn_in['W_attn'], 'L0_attn_b_attn': _L0_attn_in['b_attn'], 'L0_attn_W_proj': _L0_attn_in['W_proj'], 'L0_attn_b_proj': _L0_attn_in['b_proj'], 'L0_ffn_ln1_g': _L0_ffn_in['ln1_g'], 'L0_ffn_ln1_b': _L0_ffn_in['ln1_b'], 'L0_ffn_qkv_w': _L0_ffn_in['qkv_w'], 'L0_ffn_proj_w': _L0_ffn_in['proj_w'], 'L0_ffn_proj_b': _L0_ffn_in['proj_b'], 'L0_ffn_ln2_g': _L0_ffn_in['ln2_g'], 'L0_ffn_ln2_b': _L0_ffn_in['ln2_b'], 'L0_ffn_gate_w': _L0_ffn_in['gate_w'], 'L0_ffn_gate_b': _L0_ffn_in['gate_b'], 'L0_ffn_w1': _L0_ffn_in['w1'], 'L0_ffn_b1': _L0_ffn_in['b1'], 'L0_ffn_w2': _L0_ffn_in['w2'], 'L0_ffn_b2': _L0_ffn_in['b2']}

def reference(x, L0_tok_cls_token, L0_tok_W, L0_tok_b, L0_attn_W_attn, L0_attn_b_attn, L0_attn_W_proj, L0_attn_b_proj, L0_ffn_ln1_g, L0_ffn_ln1_b, L0_ffn_qkv_w, L0_ffn_proj_w, L0_ffn_proj_b, L0_ffn_ln2_g, L0_ffn_ln2_b, L0_ffn_gate_w, L0_ffn_gate_b, L0_ffn_w1, L0_ffn_b1, L0_ffn_w2, L0_ffn_b2):
    import jax
    import jax.numpy as jnp

    def _L0_tok_ref(images, cls_token, W, b):
        import jax, jax.numpy as jnp
        import numpy as np
        IMAGE_SIZE = 224
        NUM_CHANNELS = 3
        NUM_BINS = 16
        EMBED_DIM = 192
        FILTER_SIZE = 96
        CROP = 2 * FILTER_SIZE
        BIN_SIZE = CROP * CROP // NUM_BINS
        IN_FEATURES = NUM_CHANNELS * BIN_SIZE
        SEQ_LEN = NUM_BINS + 1

        def _sorted_radial_indices(H, W):
            y, x = np.meshgrid(np.arange(H), np.arange(W), indexing='ij')
            d = np.sqrt((x - W / 2.0) ** 2 + (y - H / 2.0) ** 2).reshape(-1)
            return jnp.asarray(np.argsort(d, kind='stable'))

        def _sinusoidal_pe(seq_len, d):
            pos = np.arange(seq_len)[:, None].astype(np.float32)
            div = np.exp(np.arange(0, d, 2).astype(np.float32) * (-np.log(10000.0) / d))
            pe = np.zeros((seq_len, d), dtype=np.float32)
            pe[:, 0::2] = np.sin(pos * div)
            pe[:, 1::2] = np.cos(pos * div)
            return jnp.asarray(pe)
        B, C, H, Wd = images.shape
        f = jnp.fft.fftshift(jnp.fft.fft2(images))
        y, x = jnp.meshgrid(jnp.arange(H), jnp.arange(Wd), indexing='ij')
        mask = (jnp.abs(x - Wd // 2) <= FILTER_SIZE) & (jnp.abs(y - H // 2) <= FILTER_SIZE)
        f = f * mask.astype(f.dtype)
        cy, cx = (H // 2, Wd // 2)
        f = f[:, :, cy - FILTER_SIZE:cy + FILTER_SIZE, cx - FILTER_SIZE:cx + FILTER_SIZE]
        power = jnp.abs(f).astype(jnp.float32)
        idx = _sorted_radial_indices(CROP, CROP)
        power_sorted = power.reshape(B, C, CROP * CROP)[:, :, idx]
        ps = power_sorted.reshape(B, C, NUM_BINS, BIN_SIZE)
        tokens = ps.transpose(0, 2, 1, 3).reshape(B, NUM_BINS, C * BIN_SIZE)
        tokens = jnp.einsum('bnf,ef->bne', tokens, W) + b
        cls = jnp.broadcast_to(cls_token, (B, 1, EMBED_DIM))
        tokens = jnp.concatenate([cls, tokens], axis=1)
        tokens = tokens + _sinusoidal_pe(SEQ_LEN, EMBED_DIM)[None]
        return tokens

    def _L0_attn_ref(x, W_attn, b_attn, W_proj, b_proj):
        import jax, jax.numpy as jnp
        import numpy as np
        B, S, D, H = (8, 256, 192, 12)
        HS = D // H
        b, s, d = x.shape
        qkv = (x @ W_attn + b_attn).reshape(b, s, 3, H, HS)
        q, k, v = (qkv[:, :, 0], qkv[:, :, 1], qkv[:, :, 2])
        scale = jnp.sqrt(jnp.asarray(HS, dtype=x.dtype))
        scores = jnp.einsum('bqhd,bkhd->bhqk', q, k) / scale
        causal = jnp.tril(jnp.ones((s, s), dtype=bool))
        scores = jnp.where(causal, scores, -jnp.inf)
        attn = jax.nn.softmax(scores, axis=-1)
        out = jnp.einsum('bhqk,bkhd->bqhd', attn, v).reshape(b, s, H * HS)
        return out @ W_proj + b_proj

    def _L0_ffn_ref(x, ln1_g, ln1_b, qkv_w, proj_w, proj_b, ln2_g, ln2_b, gate_w, gate_b, w1, b1, w2, b2):
        import jax, jax.numpy as jnp
        import numpy as np
        B, N, DIM, HEADS = (4, 256, 192, 12)
        HIDDEN, E, TOPK = (768, 8, 2)
        EPS = 1e-05

        def _layernorm(x, g, b):
            mu = jnp.mean(x, axis=-1, keepdims=True)
            var = jnp.var(x, axis=-1, keepdims=True)
            return (x - mu) * jax.lax.rsqrt(var + EPS) * g + b
        b, n, d = x.shape
        hd = d // HEADS
        scale = hd ** (-0.5)
        h = _layernorm(x, ln1_g, ln1_b)
        qkv = h @ qkv_w.T
        qkv = qkv.reshape(b, n, 3, HEADS, hd).transpose(2, 0, 3, 1, 4)
        q, k, v = (qkv[0], qkv[1], qkv[2])
        attn = jax.nn.softmax(jnp.einsum('bhnd,bhmd->bhnm', q, k) * scale, axis=-1)
        a = jnp.einsum('bhnm,bhmd->bhnd', attn, v)
        a = a.transpose(0, 2, 1, 3).reshape(b, n, d)
        a = a @ proj_w.T + proj_b
        x = x + a
        h2 = _layernorm(x, ln2_g, ln2_b)
        t = h2.reshape(-1, d)
        T = t.shape[0]
        logits = t @ gate_w.T + gate_b
        top_val, top_idx = jax.lax.top_k(logits, TOPK)
        score = jax.nn.softmax(top_val, axis=-1)
        cw = jnp.zeros((T, E), t.dtype).at[jnp.arange(T)[:, None], top_idx].add(score)
        out = jnp.zeros_like(t)
        for e in range(E):
            he = jax.nn.gelu(t @ w1[e].T + b1[e], approximate=False)
            ye = he @ w2[e].T + b2[e]
            out = out + cw[:, e:e + 1] * ye
        return x + out.reshape(b, n, d)
    h = _L0_tok_ref(x, L0_tok_cls_token, L0_tok_W, L0_tok_b)
    h = _layernorm(h + _L0_attn_ref(h, L0_attn_W_attn, L0_attn_b_attn, L0_attn_W_proj, L0_attn_b_proj), axis=-1)
    h = _layernorm(h + _L0_ffn_ref(h, L0_ffn_ln1_g, L0_ffn_ln1_b, L0_ffn_qkv_w, L0_ffn_proj_w, L0_ffn_proj_b, L0_ffn_ln2_g, L0_ffn_ln2_b, L0_ffn_gate_w, L0_ffn_gate_b, L0_ffn_w1, L0_ffn_b1, L0_ffn_w2, L0_ffn_b2), axis=-1)
    return h

_drawn_inputs = setup_inputs


def setup_inputs(seed=0):
    import zlib

    import numpy as np

    out = dict(_drawn_inputs(seed))
    spreads = {'L0_tok_b': (0.0, 0.8),
     'L0_attn_b_attn': (0.0, 0.8),
     'L0_attn_b_proj': (0.0, 0.377),
     'L0_ffn_ln1_g': (1.0, 0.6),
     'L0_ffn_ln1_b': (0.0, 0.8),
     'L0_ffn_proj_b': (0.0, 0.1),
     'L0_ffn_ln2_g': (1.0, 0.6),
     'L0_ffn_ln2_b': (0.0, 0.745),
     'L0_ffn_gate_b': (0.0, 0.341),
     'L0_ffn_b1': (0.0, 0.754),
     'L0_ffn_b2': (0.0, 0.1)}
    factors = {}
    for name, (base, spread) in spreads.items():
        noise = np.random.default_rng([zlib.crc32(name.encode()), seed]).standard_normal(out[name].shape)
        drawn = base * np.exp(spread * noise) if base else spread * noise
        out[name] = jnp.asarray(drawn.astype(out[name].dtype))
    for name, factor in factors.items():
        out[name] = (out[name] * factor).astype(out[name].dtype)
    return out
```

```python
import math
from contextlib import ExitStack

import numpy as np
import concourse.bass as bass
from concourse import mybir

F32 = mybir.dt.float32
I32 = mybir.dt.int32
ALU = mybir.AluOpType
ACT = mybir.ActivationFunctionType
AX_X = mybir.AxisListType.X

P = 128
BATCH, CHANNELS, SIDE = 64, 3, 224
IMGS = BATCH * CHANNELS
HALF = SIDE // 2
CROP = 192
FREQ = CROP // 2 + 1
PAIR = 2 * FREQ
BINS = 16
BIN = CROP * CROP // BINS
CHUNKS = BIN // P
DIM = 192
SEQ = BINS + 1
ROWS = FREQ * PAIR
EPS = 1e-5
TOKENS = BATCH * SEQ
TG_IMGS = 4
TG = TG_IMGS * SEQ
TGROUPS = BATCH // TG_IMGS
HEADS, HEAD = 12, 16
SLOT = 32
HPT = P // SLOT
QK_TILES = 2 * HEADS // HPT
KH = DIM // 2
SCALE = HEAD ** -0.5
EXPERTS, HIDDEN, TOPK = 8, 768, 2
HT = HIDDEN // P
TT = -(-TOKENS // P)
TPAD = TT * P
TC = 3 * P
NC = TT // 3


def constants():
    y = np.arange(HALF)[:, None] + 0.5
    k = np.arange(FREQ)[None, :]
    angle = 2.0 * np.pi * ((2 * y * k) % (2 * SIDE)) / (2 * SIDE)
    dft = np.concatenate([np.cos(angle), np.sin(angle)], 1).astype(np.float32)
    gy, gx = np.meshgrid(np.arange(CROP), np.arange(CROP), indexing="ij")
    dist = np.sqrt((gx - CROP / 2.0) ** 2 + (gy - CROP / 2.0) ** 2).reshape(-1)
    order = np.argsort(dist, kind="stable")
    ky, kx = (gy - CROP // 2).reshape(-1)[order], (gx - CROP // 2).reshape(-1)[order]
    sign = (ky * kx < 0).astype(np.int64)
    row = (np.abs(kx) * 2 + sign) * FREQ + np.abs(ky)
    rank_row = np.ascontiguousarray(row.reshape(BINS * CHUNKS, P).T.astype(np.int32))
    pos = np.arange(SEQ)[:, None].astype(np.float32)
    div = np.exp(np.arange(0, DIM, 2).astype(np.float32) * (-np.log(10000.0) / DIM))
    pe = np.zeros((SEQ, DIM), np.float32)
    pe[:, 0::2] = np.sin(pos * div)
    pe[:, 1::2] = np.cos(pos * div)
    tok = np.arange(TG)
    own = tok[:, None] // SEQ == tok[None, :] // SEQ
    causal = own & (tok[:, None] >= tok[None, :])
    masks = np.stack([np.where(m, 0.0, -1e30) for m in (causal, own)], 1).astype(np.float32)
    return {"dft": dft, "rank_row": rank_row, "pos": np.tile(pe, (TG_IMGS, 1)),
            "masks": masks, "identity": np.eye(P, dtype=np.float32)}


def at_least(eng, sem, n):
    if not (isinstance(n, int) and n <= 0):
        eng.wait_ge(sem, n)


def pipeline(eng, step, first, loops, end):
    for t in range(first):
        step(t, t)
    for start, stop, unroll in loops:
        with eng.Fori(start // unroll, stop // unroll) as body:
            for j in range(unroll):
                step(body * unroll + j, start + j)
        first = stop
    for t in range(first, end):
        step(t, t)


G_IMGS = 4
GROUPS = IMGS // G_IMGS
UNITS = IMGS // 2
GPC = GROUPS // CHANNELS
UPG = G_IMGS // 2
Y_RING, FOLD_RING, A_RING, UV_RING, SS_RING = 4, 2, 4, 2, 2
BODY_G = 4
BODY_U = BODY_G * UPG
S2_LAG = 2
SQ_LAG = 2
RT_LAG = 2


def spectrum(nc, ctx, sem, xh, table, dft_in):
    sb = lambda name, shape, dt=F32: ctx.enter_context(nc.sbuf_tensor(name, shape, dt))
    R = sb("power", [FREQ, PAIR, 2 * BATCH])
    img = sb("img", [HALF, Y_RING, 2, G_IMGS * SIDE])
    fold = sb("fold", [HALF, FOLD_RING, 2, G_IMGS * SIDE])
    dft = sb("dft", [HALF, PAIR])
    far = sb("far", [HALF, 2, 2, PAIR])
    folded = sb("folded", [HALF, A_RING, 2, 2, PAIR])
    odd = sb("odd", [FREQ, 2, 2, PAIR])
    uv = sb("uv", [FREQ, UV_RING, 2, G_IMGS, PAIR])
    ss = sb("ss", [FREQ, SS_RING, 2, G_IMGS, FREQ])
    ps1 = ctx.enter_context(nc.psum_tensor("ps1", [P, 2, 2, 512], F32))
    ps2 = ctx.enter_context(nc.psum_tensor("ps2", [P, 2, 2, 512], F32))

    img_in = [sem(f"img_in{i}") for i in range(Y_RING)]
    dft_in_s = sem("dft_in_s")
    fold_done = sem("fold_done")
    dft1_done = sem("dft1_done")
    far_done = sem("far_done")
    folded_done = sem("folded_done")
    dft2_done = sem("dft2_done")
    odd_done = sem("odd_done")
    uv_done = sem("uv_done")
    sq_done = sem("sq_done")
    ss_done = sem("ss_done")
    root_done = sem("root_done")
    root_room = sem("root_room")
    stored = [sem(f"stored{c}") for c in range(CHANNELS)]

    def program_sync(sp):
        sp.dma_start(dft[:, :], dft_in).then_inc(dft_in_s, 16)
        sp.sem_inc(root_room, 2 * GPC)

        def load(g, j):
            at_least(sp, fold_done, g - Y_RING + 1)
            sp.dma_start(img[:, j % Y_RING, :, :].rearrange("p h n -> p h n"),
                         xh[:, :, bass.ds(g * G_IMGS * SIDE, G_IMGS * SIDE)].rearrange("h p n -> p h n")
                         ).then_inc(img_in[j % Y_RING], 16)

        def store(c):
            sp.wait_ge(root_done, GPC * (c + 1))
            src = R[:, :, (c % 2) * BATCH:(c % 2) * BATCH + BATCH]
            dst = table.rearrange("(l r) i -> l r i", l=FREQ)[:, :, c * BATCH:(c + 1) * BATCH]
            for lo, hi in ((0, FREQ - 1), (FREQ - 1, FREQ)):
                sp.dma_start(dst[lo:hi], src[lo:hi]).then_inc(stored[c], 16)

        for g in range(Y_RING):
            load(g, g)
        at = Y_RING
        for c in range(CHANNELS):
            until = min(GPC * (c + 1) + 2 * BODY_G, GROUPS)
            with sp.Fori(at // BODY_G, until // BODY_G) as body:
                for j in range(BODY_G):
                    load(body * BODY_G + j, j)
            at = until
            if c == 2:
                pass
            store(c)
            if c == 0:
                sp.wait_ge(stored[0], 32)
                sp.sem_inc(root_room, GPC)

    def program_pool(pool):
        def fold_group(g, j):
            pool.wait_ge(img_in[j % Y_RING], g // Y_RING * 16 + 16)
            at_least(pool, dft1_done, (g - FOLD_RING + 1) * UPG)
            for odd_part, op in ((0, ALU.add), (1, ALU.subtract)):
                last = pool.tensor_tensor(fold[:, j % FOLD_RING, odd_part, :], img[:, j % Y_RING, 0, :],
                                          img[:, j % Y_RING, 1, :], op)
            last.then_inc(fold_done, 1)

        def sum_group(g, j):
            pool.wait_ge(sq_done, UPG * (g + 1))
            at_least(pool, root_done, g - SS_RING + 1)
            for s in range(2):
                last = pool.tensor_tensor(ss[:, j % SS_RING, s], uv[:, j % UV_RING, s, :, 0:FREQ],
                                          uv[:, j % UV_RING, 1 - s, :, FREQ:PAIR], ALU.add)
            last.then_inc(ss_done, UPG)

        def step(t, j):
            if not isinstance(t, int) or t < GROUPS:
                fold_group(t, j)
            if not isinstance(t, int) or t >= SUM_LAG:
                sum_group(t - SUM_LAG, j - SUM_LAG)

        SUM_LAG = 3
        pipeline(pool, step, BODY_G, [(BODY_G, GROUPS, BODY_G)], GROUPS + SUM_LAG)

    def program_tensor(pe):
        pe.wait_ge(dft_in_s, 16)

        def first_dft(u, j):
            if j % UPG == 0:
                pe.wait_ge(fold_done, u // UPG + 1)
            at_least(pe, folded_done, u - 1)
            for i in range(2):
                for chunk in range(2):
                    for part in range(2):
                        x0 = ((j % UPG) * 2 + i) * SIDE + chunk * HALF
                        col = chunk * PAIR + part * FREQ
                        last = pe.matmul(ps1[0:HALF, j % 2, i, col:col + FREQ],
                                         fold[:, j // UPG % FOLD_RING, part, x0:x0 + HALF],
                                         dft[:, part * FREQ:(part + 1) * FREQ], start=True, stop=True)
            last.then_inc(dft1_done, 1)

        def second_dft(u, j):
            pe.wait_ge(folded_done, u + 1)
            at_least(pe, uv_done, u - 1)
            src = folded[:, j % A_RING]
            pe.matmul(ps2[0:FREQ, j % 2, 0, 0:2 * PAIR], dft[:, 0:FREQ], src[:, 0], start=True, stop=True)
            out = ps2[0:FREQ, j % 2, 1, 0:2 * PAIR].rearrange("p (i c) -> p i c", i=2)
            for part in range(2):
                last = pe.matmul(out[:, :, part * FREQ:(part + 1) * FREQ], dft[:, FREQ:PAIR],
                                 src[:, 1, :, (1 - part) * FREQ:(2 - part) * FREQ], start=True, stop=True)
            last.then_inc(dft2_done, 1)

        def step(t, j):
            if not isinstance(t, int) or t < UNITS:
                first_dft(t, j)
            if not isinstance(t, int) or t >= S2_LAG:
                second_dft(t - S2_LAG, j - S2_LAG)

        pipeline(pe, step, BODY_U, [(BODY_U, UNITS, BODY_U)], UNITS + S2_LAG)

    def program_scalar(act):
        def far_copy(u, j):
            act.wait_ge(dft1_done, u + 1)
            at_least(act, folded_done, u - 1)
            act.activation(far[:, j % 2], ps1[0:HALF, j % 2, :, PAIR:2 * PAIR], ACT.Copy).then_inc(far_done, 1)

        def odd_copy(u, j):
            act.wait_ge(dft2_done, u + 1)
            at_least(act, uv_done, u - 1)
            act.activation(odd[:, j % 2], ps2[0:FREQ, j % 2, 1, 0:2 * PAIR].rearrange("p (i c) -> p i c", i=2),
                           ACT.Copy).then_inc(odd_done, 1)

        def square(u, j):
            act.wait_ge(uv_done, u + 1)
            i0 = (j % UPG) * 2
            v = uv[:, j // UPG % UV_RING, :, i0:i0 + 2, :]
            act.activation(v, v, ACT.Square).then_inc(sq_done, 1)

        def root(g, j):
            act.wait_ge(ss_done, UPG * (g + 1))
            act.wait_ge(root_room, g + 1)
            col = (g * G_IMGS) % (2 * BATCH)
            out = R[:, :, bass.ds(col, G_IMGS)].rearrange("p (s k) i -> p s i k", s=2)
            act.activation(out, ss[:, j % SS_RING], ACT.Sqrt).then_inc(root_done, 1)

        ODD = S2_LAG
        SQ = ODD + SQ_LAG
        RT = SQ + 3

        def step(t, j):
            dyn = not isinstance(t, int)
            if dyn or t < UNITS:
                far_copy(t, j)
            if dyn or ODD <= t < UNITS + ODD:
                odd_copy(t - ODD, j - ODD)
            if dyn or SQ <= t < UNITS + SQ:
                square(t - SQ, j - SQ)
            if (j - RT) % UPG == 0 and (dyn or t >= RT):
                root((t - RT) // UPG, (j - RT) // UPG)

        pipeline(act, step, BODY_U, [(BODY_U, UNITS, BODY_U)], UNITS + RT)

    def program_vector(dve):
        def fold_columns(u, j):
            dve.wait_ge(far_done, u + 1)
            at_least(dve, dft2_done, u - A_RING + 1)
            near = ps1[0:HALF, j % 2, :, 0:PAIR]
            for part, op in ((0, ALU.add), (1, ALU.subtract)):
                last = dve.tensor_tensor(folded[:, j % A_RING, part], near, far[:, j % 2], op)
            last.then_inc(folded_done, 1)

        def combine(u, j):
            dve.wait_ge(odd_done, u + 1)
            if j % UPG == 0:
                at_least(dve, ss_done, u - (UV_RING - 1) * UPG)
            even = ps2[0:FREQ, j % 2, 0, 0:2 * PAIR].rearrange("p (i c) -> p i c", i=2)
            i0 = (j % UPG) * 2
            for part, op in ((0, ALU.subtract), (1, ALU.add)):
                last = dve.tensor_tensor(uv[:, j // UPG % UV_RING, part, i0:i0 + 2, :], even, odd[:, j % 2], op)
            last.then_inc(uv_done, 1)

        ODD = S2_LAG

        def step(t, j):
            if not isinstance(t, int) or t < UNITS:
                fold_columns(t, j)
            if not isinstance(t, int) or t >= ODD:
                combine(t - ODD, j - ODD)

        pipeline(dve, step, BODY_U, [(BODY_U, UNITS, BODY_U)], UNITS + ODD)

    return program_sync, program_pool, program_tensor, program_scalar, program_vector, stored, root_done




def tokens_of_rings(nc, ctx, sem, table, rank_row_c, w_tok, raw, ps, spectrum_done):
    sb = lambda name, shape, dt=F32: ctx.enter_context(nc.sbuf_tensor(name, shape, dt))
    RING = 6
    rank_row = sb("rank_row", [P, 2, 2 * CHUNKS], I32)
    wt = sb("w_tok", [P, CHANNELS, CHUNKS, DIM])
    rows = sb("rows", [P, RING, 2, IMGS])
    tok = sb("tok", [P, 2, DIM])
    zeros = sb("zeros", [BATCH, DIM])
    index_in, wt_in = [sem(f"index_in{i}") for i in range(2)], sem("wt_in")
    gathered = [sem(f"gathered{i}") for i in range(RING)]
    rows_used, tok_done, tok_out = sem("rows_used"), sem("tok_done"), sem("tok_out")
    tok_stored = [sem(f"tok_stored{i}") for i in range(2)]
    zeros_set, zeros_stored, gate = sem("zeros_set"), sem("zeros_stored"), sem("gather_gate")
    PAIRS = BINS // 2
    STEPS = PAIRS * CHUNKS
    UNROLL = 2 * CHUNKS

    def program_sync(sp):
        spectrum_done(sp)
        def load_index(q, j):
            at_least(sp, rows_used, (q - 1) * CHUNKS)
            sp.dma_start(rank_row[:, j % 2, :], rank_row_c[:, bass.ds(q * 2 * CHUNKS, 2 * CHUNKS)]
                         ).then_inc(index_in[j % 2], 16)

        load_index(0, 0)
        load_index(1, 1)
        for c in range(CHANNELS):
            sp.dma_start(wt[:, c], w_tok[c * BIN:(c + 1) * BIN, :].rearrange("(j p) e -> p j e", p=P)
                         ).then_inc(wt_in, 16)
        sp.wait_ge(zeros_set, 1)
        sp.dma_start(raw.rearrange("(b s) e -> b s e", s=SEQ)[:, 0, :], zeros[:, :]).then_inc(zeros_stored, 16)

        def store(q, j):
            sp.wait_ge(tok_out, q + 1)
            for half in range(2):
                sp.dma_start(raw.rearrange("(b s) e -> b s e", s=SEQ)[:, bass.ds(2 * q + half + 1, 1), :],
                             tok[half * BATCH:(half + 1) * BATCH, j % 2, None, :]).then_inc(tok_stored[j % 2], 16)

        def step(q, j):
            if not isinstance(q, int) or q >= 2:
                load_index(q, j)
                store(q - 2, j - 2)

        pipeline(sp, step, 2, [(2, PAIRS, 2)], PAIRS)
        for q in range(PAIRS - 2, PAIRS):
            store(q, q)
        sp.wait_ge(zeros_stored, 16)
        for s in tok_stored:
            sp.wait_ge(s, 32 * PAIRS // 2)

    def program_pool(pool):
        spectrum_done(pool)

        def step(n, j):
            at_least(pool, rows_used, n - RING + 1)
            q, chunk = j // CHUNKS % 2, j % CHUNKS
            if chunk == 0:
                pool.wait_ge(index_in[q], n // UNROLL * 16 + 16)
            pool.sem_inc(gate, 1)
            for half in range(2):
                pool.indirect_dma_start(
                    out=rows[:, j % RING, half, :], out_offset=None, in_=table,
                    in_offset=bass.IndirectOffsetOnAxis(
                        ap=rank_row[:, q, half * CHUNKS + chunk, None], axis=0)
                ).then_inc(gathered[j % RING], 16)

        pipeline(pool, step, UNROLL, [(UNROLL, STEPS, UNROLL)], STEPS)

    def program_tensor(pe):
        pe.wait_ge(wt_in, 16 * CHANNELS)

        def step(n, j):
            q, chunk = j // CHUNKS, j % CHUNKS
            if chunk == 0:
                at_least(pe, tok_out, (n - CHUNKS) // CHUNKS)
            pe.wait_ge(gathered[j % RING], n // RING * 32 + 32)
            for c in range(CHANNELS):
                pair = rows[:, j % RING].rearrange("p h (b c) -> p c (h b)", c=CHANNELS)
                last = pe.matmul(ps[:, q % 2, 0:DIM], pair[:, c, :],
                                 wt[:, c, chunk, :], start=(chunk == 0 and c == 0),
                                 stop=(chunk == CHUNKS - 1 and c == CHANNELS - 1))
            last.then_inc(rows_used, 1)

        pipeline(pe, step, UNROLL, [(UNROLL, STEPS, UNROLL)], STEPS)

    def program_scalar(act):
        def step(q, j):
            act.wait_ge(rows_used, (q + 1) * CHUNKS)
            at_least(act, tok_stored[j % 2], q // 2 * 32)
            act.activation(tok[:, j % 2, :], ps[:, j % 2, 0:DIM], ACT.Copy).then_inc(tok_out, 1)

        pipeline(act, step, 2, [(2, PAIRS, 2)], PAIRS)

    def program_vector(dve):
        spectrum_done(dve)
        dve.memset(zeros[:, :], 0.0).then_inc(zeros_set, 1)

    def done(eng):
        eng.wait_ge(zeros_stored, 16)
        for s in tok_stored:
            eng.wait_ge(s, 32 * PAIRS // 2)

    return program_sync, program_pool, program_tensor, program_scalar, program_vector, done


class Chain:

    def __init__(self, eng, sem, per):
        self.eng, self.sem, self.per = eng, sem, per

    def begin(self, item):
        self.base, self.n = item * self.per, 0

    def did(self, ins):
        self.n += 1
        return ins.then_inc(self.sem, 1)

    def wait(self):
        self.eng.wait_ge(self.sem, self.base + self.n)

    def end(self):
        assert self.n == self.per, self.n


def attention(nc, ctx, sem, name, W, layer, raw, x_all, tT, x_out, ready):
    sb = lambda n, shape, dt=F32: ctx.enter_context(nc.sbuf_tensor(f"{name}_{n}", shape, dt))
    S = lambda n: sem(f"{name}_{n}")
    xin = sb("xin", [TG, 2, DIM])
    xT = sb("xT", [KH, 2, 2, TG])
    qk = sb("qk", [P, 2, QK_TILES, TG])
    v = sb("v", [TG, 4, DIM])
    s = sb("s", [TG, 2, HEADS, TG])
    mx = sb("mx", [TG, 2, HEADS])
    rs = sb("rs", [TG, 2, HEADS])
    pT = sb("pT", [TG, HEADS, TG])
    o = sb("o", [TG, 2, HEADS, HEAD])
    oT = sb("oT", [KH, 2, TG])
    z = sb("z", [TG, 2, DIM])
    st = sb("st", [TG, 2, 6])
    mv = sb("mv", [TG, 2, 2])
    st0 = sb("st0", [TG, 6])
    mv0 = sb("mv0", [TG, 2])
    hn = sb("hn", [TG, 2, DIM])
    if layer:
        xb = sb("xb", [TG, TGROUPS, DIM])
        z2 = sb("z2", [TG, 2, DIM])
    psum = W["psum"]
    psX, psQ, psO, psT = psum[:, 0], psum[:, 1], psum[:, 2], psum[:, 7]
    HB = HEADS // HPT
    psS = psum[0:TG, 3:7, 0:HB * TG]
    psP = psum[0:TG, 3:7, HB * TG:2 * HB * TG]

    raw_in = [S(f"raw_in{i}") for i in range(2)]
    xin_done, ln0, pow0 = S("xin_done"), S("ln0"), S("pow0")
    xtr, xT_done, qk_mm, qk_done, v_mm, v_done = S("xtr"), S("xT"), S("qk_mm"), S("qk"), S("v_mm"), S("v")
    sc_mm, maxed, less, exped, summed = S("sc"), S("maxed"), S("less"), S("exp"), S("sum")
    ptr, pT_done, av, o_done, otr, oT_done, proj = S("ptr"), S("pT"), S("av"), S("o"), S("otr"), S("oT"), S("proj")
    ln1, pow1, z_done, ttr, tT_done = S("ln1"), S("pow1"), S("z"), S("ttr"), S("tT")
    z_stored = [S(f"z_stored{i}") for i in range(2)]
    G = TGROUPS
    LAGS = 5
    U = 4
    L1 = layer == 1

    def run(eng, parts):
        def step(t, j):
            for lag, f in parts:
                if not isinstance(t, int) or lag <= t < G + lag:
                    f(t - lag, (j - lag) % U)
        first = 2 * U
        pipeline(eng, step, first, [(first, G, U)], G + LAGS)

    def program_sync(sp):
        if not L1:
            ready(sp)

            def load(g, j):
                at_least(sp, xin_done, g - 1)
                sp.dma_start(z[:, j % 2, :], raw[bass.ds(g * TG, TG), :]).then_inc(raw_in[j % 2], 16)
            run(sp, [(0, load)])
        else:
            def store(g, j):
                sp.wait_ge(twice, g + 1)
                sp.dma_start(x_out[bass.ds(g * TG, TG), :], z2[:, j % 2, :]).then_inc(z_stored[j % 2], 16)
            run(sp, [(0, store)])

    def program_pool(pool):
        pool.wait_ge(W["in"], W["in_n"])
        pool.wait_ge(W["half_set"], 1)

        def inverse_root(stat, sem):
            pool.tensor_tensor(stat, stat, W["minus_half"][0:TG, :], ALU.pow).then_inc(sem, 1)

        def begin(g, j):
            if L1:
                pool.wait_ge(ln0, 3 * (g + 1))
                inverse_root(mv0[:, 1:2], pow0)

        def subtract_max(g, j):
            pool.wait_ge(maxed, g + 1)
            pool.tensor_tensor(s[:, j % 2], s[:, j % 2], mx[:, j % 2, :, None].to_broadcast([TG, HEADS, TG]),
                               ALU.subtract).then_inc(less, 1)

        def end(g, j):
            pool.wait_ge(ln1, LN1_STATS * (g + 1) - (LN1_STATS - LN1_AT))
            inverse_root(mv[:, j % 2, 1:2], pow1)
            if L1:
                pool.wait_ge(z_done, g + 1)
                at_least(pool, z_stored[j % 2], g // 2 * 16)
                pool.sem_inc(gate, 1)
                pool.tensor_tensor(z2[:, j % 2, None, :], z[:, j % 2, None, :], x_all[:, bass.ds(g, 1), :], ALU.add
                                   ).then_inc(twice, 1)

        run(pool, [(0, begin), (2, subtract_max), (4, end)])

    LN1_STATS = 5 if L1 else 4
    LN1_AT = 3

    def program_tensor(pe):
        pe.wait_ge(W["in"], W["in_n"])

        def x_transposes(g, j):
            pe.wait_ge(xin_done, g + 1)
            at_least(pe, v_done, g)
            for h in range(2):
                last = pe.transpose(psX[0:KH, h * TG:(h + 1) * TG], xin[:, j % 2, h * KH:(h + 1) * KH],
                                    W["identity"][0:TG, 0:TG])
            last.then_inc(xtr, 1)

        def p_transposes(g, j):
            pe.wait_ge(exped, g + 1)
            at_least(pe, pT_done, g)
            if isinstance(g, int):
                pe.wait_ge(mk, min(g + 2, G))
            else:
                pe.wait_ge(mk, g + 2)
            for h in range(HEADS):
                last = pe.transpose(psP[:, h // HB, h % HB * TG:(h % HB + 1) * TG], s[:, j % 2, h, :],
                                    W["identity"][0:TG, 0:TG])
            last.then_inc(ptr, 1)

        def o_transposes(g, j):
            pe.wait_ge(o_done, g + 1)
            at_least(pe, tT_done if L1 else z_done, g)
            for h in range(2):
                ov = o[:, j % 2].rearrange("p h d -> p (h d)")
                last = pe.transpose(psT[0:KH, h * TG:(h + 1) * TG], ov[:, h * KH:(h + 1) * KH],
                                    W["identity"][0:TG, 0:TG])
            last.then_inc(otr, 1)

        def projections(g, j):
            pe.wait_ge(xT_done, g + 1)
            at_least(pe, qk_done, g)
            for t in range(QK_TILES):
                for h in range(2):
                    last = pe.matmul(psQ[:, t * TG:(t + 1) * TG], W["wqk"][:, h, t * P:(t + 1) * P],
                                     xT[:, j % 2, h, :], start=(h == 0), stop=(h == 1))
            last.then_inc(qk_mm, 1)
            for h in range(2):
                last = pe.matmul(psX[0:TG, 256:256 + DIM], xT[:, j % 2, h, :], W["wv"][:, h, :],
                                 start=(h == 0), stop=(h == 1))
            last.then_inc(v_mm, 1)

        def values(g, j):
            pe.wait_ge(pT_done, g + 1)
            pe.wait_ge(v_done, g + 1)
            at_least(pe, o_done, g)
            for h in range(HEADS):
                last = pe.matmul(psO[0:TG, h * HEAD:(h + 1) * HEAD], pT[:, h % HPT * HB + h // HPT, :],
                                 v[:, j % 4, h * HEAD:(h + 1) * HEAD], start=True, stop=True)
            last.then_inc(av, 1)

        def out_projection(g, j):
            pe.wait_ge(oT_done, g + 1)
            for h in range(2):
                last = pe.matmul(psT[0:TG, 256:256 + DIM], oT[:, h, :], W["wp"][:, h, :],
                                 start=(h == 0), stop=(h == 1))
            last.then_inc(proj, 1)

        def scores(g, j):
            pe.wait_ge(qk_done, g + 1)
            at_least(pe, mk, g)
            at_least(pe, pT_done, g - 1)
            for h in range(HEADS):
                p0 = h % HPT * SLOT
                last = pe.matmul(psS[:, h % HPT, h // HPT * TG:(h // HPT + 1) * TG],
                                 qk[p0:p0 + SLOT, j % 2, h // HPT, :],
                                 qk[p0:p0 + SLOT, j % 2, QK_TILES // 2 + h // HPT, :], start=True, stop=True)
            last.then_inc(sc_mm, 1)

        def t_transposes(g, j):
            pe.wait_ge(ln1, LN1_STATS * (g + 1))
            for h in range(2):
                last = pe.transpose(psT[0:KH, h * TG:(h + 1) * TG], hn[:, j % 2, h * KH:(h + 1) * KH],
                                    W["identity"][0:TG, 0:TG])
            last.then_inc(ttr, 1)

        parts = [(0, x_transposes), (3, p_transposes), (4, o_transposes), (0, projections), (4, out_projection),
                 (3, values), (1, scores)]
        if L1:
            parts.append((4, t_transposes))
        run(pe, parts)

    def program_scalar(act):
        act.wait_ge(W["in"], W["in_n"])

        def copy_xT(g, j):
            act.wait_ge(xtr, g + 1)
            at_least(act, v_mm, g - 1)
            act.activation(xT[:, j % 2].rearrange("p h t -> p (h t)"), psX[0:KH, 0:2 * TG], ACT.Copy
                           ).then_inc(xT_done, 1)

        def copy_pT(g, j):
            act.wait_ge(ptr, g + 1)
            at_least(act, av, g)
            act.activation(pT[:, :, :].rearrange("p (b h) t -> p b (h t)", b=HPT), psP, ACT.Copy
                           ).then_inc(pT_done, 1)

        def copy_oT(g, j):
            act.wait_ge(otr, g + 1)
            at_least(act, proj, g)
            act.activation(oT[:, :, :].rearrange("p h t -> p (h t)"), psT[0:KH, 0:2 * TG], ACT.Copy
                           ).then_inc(oT_done, 1)

        def exponent(g, j):
            act.wait_ge(less, g + 1)
            act.activation(s[:, j % 2], s[:, j % 2], ACT.Exp, scale=SCALE).then_inc(exped, 1)

        def copy_tT(g, j):
            act.wait_ge(ttr, g + 1)
            act.activation(tT[:, :, bass.ds(g * TG, TG)],
                           psT[0:KH, 0:2 * TG].rearrange("p (h t) -> p h t", h=2), ACT.Copy
                           ).then_inc(tT_done, 1)

        parts = [(0, copy_xT), (3, copy_pT), (4, copy_oT), (2, exponent)]
        if L1:
            parts.append((4, copy_tT))
        run(act, parts)

    def program_vector(dve):
        dve.wait_ge(W["in"], W["in_n"])
        dve.wait_ge(W["pos_done"], 1)

        def begin(g, j):
            at_least(dve, xtr, g - 1)
            if not L1:
                dve.wait_ge(raw_in[j % 2], g // 2 * 16 + 16)
                dve.tensor_tensor(xin[:, j % 2, :], z[:, j % 2, :], W["pos"], ALU.add).then_inc(xin_done, 1)
                dve.wait_ge(xin_done, g + 1)
                dve.tensor_tensor(x_all[:, bass.ds(g, 1), :], xin[:, j % 2, None, :], W["bp"][:, None, :],
                                  ALU.add).then_inc(ln0, 1)
            else:
                c = Chain(dve, ln0, 3)
                c.begin(g)
                xg = x_all[:, bass.ds(g, 1), :].rearrange("p a d -> p (a d)")
                at_least(dve, xin_done, g)
                c.did(dve.bn_stats(st0[:, :], xg))
                c.wait()
                dve.sem_inc(gate, 1)
                c.did(dve.bn_aggr(mv0[:, :], st0[:, :]))
                c.wait()
                c.did(dve.tensor_scalar(mv0[:, 1:2], mv0[:, 1:2], EPS, None, ALU.add))
                c.end()
                dve.wait_ge(pow0, g + 1)
                dve.tensor_scalar(xin[:, j % 2, :], xg, mv0[:, 0:1], mv0[:, 1:2], ALU.subtract, ALU.mult
                                  ).then_inc(lnx, 1)
                dve.wait_ge(lnx, 3 * g + 1)
                dve.tensor_tensor(xin[:, j % 2, :], xin[:, j % 2, :], W["g1"], ALU.mult).then_inc(lnx, 1)
                dve.wait_ge(lnx, 3 * g + 2)
                dve.tensor_tensor(xin[:, j % 2, :], xin[:, j % 2, :], W["b1"], ALU.add).then_inc(xin_done, 1)
                dve.tensor_tensor(xb[:, bass.ds(g, 1), :], x_all[:, bass.ds(g, 1), :], W["bp"][:, None, :], ALU.add
                                  ).then_inc(lnx, 1)

        def add_biases(g, j):
            dve.wait_ge(qk_mm, g + 1)
            at_least(dve, sc_mm, g - 1)
            dve.tensor_tensor(qk[:, j % 2], psQ[:, 0:QK_TILES * TG].rearrange("p (t n) -> p t n", t=QK_TILES),
                              W["bqk"][:, :, None].to_broadcast([P, QK_TILES, TG]), ALU.add).then_inc(qk_done, 1)
            dve.wait_ge(v_mm, g + 1)
            at_least(dve, av, g - 3)
            dve.tensor_tensor(v[:, j % 4, :], psX[0:TG, 256:256 + DIM], W["bv"], ALU.add).then_inc(v_done, 1)

        def mask_and_max(g, j):
            dve.wait_ge(sc_mm, g + 1)
            at_least(dve, ptr, g - 1)
            dve.tensor_tensor(s[:, j % 2].rearrange("p (b h) t -> p b h t", b=HPT),
                              psS.rearrange("p b (h t) -> p b h t", h=HB),
                              W["mask"][:, None, None, :].to_broadcast([TG, HPT, HB, TG]), ALU.add
                              ).then_inc(mk, 1)
            dve.wait_ge(mk, g + 1)
            at_least(dve, less, g - 1)
            dve.tensor_reduce(mx[:, j % 2, :], s[:, j % 2], AX_X, ALU.max).then_inc(maxed, 1)

        def sums(g, j):
            dve.wait_ge(exped, g + 1)
            dve.tensor_reduce(rs[:, j % 2, :], s[:, j % 2], AX_X, ALU.add).then_inc(summed, 1)
            dve.wait_ge(summed, 2 * g + 1)
            dve.reciprocal(rs[:, j % 2, :], rs[:, j % 2, :]).then_inc(summed, 1)

        def scale_out(g, j):
            dve.wait_ge(summed, 2 * (g + 1))
            dve.wait_ge(av, g + 1)
            at_least(dve, otr, g - 1)
            dve.tensor_tensor(o[:, j % 2].rearrange("p (h b) d -> p h b d", b=HPT),
                              psO[0:TG, 0:DIM].rearrange("p (h b d) -> p h b d", b=HPT, d=HEAD),
                              rs[:, j % 2].rearrange("p (b h) -> p h b", b=HPT)[:, :, :, None].to_broadcast(
                                  [TG, HB, HPT, HEAD]), ALU.mult).then_inc(o_done, 1)

        def close(g, j):
            dve.wait_ge(proj, g + 1)
            if L1:
                at_least(dve, twice, g - 1)
                dve.wait_ge(lnx, 3 * (g + 1))
            else:
                dve.wait_ge(ln0, g + 1)
            xg = (xb if L1 else x_all)[:, bass.ds(g, 1), :].rearrange("p a d -> p (a d)")
            zz = z[:, j % 2, :] if L1 else hn[:, j % 2, :]
            dve.tensor_tensor(zz, psT[0:TG, 256:256 + DIM], xg, ALU.add).then_inc(z_done, 1)
            dve.wait_ge(z_done, g + 1)
            c = Chain(dve, ln1, LN1_STATS)
            c.begin(g)
            c.did(dve.bn_stats(st[:, j % 2, :], zz))
            c.wait()
            dve.sem_inc(gate, 1)
            c.did(dve.bn_aggr(mv[:, j % 2, :], st[:, j % 2, :]))
            c.wait()
            c.did(dve.tensor_scalar(mv[:, j % 2, 1:2], mv[:, j % 2, 1:2], EPS, None, ALU.add))
            dve.wait_ge(pow1, g + 1)
            out = hn[:, j % 2, :] if L1 else xg
            if L1:
                at_least(dve, ttr, g - 1)
            c.did(dve.tensor_scalar(out, zz, mv[:, j % 2, 0:1], mv[:, j % 2, 1:2], ALU.subtract, ALU.mult))
            if L1:
                c.wait()
                dve.tensor_tensor(out, out, W["g2"], ALU.mult).then_inc(lny, 1)
                dve.wait_ge(lny, g + 1)
                c.did(dve.tensor_tensor(out, out, W["b2"], ALU.add))
            c.end()

        run(dve, [(2, mask_and_max), (0, begin), (3, sums), (0, add_biases), (4, close), (3, scale_out)])

    lnx, lny, mk, gate, twice = S("lnx"), S("lny"), S("mk"), S("gate"), S("twice")

    def done(eng):
        if L1:
            eng.wait_ge(tT_done, G)
            for i in range(2):
                eng.wait_ge(z_stored[i], 16 * G // 2)
        else:
            eng.wait_ge(ln1, LN1_STATS * G)

    return program_sync, program_pool, program_tensor, program_scalar, program_vector, done


def experts(nc, ctx, sem, W, tT, x_out, out, attention_done):
    sb = lambda n, shape, dt=F32: ctx.enter_context(nc.sbuf_tensor(f"moe_{n}", shape, dt))
    S = lambda n: sem(f"moe_{n}")
    w1 = sb("w1", [KH, 2, 2, HIDDEN])
    w2 = sb("w2", [P, 2, HT, DIM])
    hT = sb("hT", [P, 2, HT, TC])
    acc = sb("acc", [P, TT, DIM])
    res = sb("res", [P, TT, DIM])
    logits = sb("logits", [P, TT, EXPERTS])
    top = sb("top", [P, TT, 8])
    topi = sb("topi", [P, TT, 8], mybir.dt.uint32)
    topf = sb("topf", [P, TT, TOPK])
    e21 = sb("e21", [P, TT])
    den = sb("den", [P, TT])
    share = sb("share", [P, TT, TOPK])
    pick = sb("pick", [P, TOPK, TT, EXPERTS])
    cw = sb("cw", [P, TT, EXPERTS])
    cwT = sb("cwT", [EXPERTS, TPAD])
    st = sb("st", [P, TT, 6])
    mv = sb("mv", [P, TT, 2])
    psum = W["psum"]
    w_in = [S(f"w_in{i}") for i in range(2)]
    res_in, res_set = S("res_in"), S("res_set")
    route_mm, route, e_done, cwt_tr, cwt_done, b2_mm, acc0 = (
        S("route_mm"), S("route"), S("e_done"), S("cwt_tr"), S("cwt_done"), S("b2_mm"), S("acc0"))
    h_mm, g_done, y_mm, acc_done, ln, powed, normed, out_done = (
        S("h_mm"), S("g_done"), S("y_mm"), S("acc_done"), S("ln"), S("pow"), S("normed"), S("out"))
    N = EXPERTS * NC
    TPC = TC // P
    U = 2 * NC
    H_BANKS, Y_BANKS = 4, 3
    TAIL = TOKENS - (TT - 1) * P

    def program_sync(sp):
        def load(e, j):
            at_least(sp, y_mm, (e - 1) * NC * TPC)
            sp.dma_start(w1[:, j % 2], W["w1"][bass.ds(e * 2, 2)].rearrange("h p n -> p h n")).then_inc(w_in[j % 2], 16)
            sp.dma_start(w2[:, j % 2], W["w2"][bass.ds(e * HT, HT)].rearrange("m p n -> p m n")).then_inc(w_in[j % 2], 16)

        load(0, 0)
        load(1, 1)
        attention_done(sp)
        sp.wait_ge(res_set, 1)
        sp.dma_start(res[:, 0:TT - 1, :], x_out[0:(TT - 1) * P, :].rearrange("(t p) e -> p t e", p=P)).then_inc(res_in, 16)
        sp.dma_start(res[0:TAIL, TT - 1, :], x_out[(TT - 1) * P:TOKENS, :]).then_inc(res_in, 16)
        pipeline(sp, lambda e, j: load(e, j), 0, [(2, EXPERTS, 2)], EXPERTS)
        sp.wait_ge(normed, TT)
        flat = out.rearrange("b s e -> (b s) e")
        sp.dma_start(flat[0:(TT - 1) * P, :].rearrange("(t p) e -> p t e", p=P), res[:, 0:TT - 1, :]).then_inc(out_done, 16)
        sp.dma_start(flat[(TT - 1) * P:TOKENS, :], res[0:TAIL, TT - 1, :]).then_inc(out_done, 16)
        sp.wait_ge(out_done, 32)

    def program_pool(pool):
        pool.wait_ge(ln, 2 * TT)
        pool.tensor_scalar(mv[:, :, 1:2], mv[:, :, 1:2], EPS, None, ALU.add).then_inc(powed, 1)
        pool.wait_ge(powed, 1)
        pool.tensor_tensor(mv[:, :, 1:2], mv[:, :, 1:2], W["minus_half"][:, :, None].to_broadcast([P, TT, 1]), ALU.pow
                           ).then_inc(powed, 1)

    def program_tensor(pe):
        attention_done(pe)
        pe.wait_ge(W["in"], W["in_n"])
        pe.wait_ge(W["pad_set"], 1)
        for t in range(TT):
            for h in range(2):
                last = pe.matmul(psum[:, 0, t * EXPERTS:(t + 1) * EXPERTS], tT[:, h, t * P:(t + 1) * P],
                                 W["gate"][:, h, :], start=(h == 0), stop=(h == 1))
        last.then_inc(route_mm, 1)
        pe.wait_ge(route, ROUTE_MARKS)
        for t in range(TT):
            last = pe.transpose(psum[0:EXPERTS, 1 + t // 4, t % 4 * P:(t % 4 + 1) * P], cw[:, t, :], W["identity"])
        last.then_inc(cwt_tr, 1)
        pe.wait_ge(cwt_done, 3)
        for t in range(TT):
            at = (t // 2) if t // 2 < 1 else t // 2 + 3
            last = pe.matmul(psum[:, B2_BANKS[t // 2], t % 2 * DIM:(t % 2 + 1) * DIM], cwT[:, t * P:(t + 1) * P],
                             W["b2"], start=True, stop=True)
        last.then_inc(b2_mm, 1)
        pe.wait_ge(acc0, TT)

        def hidden(n, j):
            if j % NC == 0:
                pe.wait_ge(w_in[j // NC % 2], n // U * 32 + 32)
            c = j % NC
            for m in range(HT):
                at_least(pe, g_done, n * HT + m - H_BANKS + 1)
                for h in range(2):
                    last = pe.matmul(psum[:, (j * HT + m) % H_BANKS, 0:TC], w1[:, j // NC % 2, h, m * P:(m + 1) * P],
                                     tT[:, h, c * TC:(c + 1) * TC], start=(h == 0), stop=(h == 1))
                last.then_inc(h_mm, 1)

        def output(n, j):
            pe.wait_ge(g_done, (n + 1) * HT)
            for t in range(TPC):
                at_least(pe, acc_done, n * TPC + t - Y_BANKS + 1)
                for m in range(HT):
                    last = pe.matmul(psum[:, H_BANKS + (j * TPC + t) % Y_BANKS, 0:DIM],
                                     hT[:, j % 2, m, t * P:(t + 1) * P], w2[:, j // NC % 2, m, :],
                                     start=(m == 0), stop=(m == HT - 1))
                last.then_inc(y_mm, 1)

        def step(n, j):
            if not isinstance(n, int) or n < N:
                hidden(n, j % U)
            if not isinstance(n, int) or n >= 1:
                output(n - 1, (j - 1) % U)

        pipeline(pe, step, U, [(U, N, U)], N + 1)

    B2_BANKS = [0, 4, 5, 6, 7]
    ROUTE_MARKS = 9

    def program_scalar(act):
        act.wait_ge(route, 3)
        act.activation(e21[:, :], e21[:, :], ACT.Exp).then_inc(e_done, 1)
        act.wait_ge(cwt_tr, 1)
        for b in range(3):
            n = min(4, TT - 4 * b) * P
            act.activation(cwT[:, b * 4 * P:b * 4 * P + n], psum[0:EXPERTS, 1 + b, 0:n], ACT.Copy).then_inc(cwt_done, 1)

        def gelu(n, j):
            at_least(act, y_mm, (n - 1) * TPC)
            for m in range(HT):
                act.wait_ge(h_mm, n * HT + m + 1)
                act.activation(hT[:, j % 2, m, :], psum[:, (j * HT + m) % H_BANKS, 0:TC], ACT.Gelu,
                               bias=W["b1"][:, bass.ds(n // NC * HT + m, 1)]).then_inc(g_done, 1)

        pipeline(act, gelu, U, [(U, N, U)], N)

    def program_vector(dve):
        dve.wait_ge(W["in"], W["in_n"])
        dve.memset(res[:, :, :], 0.0).then_inc(res_set, 1)
        c = Chain(dve, route, ROUTE_MARKS)
        c.begin(0)
        dve.wait_ge(route_mm, 1)
        c.did(dve.tensor_tensor(logits[:, :, :], psum[:, 0, 0:TT * EXPERTS].rearrange("p (t e) -> p t e", t=TT),
                                W["gate_b"][:, None, :].to_broadcast([P, TT, EXPERTS]), ALU.add))
        c.wait()
        for t in range(TT):
            last = dve.max(top[:, t, :], logits[:, t, :])
        c.did(last)
        c.wait()
        c.did(dve.tensor_tensor(e21[:, :], top[:, :, 1], top[:, :, 0], ALU.subtract))
        for t in range(TT):
            last = dve.max_index(topi[:, t, :], top[:, t, :], logits[:, t, :])
        c.did(last)
        c.wait()
        c.did(dve.tensor_copy(topf[:, :, :], topi[:, :, 0:TOPK]))
        dve.wait_ge(e_done, 1)
        dve.tensor_scalar(den[:, :], e21[:, :], 1.0, None, ALU.add).then_inc(sh, 1)
        dve.wait_ge(sh, 1)
        dve.reciprocal(share[:, :, 0], den[:, :]).then_inc(sh, 1)
        dve.wait_ge(sh, 2)
        c.did(dve.tensor_tensor(share[:, :, 1], e21[:, :], share[:, :, 0], ALU.mult))
        c.wait()
        for k in range(TOPK):
            last = dve.tensor_tensor(pick[:, k], W["iota"][:, None, :].to_broadcast([P, TT, EXPERTS]),
                                     topf[:, :, k, None].to_broadcast([P, TT, EXPERTS]), ALU.is_equal)
        c.did(last)
        c.wait()
        for k in range(TOPK):
            last = dve.tensor_tensor(pick[:, k], pick[:, k], share[:, :, k, None].to_broadcast([P, TT, EXPERTS]),
                                     ALU.mult)
        c.did(last)
        c.wait()
        c.did(dve.tensor_tensor(cw[:, :, :], pick[:, 0], pick[:, 1], ALU.add))
        c.end()
        dve.wait_ge(b2_mm, 1)
        dve.wait_ge(res_in, 32)
        for t in range(TT):
            dve.tensor_tensor(acc[:, t, :], psum[:, B2_BANKS[t // 2], t % 2 * DIM:(t % 2 + 1) * DIM], res[:, t, :],
                              ALU.add).then_inc(acc0, 1)
        dve.wait_ge(acc0, TT)

        def add(n, j):
            for t in range(TPC):
                tile = j % NC * TPC + t
                dve.wait_ge(y_mm, n * TPC + t + 1)
                at_least(dve, acc_done, n * TPC + t - TT + 1)
                dve.scalar_tensor_tensor(out=acc[:, tile, :], in0=psum[:, H_BANKS + (j * TPC + t) % Y_BANKS, 0:DIM],
                                         scalar=cw[:, tile, bass.ds(n // NC, 1)], in1=acc[:, tile, :],
                                         op0=ALU.mult, op1=ALU.add).then_inc(acc_done, 1)

        pipeline(dve, add, U, [(U, N, U)], N)
        dve.wait_ge(acc_done, N * TPC)
        for t in range(TT):
            dve.bn_stats(st[:, t, :], acc[:, t, :]).then_inc(ln, 1)
        dve.wait_ge(ln, TT)
        for t in range(TT):
            dve.bn_aggr(mv[:, t, :], st[:, t, :]).then_inc(ln, 1)
        dve.wait_ge(powed, 2)
        for t in range(TT):
            dve.tensor_scalar(res[:, t, :], acc[:, t, :], mv[:, t, 0:1], mv[:, t, 1:2], ALU.subtract, ALU.mult
                              ).then_inc(normed, 1)

    sh = S("sh")
    return program_sync, program_pool, program_tensor, program_scalar, program_vector


INPUTS = ["dft", "rank_row", "pos", "masks", "identity", "x", "cls", "w_tok", "b_tok",
          "wqk0", "wv0", "bqk0", "bv0", "wp0", "bp0", "wqk1", "wv1", "wp1", "bp1",
          "g1", "be1", "g2", "be2", "gate", "gate_b", "w1", "b1", "w2", "b2"]


def build(nc, a, out):
    table = nc.dram_tensor("power_table", (ROWS, IMGS), F32, kind="Internal").ap()
    raw = nc.dram_tensor("ring_tokens", (TOKENS, DIM), F32, kind="Internal").ap()
    x_out = nc.dram_tensor("attended", (TOKENS, DIM), F32, kind="Internal").ap()
    with ExitStack() as ctx:
        sem = lambda name: ctx.enter_context(nc.semaphore(name))
        with ExitStack() as first:
            *spec, stored, root_done = spectrum(nc, first, sem, a["x"], table, a["dft"])

        def spectrum_done(eng):
            eng.wait_ge(root_done, GROUPS)
            for s in stored:
                eng.wait_ge(s, 32)

        sb = lambda n, shape, dt=F32: ctx.enter_context(nc.sbuf_tensor(n, shape, dt))
        psum = ctx.enter_context(nc.psum_tensor("psum", [P, 8, 512], F32))
        identity = sb("identity", [P, P])
        masks = sb("masks", [TG, 2, TG])
        pos = sb("pos", [TG, DIM])
        first_bias = sb("first_bias", [TG, DIM])
        minus_half = sb("minus_half", [P, 1])
        x_all = sb("x_all", [TG, TGROUPS, DIM])
        tT = sb("tT", [KH, 2, TPAD])
        iota = sb("iota", [P, EXPERTS])
        gate = sb("gate", [KH, 2, EXPERTS])
        gate_b = sb("gate_b", [P, EXPERTS])
        b1 = sb("b1", [P, EXPERTS * HT])
        b2 = sb("b2", [EXPERTS, DIM])
        half_set, pos_done, pad_set, loaded, iota_set = (
            sem("half_set"), sem("pos_done"), sem("pad_set"), sem("loaded"), sem("iota_set"))
        shared = {"psum": psum, "identity": identity[:, :], "minus_half": minus_half[:, :], "half_set": half_set,
                  "pos_done": pos_done, "pad_set": pad_set, "in": loaded}
        layers = []
        for l in range(2):
            w = dict(shared, mask=masks[:, l, :])
            for n, shape in (("wqk", [KH, 2, QK_TILES * P]), ("wv", [KH, 2, DIM]), ("wp", [KH, 2, DIM]),
                             ("bqk", [P, QK_TILES]), ("bv", [TG, DIM]), ("bp", [TG, DIM])):
                w[n] = sb(f"{n}{l}", shape)[:]
            if l:
                for n in ("g1", "b1", "g2", "b2"):
                    w[n] = sb(f"ln_{n}", [TG, DIM])[:]
            else:
                w["pos"] = pos[:, :]
            layers.append(w)
        moe = dict(shared, gate=gate[:], gate_b=gate_b[:], b1=b1[:], b2=b2[:], iota=iota[:], w1=a["w1"], w2=a["w2"])

        def row(name, n):
            return a[name].to_broadcast([n, a[name].shape[1]])

        loads = [(identity[:, :], a["identity"]), (masks[:], a["masks"]), (pos[:, :], a["pos"]),
                 (gate[:], a["gate"].rearrange("(h p) e -> p h e", h=2)), (gate_b[:, :], row("gate_b", P)),
                 (b1[:, :], a["b1"]), (b2[:, :], a["b2"]),
                 (layers[0]["bqk"], a["bqk0"]), (layers[0]["bv"], row("bv0", TG)),
                 (layers[1]["g1"], row("g1", TG)), (layers[1]["b1"], row("be1", TG)),
                 (layers[1]["g2"], row("g2", TG)), (layers[1]["b2"], row("be2", TG))]
        for l in range(2):
            for n in ("wqk", "wv", "wp"):
                loads.append((layers[l][n], a[f"{n}{l}"].rearrange("(h p) e -> p h e", h=2)))
            loads.append((layers[l]["bp"], row(f"bp{l}", TG)))
        for i in range(TG_IMGS):
            loads.append((first_bias[i * SEQ:i * SEQ + 1, :], a["cls"]))
            loads.append((first_bias[i * SEQ + 1:(i + 1) * SEQ, :], row("b_tok", BINS)))
        for w in layers + [moe]:
            w["in_n"] = 16 * len(loads)

        with ExitStack() as second:
            rings = tokens_of_rings(nc, second, sem, table, a["rank_row"], a["w_tok"], raw, psum, spectrum_done)
        rings_done = rings[-1]
        att0 = attention(nc, ctx, sem, "a0", layers[0], 0, raw, x_all, tT, x_out, rings_done)
        att1 = attention(nc, ctx, sem, "a1", layers[1], 1, raw, x_all, tT, x_out, att0[-1])
        moe_p = experts(nc, ctx, sem, moe, tT, x_out, out, att1[-1])
        block = ctx.enter_context(nc.Block())

        @block.sync
        def _(sp):
            spec[0](sp)
            rings[0](sp)
            att0[0](sp)
            att1[0](sp)
            moe_p[0](sp)

        @block.gpsimd
        def _(pool):
            spec[1](pool)
            rings[1](pool)
            rings_done(pool)
            att0[1](pool)
            att0[-1](pool)
            att1[1](pool)
            moe_p[1](pool)

        @block.tensor
        def _(pe):
            spec[2](pe)
            spectrum_done(pe)
            rings[2](pe)
            rings_done(pe)
            att0[2](pe)
            att0[-1](pe)
            att1[2](pe)
            moe_p[2](pe)

        @block.scalar
        def _(act):
            spec[3](act)
            spectrum_done(act)
            for dst, src in loads:
                act.dma_start(dst, src).then_inc(loaded, 16)
            rings[3](act)
            rings_done(act)
            att0[3](act)
            att0[-1](act)
            att1[3](act)
            moe_p[3](act)

        @block.vector
        def _(dve):
            spec[4](dve)
            rings[4](dve)
            dve.memset(minus_half[:, :], -0.5).then_inc(half_set, 1)
            dve.memset(tT[:, :, TOKENS:TPAD], 0.0).then_inc(pad_set, 1)
            dve.memset(layers[1]["bqk"], 0.0)
            dve.memset(layers[1]["bv"], 0.0).then_inc(half_set, 1)
            for e in range(EXPERTS):
                dve.memset(iota[:, e:e + 1], float(e)).then_inc(iota_set, 1)
            dve.wait_ge(loaded, layers[0]["in_n"])
            dve.tensor_tensor(pos[:, :], pos[:, :], first_bias[:, :], ALU.add).then_inc(pos_done, 1)
            rings_done(dve)
            att0[4](dve)
            att0[-1](dve)
            dve.wait_ge(half_set, 2)
            att1[4](dve)
            dve.wait_ge(iota_set, EXPERTS)
            moe_p[4](dve)


def slots(w):
    lead = w.shape[:-1]
    w = w.reshape(*lead, 3, HEADS, HEAD)
    out = np.zeros((*lead, 2, HEADS, SLOT), w.dtype)
    out[..., :HEAD] = w[..., 0:2, :, :]
    return out.reshape(*lead, 2 * HEADS * SLOT)


def kernel(**inputs):
    import concourse.bacc as _bacc
    from concourse.bass_utils import run_bass_kernel_spmd as _run
    i = {n: np.asarray(v) for n, v in inputs.items()}
    x = np.roll(i["x"], (BATCH // 2, CHANNELS // 2), axis=(0, 1))
    x = x.transpose(2, 0, 1, 3).reshape(SIDE, IMGS, SIDE)
    x = np.concatenate([x[:, :, :HALF], x[:, :, :HALF - 1:-1]], 2)
    wa, wf = i["L0_attn_W_attn"], i["L0_ffn_qkv_w"].T
    ba = i["L0_attn_b_attn"]
    arrays = dict(
        constants(),
        x=np.stack([x[:HALF], x[:HALF - 1:-1]]).reshape(2, HALF, IMGS * SIDE),
        cls=i["L0_tok_cls_token"].reshape(1, DIM), w_tok=i["L0_tok_W"].T, b_tok=i["L0_tok_b"][None],
        wqk0=slots(wa), wv0=wa[:, 2 * DIM:], bqk0=slots(ba).reshape(QK_TILES, P).T, bv0=ba[None, 2 * DIM:],
        wp0=i["L0_attn_W_proj"], bp0=i["L0_attn_b_proj"][None],
        wqk1=slots(wf), wv1=wf[:, 2 * DIM:], wp1=i["L0_ffn_proj_w"].T, bp1=i["L0_ffn_proj_b"][None],
        g1=i["L0_ffn_ln1_g"][None], be1=i["L0_ffn_ln1_b"][None],
        g2=i["L0_ffn_ln2_g"][None], be2=i["L0_ffn_ln2_b"][None],
        gate=i["L0_ffn_gate_w"].T, gate_b=i["L0_ffn_gate_b"][None],
        w1=i["L0_ffn_w1"].transpose(0, 2, 1).reshape(EXPERTS * 2, KH, HIDDEN),
        b1=i["L0_ffn_b1"].reshape(EXPERTS * HT, P).T,
        w2=i["L0_ffn_w2"].transpose(0, 2, 1).reshape(EXPERTS * HT, P, DIM), b2=i["L0_ffn_b2"])
    nc = _bacc.Bacc("TRN2", target_bir_lowering=False, num_devices=1)
    feed, aps = {}, {}
    for n in INPUTS:
        v = np.ascontiguousarray(arrays[n])
        feed[f"in_{n}"] = v
        aps[n] = nc.dram_tensor(f"in_{n}", v.shape, mybir.dt.from_np(v.dtype), kind="ExternalInput").ap()
    out = nc.dram_tensor("out_0", (BATCH, SEQ, DIM), F32, kind="ExternalOutput").ap()
    build(nc, aps, out)
    return _run(nc, [feed], core_ids=[0]).results[0]["out_0"]
```

```python
import math
from contextlib import ExitStack

import numpy as np
import concourse.bass as bass
from concourse import mybir

F32 = mybir.dt.float32
I32 = mybir.dt.int32
ALU = mybir.AluOpType
ACT = mybir.ActivationFunctionType
AX_X = mybir.AxisListType.X

P = 128
BATCH, CHANNELS, SIDE = 64, 3, 224
IMGS = BATCH * CHANNELS
HALF = SIDE // 2
CROP = 192
FREQ = CROP // 2 + 1
PAIR = 2 * FREQ
BINS = 16
BIN = CROP * CROP // BINS
CHUNKS = BIN // P
DIM = 192
SEQ = BINS + 1
ROWS = FREQ * PAIR
EPS = 1e-5
TOKENS = BATCH * SEQ
TG_IMGS = 6
TG = TG_IMGS * SEQ
TGROUPS = -(-BATCH // TG_IMGS)
HEADS, HEAD = 12, 16
SLOT = 32
KH = DIM // 2
SCALE = HEAD ** -0.5
EXPERTS, HIDDEN, TOPK = 8, 768, 2
HT = HIDDEN // P
TT = -(-TOKENS // P)
TPAD = TT * P
TC = 3 * P
NC = TT // 3
MT = TOKENS * TOPK // P + EXPERTS - 1
SHARE_T = TT - 1
TAIL = TOKENS - SHARE_T * P


def constants():
    y = np.arange(HALF)[:, None] + 0.5
    k = np.arange(FREQ)[None, :]
    angle = 2.0 * np.pi * ((2 * y * k) % (2 * SIDE)) / (2 * SIDE)
    dft = np.concatenate([np.cos(angle), np.sin(angle)], 1).astype(np.float32)
    gy, gx = np.meshgrid(np.arange(CROP), np.arange(CROP), indexing="ij")
    dist = np.sqrt((gx - CROP / 2.0) ** 2 + (gy - CROP / 2.0) ** 2).reshape(-1)
    order = np.argsort(dist, kind="stable")
    ky, kx = (gy - CROP // 2).reshape(-1)[order], (gx - CROP // 2).reshape(-1)[order]
    sign = (ky * kx < 0).astype(np.int64)
    row = (np.abs(kx) * 2 + sign) * FREQ + np.abs(ky)
    rank_row = np.ascontiguousarray(row.reshape(BINS * CHUNKS, P).T.astype(np.int32))
    pos = np.arange(SEQ)[:, None].astype(np.float32)
    div = np.exp(np.arange(0, DIM, 2).astype(np.float32) * (-np.log(10000.0) / DIM))
    pe = np.zeros((SEQ, DIM), np.float32)
    pe[:, 0::2] = np.sin(pos * div)
    pe[:, 1::2] = np.cos(pos * div)
    tok = np.arange(TG)
    own = tok[:, None] // SEQ == tok[None, :] // SEQ
    causal = own & (tok[:, None] >= tok[None, :])
    masks = np.stack([np.where(m, 0.0, -1e30) for m in (causal, own)], 1).astype(np.float32)
    n = np.arange(P)
    e = np.arange(EXPERTS)
    return {"dft": dft, "rank_row": rank_row, "masks": masks, "identity": np.eye(P, dtype=np.float32),
            "ring_pos": pe[1:].reshape(BINS // 2, 2, 1, DIM).repeat(BATCH, 2).transpose(1, 2, 0, 3).reshape(
                P, BINS // 2, DIM),
            "cls_pos": pe[None, 0],
            "own": (np.arange(KH)[:, None] // HEAD == np.arange(HPH)).astype(np.float32),
            "before": (n[:, None] < n[None, :]).astype(np.float32), "all_ones": np.ones((P, P), np.float32),
            "iota": np.tile(np.arange(MT, dtype=np.float32), (P, 1)),
            "multiples": np.tile(P * np.arange(TT, dtype=np.float32), (P, 1)),
            "not_past": np.tile((e[None, :] <= e[:, None]).astype(np.float32), (P, 1, 1))}


def at_least(eng, sem, n):
    if not (isinstance(n, int) and n <= 0):
        eng.wait_ge(sem, n)


def pipeline(eng, step, first, loops, end):
    for t in range(first):
        step(t, t)
    for start, stop, unroll in loops:
        with eng.Fori(start // unroll, stop // unroll) as body:
            for j in range(unroll):
                step(body * unroll + j, start + j)
        first = stop
    for t in range(first, end):
        step(t, t)


G_IMGS = 4
GROUPS = IMGS // G_IMGS
UNITS = IMGS // 2
GPC = GROUPS // CHANNELS
UPG = G_IMGS // 2
PIECES = 8
PIECE = PAIR // PIECES
STORES = 16 * (PIECES + 2)
Y_RING, FOLD_RING, A_RING, UV_RING, SS_RING = 4, 2, 4, 2, 2
BODY_G = 4
BODY_U = BODY_G * UPG
S2_LAG = 2
SQ_LAG = 2
RT_LAG = 2


def spectrum(nc, ctx, sem, xh, table, dft_in):
    sb = lambda name, shape, dt=F32: ctx.enter_context(nc.sbuf_tensor(name, shape, dt))
    R = sb("power", [FREQ, PAIR, 2 * BATCH])
    img = sb("img", [HALF, Y_RING, 2, G_IMGS * SIDE])
    fold = sb("fold", [HALF, FOLD_RING, 2, G_IMGS * SIDE])
    dft = sb("dft", [HALF, PAIR])
    far = sb("far", [HALF, 2, 2, PAIR])
    folded = sb("folded", [HALF, A_RING, 2, 2, PAIR])
    odd = sb("odd", [FREQ, 2, 2, PAIR])
    uv = sb("uv", [FREQ, UV_RING, 2, G_IMGS, PAIR])
    ss = sb("ss", [FREQ, SS_RING, 2, G_IMGS, FREQ])
    ps1 = ctx.enter_context(nc.psum_tensor("ps1", [P, 2, 2, 512], F32))
    ps2 = ctx.enter_context(nc.psum_tensor("ps2", [P, 2, 2, 512], F32))

    img_in = [sem(f"img_in{i}") for i in range(Y_RING)]
    dft_in_s = sem("dft_in_s")
    fold_done = sem("fold_done")
    odd_fold = sem("odd_fold")
    dft1_done = sem("dft1_done")
    far_done = sem("far_done")
    folded_done = sem("folded_done")
    dft2_done = sem("dft2_done")
    odd_done = sem("odd_done")
    uv_done = sem("uv_done")
    sq_done = sem("sq_done")
    ss_done = sem("ss_done")
    root_done = sem("root_done")
    root_room = sem("root_room")
    stored = [sem(f"stored{c}") for c in range(CHANNELS)]

    def program_sync(sp):
        sp.dma_start(dft[:, :], dft_in).then_inc(dft_in_s, 16)
        sp.sem_inc(root_room, 2 * GPC)

        def load(g, j):
            at_least(sp, fold_done, g - Y_RING + 1)
            at_least(sp, odd_fold, g - Y_RING + 1)
            sp.dma_start(img[:, j % Y_RING, :, :].rearrange("p h n -> p h n"),
                         xh[:, :, bass.ds(g * G_IMGS * SIDE, G_IMGS * SIDE)].rearrange("h p n -> p h n")
                         ).then_inc(img_in[j % Y_RING], 16)

        def part_of(c, lo, n, rows):
            src = R[:, :, (c % 2) * BATCH:(c % 2) * BATCH + BATCH]
            dst = table.rearrange("(l r) i -> l r i", l=FREQ)[:, :, c * BATCH:(c + 1) * BATCH]
            sp.dma_start(dst[rows, bass.ds(lo, n)], src[rows, bass.ds(lo, n)]).then_inc(stored[c], 16)

        all_but_one, last_row = slice(0, FREQ - 1), slice(FREQ - 1, FREQ)

        for g in range(Y_RING):
            load(g, g)
        with sp.Fori(1, (GPC + 2 * BODY_G) // BODY_G) as body:
            for j in range(BODY_G):
                load(body * BODY_G + j, j)
        for c in range(CHANNELS - 1):
            sp.wait_ge(root_done, GPC * (c + 1))
            first = GPC * (c + 1) + 2 * BODY_G
            with sp.Fori(first // BODY_G, first // BODY_G + PIECES // BODY_G) as body:
                for j in range(BODY_G):
                    load(body * BODY_G + j, j)
                    part_of(c, (body * BODY_G + j - first) * PIECE, PIECE, all_but_one)
            part_of(c, PIECES * PIECE, PAIR - PIECES * PIECE, all_but_one)
            part_of(c, 0, PAIR, last_row)
            if c == 0:
                sp.wait_ge(stored[0], STORES)
                sp.sem_inc(root_room, GPC)
            until = min(first + GPC, GROUPS)
            if until > first + PIECES:
                with sp.Fori((first + PIECES) // BODY_G, until // BODY_G) as body:
                    for j in range(BODY_G):
                        load(body * BODY_G + j, j)
        sp.wait_ge(root_done, GROUPS)
        part_of(CHANNELS - 1, 0, PAIR, all_but_one)
        part_of(CHANNELS - 1, 0, PAIR, last_row)

    def program_pool(pool):
        def fold_group(g, j):
            pool.wait_ge(img_in[j % Y_RING], g // Y_RING * 16 + 16)
            at_least(pool, dft1_done, (g - FOLD_RING + 1) * UPG)
            pool.tensor_tensor(fold[:, j % FOLD_RING, 0], img[:, j % Y_RING, 0], img[:, j % Y_RING, 1], ALU.add
                               ).then_inc(fold_done, 1)

        def sum_group(g, j):
            pool.wait_ge(sq_done, UPG * (g + 1))
            at_least(pool, root_done, g - SS_RING + 1)
            for s in range(2):
                last = pool.tensor_tensor(ss[:, j % SS_RING, s], uv[:, j % UV_RING, s, :, 0:FREQ],
                                          uv[:, j % UV_RING, 1 - s, :, FREQ:PAIR], ALU.add)
            last.then_inc(ss_done, UPG)

        def step(t, j):
            if not isinstance(t, int) or t < GROUPS:
                fold_group(t, j)
            if not isinstance(t, int) or t >= SUM_LAG:
                sum_group(t - SUM_LAG, j - SUM_LAG)

        SUM_LAG = 3
        pipeline(pool, step, BODY_G, [(BODY_G, GROUPS, BODY_G)], GROUPS + SUM_LAG)

    def program_tensor(pe):
        pe.wait_ge(dft_in_s, 16)

        def first_dft(u, j):
            if j % UPG == 0:
                pe.wait_ge(fold_done, u // UPG + 1)
                pe.wait_ge(odd_fold, u // UPG + 1)
            at_least(pe, folded_done, u - 1)
            for i in range(2):
                for chunk in range(2):
                    for part in range(2):
                        x0 = ((j % UPG) * 2 + i) * SIDE + chunk * HALF
                        col = chunk * PAIR + part * FREQ
                        last = pe.matmul(ps1[0:HALF, j % 2, i, col:col + FREQ],
                                         fold[:, j // UPG % FOLD_RING, part, x0:x0 + HALF],
                                         dft[:, part * FREQ:(part + 1) * FREQ], start=True, stop=True)
            last.then_inc(dft1_done, 1)

        def second_dft(u, j):
            pe.wait_ge(folded_done, u + 1)
            at_least(pe, uv_done, u - 1)
            src = folded[:, j % A_RING]
            pe.matmul(ps2[0:FREQ, j % 2, 0, 0:2 * PAIR], dft[:, 0:FREQ], src[:, 0], start=True, stop=True)
            out = ps2[0:FREQ, j % 2, 1, 0:2 * PAIR].rearrange("p (i c) -> p i c", i=2)
            for part in range(2):
                last = pe.matmul(out[:, :, part * FREQ:(part + 1) * FREQ], dft[:, FREQ:PAIR],
                                 src[:, 1, :, (1 - part) * FREQ:(2 - part) * FREQ], start=True, stop=True)
            last.then_inc(dft2_done, 1)

        def step(t, j):
            if not isinstance(t, int) or t < UNITS:
                first_dft(t, j)
            if not isinstance(t, int) or t >= S2_LAG:
                second_dft(t - S2_LAG, j - S2_LAG)

        pipeline(pe, step, BODY_U, [(BODY_U, UNITS, BODY_U)], UNITS + S2_LAG)

    def program_scalar(act):
        def far_copy(u, j):
            act.wait_ge(dft1_done, u + 1)
            at_least(act, folded_done, u - 1)
            act.activation(far[:, j % 2], ps1[0:HALF, j % 2, :, PAIR:2 * PAIR], ACT.Copy).then_inc(far_done, 1)

        def odd_copy(u, j):
            act.wait_ge(dft2_done, u + 1)
            at_least(act, uv_done, u - 1)
            act.activation(odd[:, j % 2], ps2[0:FREQ, j % 2, 1, 0:2 * PAIR].rearrange("p (i c) -> p i c", i=2),
                           ACT.Copy).then_inc(odd_done, 1)

        def square(u, j):
            act.wait_ge(uv_done, u + 1)
            i0 = (j % UPG) * 2
            v = uv[:, j // UPG % UV_RING, :, i0:i0 + 2, :]
            act.activation(v, v, ACT.Square).then_inc(sq_done, 1)

        def root(g, j):
            act.wait_ge(ss_done, UPG * (g + 1))
            act.wait_ge(root_room, g + 1)
            col = (g * G_IMGS) % (2 * BATCH)
            out = R[:, :, bass.ds(col, G_IMGS)].rearrange("p (s k) i -> p s i k", s=2)
            act.activation(out, ss[:, j % SS_RING], ACT.Sqrt).then_inc(root_done, 1)

        ODD = S2_LAG
        SQ = ODD + SQ_LAG
        RT = SQ + 3

        def step(t, j):
            dyn = not isinstance(t, int)
            if dyn or t < UNITS:
                far_copy(t, j)
            if dyn or ODD <= t < UNITS + ODD:
                odd_copy(t - ODD, j - ODD)
            if dyn or SQ <= t < UNITS + SQ:
                square(t - SQ, j - SQ)
            if (j - RT) % UPG == 0 and (dyn or t >= RT):
                root((t - RT) // UPG, (j - RT) // UPG)

        pipeline(act, step, BODY_U, [(BODY_U, UNITS, BODY_U)], UNITS + RT)

    def program_vector(dve):
        def fold_columns(u, j):
            dve.wait_ge(far_done, u + 1)
            at_least(dve, dft2_done, u - A_RING + 1)
            near = ps1[0:HALF, j % 2, :, 0:PAIR]
            for part, op in ((0, ALU.add), (1, ALU.subtract)):
                last = dve.tensor_tensor(folded[:, j % A_RING, part], near, far[:, j % 2], op)
            last.then_inc(folded_done, 1)

        def fold_odd(g, j):
            dve.wait_ge(img_in[j % Y_RING], g // Y_RING * 16 + 16)
            at_least(dve, dft1_done, (g - FOLD_RING + 1) * UPG)
            dve.tensor_tensor(fold[:, j % FOLD_RING, 1], img[:, j % Y_RING, 0], img[:, j % Y_RING, 1], ALU.subtract
                              ).then_inc(odd_fold, 1)

        def combine(u, j):
            dve.wait_ge(odd_done, u + 1)
            if j % UPG == 0:
                at_least(dve, ss_done, u - (UV_RING - 1) * UPG)
            even = ps2[0:FREQ, j % 2, 0, 0:2 * PAIR].rearrange("p (i c) -> p i c", i=2)
            i0 = (j % UPG) * 2
            for part, op in ((0, ALU.subtract), (1, ALU.add)):
                last = dve.tensor_tensor(uv[:, j // UPG % UV_RING, part, i0:i0 + 2, :], even, odd[:, j % 2], op)
            last.then_inc(uv_done, 1)

        ODD = S2_LAG

        def step(t, j):
            if j % UPG == 0 and (not isinstance(t, int) or t + UPG < UNITS):
                fold_odd(t // UPG + 1, j // UPG + 1)
            if not isinstance(t, int) or t < UNITS:
                fold_columns(t, j)
            if not isinstance(t, int) or t >= ODD:
                combine(t - ODD, j - ODD)

        fold_odd(0, 0)
        pipeline(dve, step, BODY_U, [(BODY_U, UNITS - BODY_U, BODY_U)], UNITS + ODD)

    return program_sync, program_pool, program_tensor, program_scalar, program_vector, stored, root_done




def tokens_of_rings(nc, ctx, sem, a, table, raw, ps, spectrum_done):
    sb = lambda name, shape, dt=F32: ctx.enter_context(nc.sbuf_tensor(name, shape, dt))
    RING = 12
    rank_row = sb("rank_row", [P, 2, 2 * CHUNKS], I32)
    wt = sb("w_tok", [P, CHANNELS, CHUNKS, DIM])
    rows = sb("rows", [P, RING, 2, IMGS])
    tok = sb("tok", [P, 2, DIM])
    ring_pos = sb("ring_pos", [P, BINS // 2, DIM])
    b_tok = sb("b_tok", [P, DIM])
    cls = sb("cls", [BATCH, DIM])
    cls_pos = sb("cls_pos", [BATCH, DIM])
    index_in, wt_in = [sem(f"index_in{i}") for i in range(2)], sem("wt_in")
    gathered = [sem(f"gathered{i}") for i in range(RING)]
    rows_used, tok_done, tok_out = sem("rows_used"), sem("tok_done"), sem("tok_out")
    tok_stored = [sem(f"tok_stored{i}") for i in range(2)]
    adds_in, adds_set, cls_set, cls_stored, gate = (
        sem("adds_in"), sem("adds_set"), sem("cls_set"), sem("cls_stored"), sem("gather_gate"))
    PAIRS = BINS // 2
    STEPS = PAIRS * CHUNKS
    UNROLL = 2 * CHUNKS

    def program_sync(sp):
        spectrum_done(sp)
        def load_index(q, j):
            at_least(sp, rows_used, (q - 1) * CHUNKS)
            sp.dma_start(rank_row[:, j % 2, :], a["rank_row"][:, bass.ds(q * 2 * CHUNKS, 2 * CHUNKS)]
                         ).then_inc(index_in[j % 2], 16)

        load_index(0, 0)
        load_index(1, 1)
        for c in range(CHANNELS):
            sp.dma_start(wt[:, c], a["w_tok"][c * BIN:(c + 1) * BIN, :].rearrange("(j p) e -> p j e", p=P)
                         ).then_inc(wt_in, 16)
        for dst, src in ((ring_pos[:, :, :], a["ring_pos"]), (b_tok[:, :], a["b_tok"].to_broadcast([P, DIM])),
                         (cls[:, :], a["cls"].to_broadcast([BATCH, DIM])),
                         (cls_pos[:, :], a["cls_pos"].to_broadcast([BATCH, DIM]))):
            sp.dma_start(dst, src).then_inc(adds_in, 16)
        sp.wait_ge(cls_set, 1)
        sp.dma_start(raw.rearrange("(b s) e -> b s e", s=SEQ)[:, 0, :], cls[:, :]).then_inc(cls_stored, 16)

        def store(q, j):
            sp.wait_ge(tok_out, q + 1)
            for half in range(2):
                sp.dma_start(raw.rearrange("(b s) e -> b s e", s=SEQ)[:, bass.ds(2 * q + half + 1, 1), :],
                             tok[half * BATCH:(half + 1) * BATCH, j % 2, None, :]).then_inc(tok_stored[j % 2], 16)

        def step(q, j):
            if not isinstance(q, int) or q >= 2:
                load_index(q, j)
                store(q - 2, j - 2)

        pipeline(sp, step, 2, [(2, PAIRS, 2)], PAIRS)
        for q in range(PAIRS - 2, PAIRS):
            store(q, q)
        sp.wait_ge(cls_stored, 16)
        for s in tok_stored:
            sp.wait_ge(s, 32 * PAIRS // 2)

    def program_pool(pool):
        spectrum_done(pool)

        def step(n, j):
            at_least(pool, rows_used, n - RING + 1)
            q, chunk = j // CHUNKS % 2, j % CHUNKS
            if chunk == 0:
                pool.wait_ge(index_in[q], n // UNROLL * 16 + 16)
            pool.sem_inc(gate, 1)
            for half in range(2):
                pool.indirect_dma_start(
                    out=rows[:, j % RING, half, :], out_offset=None, in_=table,
                    in_offset=bass.IndirectOffsetOnAxis(
                        ap=rank_row[:, q, half * CHUNKS + chunk, None], axis=0)
                ).then_inc(gathered[j % RING], 16)

        pipeline(pool, step, UNROLL, [(UNROLL, STEPS, UNROLL)], STEPS)

    def program_tensor(pe):
        pe.wait_ge(wt_in, 16 * CHANNELS)

        def step(n, j):
            q, chunk = j // CHUNKS, j % CHUNKS
            if chunk == 0:
                at_least(pe, tok_out, (n - CHUNKS) // CHUNKS)
            pe.wait_ge(gathered[j % RING], n // RING * 32 + 32)
            for c in range(CHANNELS):
                pair = rows[:, j % RING].rearrange("p h (b c) -> p c (h b)", c=CHANNELS)
                last = pe.matmul(ps[:, q % 2, 0:DIM], pair[:, c, :],
                                 wt[:, c, chunk, :], start=(chunk == 0 and c == 0),
                                 stop=(chunk == CHUNKS - 1 and c == CHANNELS - 1))
            last.then_inc(rows_used, 1)

        pipeline(pe, step, UNROLL, [(UNROLL, STEPS, UNROLL)], STEPS)

    def program_vector(dve):
        spectrum_done(dve)
        dve.wait_ge(adds_in, 64)
        dve.tensor_tensor(cls[:, :], cls[:, :], cls_pos[:, :], ALU.add).then_inc(cls_set, 1)
        dve.tensor_tensor(ring_pos[:, :, :], ring_pos[:, :, :], b_tok[:, None, :].to_broadcast([P, BINS // 2, DIM]),
                          ALU.add).then_inc(adds_set, 1)
        dve.wait_ge(adds_set, 1)

        def step(q, j):
            dve.wait_ge(rows_used, (q + 1) * CHUNKS)
            at_least(dve, tok_stored[j % 2], q // 2 * 32)
            dve.tensor_tensor(tok[:, j % 2, None, :], ps[:, j % 2, None, 0:DIM], ring_pos[:, bass.ds(q, 1), :], ALU.add
                              ).then_inc(tok_out, 1)

        pipeline(dve, step, 2, [(2, PAIRS, 2)], PAIRS)

    def done(eng):
        eng.wait_ge(cls_stored, 16)
        for s in tok_stored:
            eng.wait_ge(s, 32 * PAIRS // 2)

    return program_sync, program_pool, program_tensor, program_vector, done, wt_in


class Chain:

    def __init__(self, eng, sem, per):
        self.eng, self.sem, self.per = eng, sem, per

    def begin(self, item):
        self.base, self.n = item * self.per, 0

    def did(self, ins):
        self.n += 1
        return ins.then_inc(self.sem, 1)

    def wait(self):
        self.eng.wait_ge(self.sem, self.base + self.n)

    def end(self):
        assert self.n == self.per, self.n


HPH = HEADS // 2
SLOTS = KH // SLOT
V_OF_CHUNK = [(c * TC) // TG for c in range(NC + 1)]


def attention_buffers(sb):
    return {
        "xT": sb("xT", [KH + 1, 2, TPAD]),
        "qk": sb("qk", [KH, 4, TPAD]),
        "k_own": sb("k_own", [KH, 2, 2, HPH, TG]),
        "v": sb("v", [TG, TGROUPS, HEADS, SLOT]),
        "s": sb("s", [TG, 4, HEADS, TG]),
        "mx": sb("mx", [TG, 4, HEADS]),
        "rs": sb("rs", [TG, 4, HEADS]),
        "pT": sb("pT", [TG, 2, HEADS, TG]),
        "st": sb("st", [P, TT, 6]),
        "mv": sb("mv", [P, TT, 2]),
    }


def inverse_root(pool, W, var, sem, done_before):
    pool.tensor_scalar(var, var, EPS, None, ALU.add).then_inc(sem, 1)
    pool.wait_ge(sem, done_before + 1)
    pool.tensor_tensor(var, var, W["minus_half"][:, :, None].to_broadcast([P, var.shape[1], 1]), ALU.pow
                       ).then_inc(sem, 1)


def statistics(dve, c, x, st, mv, sem):
    for t in range(c * 3, c * 3 + 3):
        last = dve.bn_stats(st[:, t, :], x[:, t, :])
    last.then_inc(sem, 1)
    dve.wait_ge(sem, 2 * c + 1)
    for t in range(c * 3, c * 3 + 3):
        last = dve.bn_aggr(mv[:, t, :], st[:, t, :])
    last.then_inc(sem, 1)


def normalise(dve, c, x, mv, out, powed, sem):
    dve.wait_ge(powed, 2 * (c + 1))
    for t in range(c * 3, c * 3 + 3):
        last = dve.tensor_scalar(out[:, t, :], x[:, t, :], mv[:, t, 0:1], mv[:, t, 1:2], ALU.subtract, ALU.mult)
    last.then_inc(sem, 1)


def attention(sem, name, W, B, layer, raw, x_all, ready):
    S = lambda n: sem(f"{name}_{n}")
    psum = W["psum"]
    xT, qk, k_own, v, s, mx, rs = B["xT"], B["qk"], B["k_own"], B["v"], B["s"], B["mx"], B["rs"]
    pT, st, mv = B["pT"], B["st"], B["mv"]
    L1 = layer == 1
    xin = W["normed"] if L1 else x_all
    z = W["z"] if L1 else x_all
    G = TGROUPS
    QK_BANKS = 4
    scores_psum = psum[0:TG, 0:4, 0:HEADS // 4 * TG]
    probs_psum = psum[0:TG, 4:7, 0:HEADS // 3 * TG]

    raw_in = [S(f"raw_in{c}") for c in range(NC)] if not L1 else None
    xin_done, stat0, pow0, t_tr, tT_done, twice = (
        [S(n) if L1 else None for n in ("xin_done", "stat0", "pow0", "t_tr", "tT", "twice")])
    x_tr, xT_done, qk_mm, qk_done, v_mm, v_done = S("x_tr"), S("xT"), S("qk_mm"), S("qk"), S("v_mm"), S("v")
    k_ready, sc_mm, masked, maxed, less, exped, summed, shared_out = (
        S("k_ready"), S("sc"), S("masked"), S("maxed"), S("less"), S("exp"), S("sum"), S("shared_out"))
    p_tr, pT_done, av, oT_done = S("p_tr"), S("pT"), S("av"), S("oT")
    proj, z_done, stat1, pow1, normed = S("proj"), S("z"), S("stat1"), S("pow1"), S("normed")

    def by_groups(parts):
        for t in range(G + max(lag for lag, _ in parts)):
            for lag, f in parts:
                if lag <= t < G + lag:
                    f(t - lag)

    def output_groups(t):
        return min(G, -(-(t + 1) * P // TG))

    def program_sync(sp):
        if not L1:
            ready(sp)
            for c in range(NC):
                full = min((c + 1) * 3, TOKENS // P)
                sp.dma_start(x_all[:, c * 3:full, :],
                             raw[c * TC:full * P, :].rearrange("(t p) e -> p t e", p=P)).then_inc(raw_in[c], 16)
            sp.dma_start(x_all[0:TAIL, TT - 1, :], raw[SHARE_T * P:TOKENS, :]).then_inc(raw_in[NC - 1], 16)

    def program_pool(pool):
        pool.wait_ge(W["in"], W["in_n"])
        pool.wait_ge(W["half_set"], 1)
        if L1:
            for c in range(NC):
                pool.wait_ge(stat0, 2 * (c + 1))
                inverse_root(pool, W, mv[:, c * 3:c * 3 + 3, 1:2], pow0, 2 * c)

        def subtract_max(g):
            pool.wait_ge(maxed, g + 1)
            pool.tensor_tensor(s[:, g % 4], s[:, g % 4], mx[:, g % 4, :, None].to_broadcast([TG, HEADS, TG]),
                               ALU.subtract).then_inc(less, 1)

        def share_out(g):
            pool.wait_ge(summed, 2 * (g + 1))
            pool.tensor_tensor(s[:, g % 4], s[:, g % 4], rs[:, g % 4, :, None].to_broadcast([TG, HEADS, TG]),
                               ALU.mult).then_inc(shared_out, 1)

        by_groups([(4, share_out), (2, subtract_max)])
        for c in range(NC):
            pool.wait_ge(stat1, 2 * (c + 1))
            inverse_root(pool, W, mv[:, c * 3:c * 3 + 3, 1:2], pow1, 2 * c)
            if L1:
                pool.wait_ge(z_done, 3 * (c + 1))
                part = slice(c * 3, c * 3 + 3)
                pool.tensor_tensor(x_all[:, part, :], z[:, part, :], x_all[:, part, :], ALU.add).then_inc(twice, 1)

    def program_tensor(pe):
        pe.wait_ge(W["in"], W["in_n"])

        def x_transposes(c):
            if L1:
                pe.wait_ge(xin_done, c + 1)
            else:
                pe.wait_ge(raw_in[c], 32 if c == NC - 1 else 16)
            at_least(pe, xT_done, 2 * c)
            for h in range(2):
                for i in range(3):
                    last = pe.transpose(psum[0:KH, h, i * P:(i + 1) * P], xin[:, c * 3 + i, h * KH:(h + 1) * KH],
                                        W["identity"])
            last.then_inc(x_tr, 1)

        def projections(c):
            pe.wait_ge(xT_done, 2 * (c + 1))
            for t in range(4):
                n = c * 4 + t
                at_least(pe, qk_done, n - QK_BANKS + 1)
                for h in range(2):
                    last = pe.matmul(psum[0:KH, 2 + n % QK_BANKS, 0:TC], W["wqk"][:, h, t * KH:(t + 1) * KH],
                                     xT[0:KH, h, c * TC:(c + 1) * TC], start=(h == 0), stop=(h == 1))
                last.then_inc(qk_mm, 1)
            for g in range(V_OF_CHUNK[c], V_OF_CHUNK[c + 1]):
                at_least(pe, v_done, g - 1)
                for h in range(2):
                    last = pe.matmul(psum[0:TG, 6 + g % 2, 0:DIM], xT[0:KH, h, g * TG:(g + 1) * TG],
                                     W["wv"][:, h, :], start=(h == 0), stop=(h == 1))
                last.then_inc(v_mm, 1)

        if not L1:
            pe.wait_ge(W["pad_set"], 1)
        x_transposes(0)
        for c in range(NC):
            if c + 1 < NC:
                x_transposes(c + 1)
            projections(c)
        pe.wait_ge(qk_done, NC * 4)
        pe.wait_ge(v_done, G)
        pe.wait_ge(W["v_pad_set"], 1)

        def scores(g):
            pe.wait_ge(k_ready, g + 1)
            at_least(pe, masked, g)
            for n in range(4):
                last = pe.matmul(scores_psum[:, n, :], qk[:, n // 2, g * TG:(g + 1) * TG],
                                 k_own[:, g % 2, n // 2, n % 2 * 3:n % 2 * 3 + 3, :].rearrange("p h t -> p (h t)"),
                                 start=True, stop=True)
            last.then_inc(sc_mm, 1)

        def p_transposes(g):
            pe.wait_ge(shared_out, g + 1)
            at_least(pe, pT_done, g)
            for n in range(HEADS):
                last = pe.transpose(probs_psum[:, n // 4, n % 4 * TG:(n % 4 + 1) * TG], s[:, g % 4, n, :],
                                    W["identity"][0:TG, 0:TG])
            last.then_inc(p_tr, 1)

        def values(g):
            pe.wait_ge(pT_done, g + 1)
            at_least(pe, oT_done, g)
            for n in range(HEADS):
                slot = n % HPH // 2
                last = pe.matmul(psum[slot * SLOT:(slot + 1) * SLOT, 7, n // HPH * TG:(n // HPH + 1) * TG],
                                 v[:, g, n, :], pT[:, g % 2, n, :], start=(n % 2 == 0), stop=(n % 2 == 1))
            last.then_inc(av, 1)

        by_groups([(5, p_transposes), (6, values), (1, scores)])

        pe.wait_ge(W["ones_set"], 1)

        def out_projection(t):
            pe.wait_ge(oT_done, output_groups(t))
            at_least(pe, z_done, t - 1)
            for h in range(2):
                last = pe.matmul(psum[:, 4 + t % 2, 0:DIM], xT[0:KH + h, h, t * P:(t + 1) * P],
                                 W["wp"][0:KH + h, h, :], start=(h == 0), stop=(h == 1))
            last.then_inc(proj, 1)

        def t_transposes(c):
            pe.wait_ge(normed, c + 1)
            at_least(pe, tT_done, 2 * c)
            for h in range(2):
                for i in range(3):
                    last = pe.transpose(psum[0:KH, h, i * P:(i + 1) * P],
                                        W["normed"][:, c * 3 + i, h * KH:(h + 1) * KH], W["identity"])
            last.then_inc(t_tr, 1)

        def router_logits(c):
            pe.wait_ge(tT_done, 2 * (c + 1))
            for t in range(c * 3, c * 3 + 3):
                for h in range(2):
                    last = pe.matmul(psum[:, 2, t * EXPERTS:(t + 1) * EXPERTS], W["tT"][:, h, t * P:(t + 1) * P],
                                     W["gate"][:, h, :], start=(h == 0), stop=(h == 1))
            last.then_inc(W["logits_mm"], 1)

        for t in range(TT):
            out_projection(t)
        if L1:
            for c in range(NC + 1):
                if c < NC:
                    t_transposes(c)
                if c >= 1:
                    router_logits(c - 1)

    def program_scalar(act):
        act.wait_ge(W["in"], W["in_n"])
        for c in range(NC):
            act.wait_ge(x_tr, c + 1)
            for h in range(2):
                gain = dict(scale=W["g1"][:, h:h + 1], bias=W["b1"][:, h:h + 1]) if L1 else {}
                act.activation(xT[0:KH, h, c * TC:(c + 1) * TC], psum[0:KH, h, 0:TC], ACT.Identity, **gain
                               ).then_inc(xT_done, 1)
            for t in range(4):
                n = c * 4 + t
                act.wait_ge(qk_mm, n + 1)
                bias = {} if L1 else dict(bias=W["bqk"][:, t:t + 1])
                act.activation(qk[:, t, c * TC:(c + 1) * TC], psum[0:KH, 2 + n % QK_BANKS, 0:TC],
                               ACT.Identity, **bias).then_inc(qk_done, 1)

        def own_rows(g):
            if g == 0:
                act.wait_ge(qk_done, NC * 4)
            at_least(act, sc_mm, g - 1)
            for n in range(HPH):
                last = act.activation(k_own[:, g % 2, :, n, :], qk[:, 2:4, g * TG:(g + 1) * TG], ACT.Identity,
                                      scale=W["own"][:, n:n + 1])
            last.then_inc(k_ready, 1)

        def exponent(g):
            act.wait_ge(less, g + 1)
            act.activation(s[:, g % 4], s[:, g % 4], ACT.Exp, scale=SCALE).then_inc(exped, 1)

        def copy_pT(g):
            act.wait_ge(p_tr, g + 1)
            at_least(act, av, g - 1)
            act.activation(pT[:, g % 2].rearrange("p (b h) t -> p b (h t)", b=3), probs_psum, ACT.Copy
                           ).then_inc(pT_done, 1)

        def copy_oT(g):
            act.wait_ge(av, g + 1)
            act.activation(xT[0:KH, :, g * TG:(g + 1) * TG], psum[0:KH, 7, 0:2 * TG].rearrange("p (h t) -> p h t", h=2),
                           ACT.Copy).then_inc(oT_done, 1)

        by_groups([(3, exponent), (0, own_rows), (5, copy_pT), (6, copy_oT)])

        if L1:
            for c in range(NC):
                act.wait_ge(t_tr, c + 1)
                for h in range(2):
                    act.activation(W["tT"][:, h, c * TC:(c + 1) * TC], psum[0:KH, h, 0:TC], ACT.Identity,
                                   scale=W["g2"][:, h:h + 1], bias=W["b2"][:, h:h + 1]).then_inc(tT_done, 1)

    def program_vector(dve):
        dve.wait_ge(W["in"], W["in_n"])
        if L1:
            for c in range(NC + 1):
                if c < NC:
                    statistics(dve, c, x_all, st, mv, stat0)
                if c >= 1:
                    normalise(dve, c - 1, x_all, mv, xin, pow0, xin_done)
        for g in range(G):
            dve.wait_ge(v_mm, g + 1)
            for odd in range(2):
                out = v[:, g, :, odd * HEAD:(odd + 1) * HEAD].rearrange("p (n o) d -> p n o d", o=2)[:, :, odd, :]
                part = psum[0:TG, 6 + g % 2, 0:DIM].rearrange("p (n o d) -> p n o d", o=2, d=HEAD)[:, :, odd, :]
                if L1:
                    last = dve.tensor_copy(out, part)
                else:
                    bias = W["bv"].rearrange("p (n o d) -> p n o d", o=2, d=HEAD)[:, :, odd, :]
                    last = dve.tensor_tensor(out, part, bias, ALU.add)
            last.then_inc(v_done, 1)

        def mask_and_max(g):
            dve.wait_ge(sc_mm, g + 1)
            at_least(dve, p_tr, g - 3)
            dve.tensor_tensor(s[:, g % 4].rearrange("p (b h) t -> p b h t", b=4),
                              scores_psum.rearrange("p b (h t) -> p b h t", t=TG),
                              W["mask"][:, None, None, :].to_broadcast([TG, 4, HEADS // 4, TG]), ALU.add
                              ).then_inc(masked, 1)
            dve.wait_ge(masked, g + 1)
            at_least(dve, less, g - 3)
            dve.tensor_reduce(mx[:, g % 4, :], s[:, g % 4], AX_X, ALU.max).then_inc(maxed, 1)

        def sums(g):
            dve.wait_ge(exped, g + 1)
            at_least(dve, shared_out, g - 3)
            dve.tensor_reduce(rs[:, g % 4, :], s[:, g % 4], AX_X, ALU.add).then_inc(summed, 1)
            dve.wait_ge(summed, 2 * g + 1)
            dve.reciprocal(rs[:, g % 4, :], rs[:, g % 4, :]).then_inc(summed, 1)

        by_groups([(2, mask_and_max), (3, sums)])

        for c in range(NC + 1):
            if c < NC:
                for t in range(c * 3, c * 3 + 3):
                    dve.wait_ge(proj, t + 1)
                    dve.tensor_tensor(z[:, t, :], psum[:, 4 + t % 2, 0:DIM], x_all[:, t, :], ALU.add
                                      ).then_inc(z_done, 1)
                dve.wait_ge(z_done, 3 * (c + 1))
                statistics(dve, c, z, st, mv, stat1)
            if c >= 1:
                normalise(dve, c - 1, z, mv, W["normed"] if L1 else x_all, pow1, normed)
        dve.wait_ge(normed, NC)

    def done(eng):
        eng.wait_ge(normed, NC)
        if L1:
            eng.wait_ge(tT_done, 2 * NC)
            eng.wait_ge(twice, NC)

    return program_sync, program_pool, program_tensor, program_scalar, program_vector, done


def experts(nc, ctx, sem, W, x_all, xs, ys, out, attention_done):
    sb = lambda n, shape, dt=F32: ctx.enter_context(nc.sbuf_tensor(f"moe_{n}", shape, dt))
    S = lambda n: sem(f"moe_{n}")
    w1, normed = W["w1_buf"], W["normed"]
    w2 = sb("w2", [P, EXPERTS, HT, DIM])
    rowin = sb("rowin", [P, 4, DIM])
    rowT = sb("rowT", [KH + 1, 2, 2, P])
    h = sb("h", [P, 2, HIDDEN])
    hT = sb("hT", [P, 2, HIDDEN])
    y = sb("y", [P, 4, DIM])
    back = sb("back", [P, TT, TOPK, DIM])
    logits = sb("logits", [P, TT, EXPERTS])
    top = sb("top", [P, TT, 8])
    topi = sb("topi", [P, TT, 8], mybir.dt.uint32)
    topf = sb("topf", [P, TT, TOPK])
    e21 = sb("e21", [P, TT])
    den = sb("den", [P, TT])
    share = sb("share", [P, TT, TOPK])
    pick = sb("pick", [P, TOPK, TT, EXPERTS])
    cw = sb("cw", [P, TT, EXPERTS])
    cwT = sb("cwT", [EXPERTS, TPAD])
    both = sb("both", [P, TT + 1, EXPERTS])
    count = sb("count", [P, EXPERTS])
    over = sb("over", [P, EXPERTS, TT])
    tiles = sb("tiles", [P, EXPERTS])
    upto = sb("upto", [P, EXPERTS, EXPERTS])
    end = sb("end", [P, EXPERTS])
    start = sb("start", [P, EXPERTS])
    place = sb("place", [P, TT, EXPERTS])
    picked = sb("picked", [P, TOPK, TT, EXPERTS])
    slot_f = sb("slot_f", [P, TOPK, TT])
    slot = sb("slot", [P, TOPK, TT], I32)
    past = sb("past", [1, MT, EXPERTS])
    tile_f = sb("tile_f", [1, MT])
    tile_expert = sb("tile_expert", [1, MT], I32)
    st = sb("st", [P, TT, 6])
    mv = sb("mv", [P, TT, 2])
    psum = W["psum"]
    w2_in, route_mm, route, e_done, counted, slot_done = (
        S("w2_in"), S("route_mm"), S("route"), S("e_done"), S("counted"), S("slot"))
    sent, row_in, x_tr, rowT_done, h_mm, g_done, h_tr, hT_done, y_mm, y_done = (
        S("sent"), [S(f"row_in{i}") for i in range(4)], S("x_tr"), S("rowT"), S("h_mm"), S("g_done"), S("h_tr"),
        S("hT"), S("y_mm"), S("y"))
    y_stored = [S(f"y_stored{i}") for i in range(4)]
    gathered = [S(f"gathered{t}") for t in range(TT)]
    cw_set, cw_tr, cwT_done, b2_mm, biased = S("cw_set"), S("cw_tr"), S("cwT"), S("b2_mm"), S("biased")
    rows_set, summed, stat, powed, final, out_done = (
        S("rows_set"), S("summed"), S("stat"), S("pow"), S("final"), S("out"))
    U = 4
    ROUTE_MARKS = 16
    HALVES = 2

    def tile_rows(t):
        return P if t < SHARE_T else TAIL

    def by_tiles(eng, parts):
        lags = max(lag for lag, _ in parts)

        def step(n, j):
            for lag, f in parts:
                if not isinstance(n, int) or lag <= n < MT + lag:
                    f(n - lag, (j - lag) % U)
        first = 2 * U
        pipeline(eng, step, first, [(first, MT, U)], MT + lags)

    def program_sync(sp):
        attention_done(sp)
        for e in range(0, EXPERTS, 2):
            sp.dma_start(w2[:, e:e + 2], W["w2"][e * HT:(e + 2) * HT].rearrange("(e m) p n -> p e m n", m=HT)
                         ).then_inc(w2_in, 16)
        sp.wait_ge(sent, 16 * TOPK * TT)

        def load(i, j):
            at_least(sp, x_tr, i - 3)
            sp.dma_start(rowin[:, j, :], xs[bass.ds(i * P, P), :]).then_inc(row_in[j], 16)

        def store(i, j):
            sp.wait_ge(y_done, i + 1)
            sp.dma_start(ys[bass.ds(i * P, P), :], y[:, j, :]).then_inc(y_stored[j], 16)

        by_tiles(sp, [(0, load), (4, store)])
        flat = out.rearrange("b s e -> (b s) e")
        for c in range(NC):
            sp.wait_ge(final, c + 1)
            full = min((c + 1) * 3, SHARE_T)
            sp.dma_start(flat[c * TC:full * P, :].rearrange("(t p) e -> p t e", p=P), normed[:, c * 3:full, :]
                         ).then_inc(out_done, 16)
        sp.dma_start(flat[SHARE_T * P:TOKENS, :], normed[0:TAIL, SHARE_T, :]).then_inc(out_done, 16)
        sp.wait_ge(out_done, 16 * (NC + 1))

    def program_pool(pool):
        pool.wait_ge(W["xs_set"], 16)
        pool.wait_ge(slot_done, 1)
        for t in range(TT):
            for k in range(TOPK):
                n = tile_rows(t)
                pool.indirect_dma_start(out=xs, out_offset=bass.IndirectOffsetOnAxis(ap=slot[0:n, k, t, None], axis=0),
                                        in_=normed[0:n, t, :], in_offset=None).then_inc(sent, 16)
        for j in range(4):
            pool.wait_ge(y_stored[j], 16 * (MT // 4))
        pool.wait_ge(rows_set, 1)
        for t in range(TT):
            for k in range(TOPK):
                n = tile_rows(t)
                pool.indirect_dma_start(out=back[0:n, t, k, :], out_offset=None, in_=ys,
                                        in_offset=bass.IndirectOffsetOnAxis(ap=slot[0:n, k, t, None], axis=0)
                                        ).then_inc(gathered[t], 16)
        for c in range(NC):
            pool.wait_ge(stat, 2 * (c + 1))
            inverse_root(pool, W, mv[:, c * 3:c * 3 + 3, 1:2], powed, 2 * c)

    def program_tensor(pe):
        attention_done(pe)
        pe.wait_ge(W["in"], W["in_n"])
        pe.wait_ge(counted, 1)
        pe.matmul(psum[:, 1, 0:(TT + 1) * EXPERTS], W["before"], both[:, :, :].rearrange("p t e -> p (t e)"),
                  start=True, stop=False)
        for ahead in range(TT):
            later = TT - ahead
            last = pe.matmul(psum[:, 1, (ahead + 1) * EXPERTS:(TT + 1) * EXPERTS].rearrange("p (t e) -> p t e", t=later),
                             W["all_ones"], both[:, ahead, None, :].to_broadcast([P, later, EXPERTS]),
                             start=False, stop=(ahead == TT - 1))
        last.then_inc(route_mm, 1)
        pe.wait_ge(cw_set, 1)
        for t in range(TT):
            last = pe.transpose(psum[0:EXPERTS, 3 + t // 4, t % 4 * P:(t % 4 + 1) * P], cw[:, t, :], W["identity"])
        last.then_inc(cw_tr, 1)
        for t in range(TT):
            if t == 0:
                pe.wait_ge(cwT_done, 3)
            at_least(pe, biased, t - 1)
            pe.matmul(psum[:, 6 + t % 2, 0:DIM], cwT[:, t * P:(t + 1) * P], W["b2"], start=True, stop=True
                      ).then_inc(b2_mm, 1)
        pe.wait_ge(biased, TT)
        pe.wait_ge(w2_in, 16 * EXPERTS // 2)
        pe.wait_ge(slot_done, 2)
        pe.wait_ge(rows_set, 1)

        def expert_of(i):
            return nc.values_load(tile_expert[0:1, bass.ds(i, 1)], engines=[mybir.EngineType.PE], min_val=0,
                                  max_val=EXPERTS - 1,
                                  skip_runtime_bounds_check_because="the table is clamped to the last expert")

        def row_transposes(i, j):
            pe.wait_ge(row_in[j], i // 4 * 16 + 16)
            at_least(pe, rowT_done, 2 * i)
            for k in range(2):
                last = pe.transpose(psum[0:KH, 0, k * P:(k + 1) * P], rowin[:, j, k * KH:(k + 1) * KH], W["identity"])
            last.then_inc(x_tr, 1)

        def hidden(i, j):
            e = expert_of(i)
            pe.wait_ge(rowT_done, 2 * (i + 1))
            at_least(pe, g_done, 2 * (i - 1))
            for m in range(HALVES):
                for k in range(2):
                    last = pe.matmul(psum[:, 1 + j % 2 * 2 + m, 0:TC], rowT[0:KH + k, j % 2, k, :],
                                     w1[0:KH + k, bass.ds(e, 1), k, m * TC:(m + 1) * TC].rearrange("p a n -> p (a n)"),
                                     start=(k == 0), stop=(k == 1))
                last.then_inc(h_mm, 1)

        def hidden_transposes(i, j):
            for m in range(HALVES):
                pe.wait_ge(g_done, 2 * i + m + 1)
                at_least(pe, hT_done, 2 * i - 1 + m)
                for n in range(3):
                    last = pe.transpose(psum[:, 5 + m, n * P:(n + 1) * P], h[:, j % 2, m * TC + n * P:m * TC + (n + 1) * P],
                                        W["identity"])
                last.then_inc(h_tr, 1)

        def results(i, j):
            e = expert_of(i)
            pe.wait_ge(hT_done, 2 * (i + 1))
            at_least(pe, y_done, i)
            for m in range(HT):
                last = pe.matmul(psum[:, 7, 0:DIM], hT[:, j % 2, m * P:(m + 1) * P],
                                 w2[:, bass.ds(e, 1), m, :].rearrange("p a n -> p (a n)"),
                                 start=(m == 0), stop=(m == HT - 1))
            last.then_inc(y_mm, 1)

        by_tiles(pe, [(0, row_transposes), (1, hidden), (3, results), (2, hidden_transposes)])

    def program_scalar(act):
        act.wait_ge(route, 3)
        act.activation(e21[:, :], e21[:, :], ACT.Exp).then_inc(e_done, 1)
        act.wait_ge(cw_tr, 1)
        for b in range(3):
            n = min(4, TT - 4 * b) * P
            act.activation(cwT[:, b * 4 * P:b * 4 * P + n], psum[0:EXPERTS, 3 + b, 0:n], ACT.Copy).then_inc(cwT_done, 1)

        def copy_rowT(i, j):
            act.wait_ge(x_tr, i + 1)
            at_least(act, h_mm, 2 * (i - 1))
            for k in range(2):
                act.activation(rowT[0:KH, j % 2, k, :], psum[0:KH, 0, k * P:(k + 1) * P], ACT.Identity,
                               scale=W["g2"][:, k:k + 1], bias=W["be2"][:, k:k + 1]).then_inc(rowT_done, 1)

        def gelu(i, j):
            at_least(act, h_tr, 2 * (i - 1))
            for m in range(HALVES):
                act.wait_ge(h_mm, 2 * i + m + 1)
                act.activation(h[:, j % 2, m * TC:(m + 1) * TC], psum[:, 1 + j % 2 * 2 + m, 0:TC], ACT.Gelu
                               ).then_inc(g_done, 1)

        by_tiles(act, [(0, copy_rowT), (1, gelu)])

    def program_vector(dve):
        attention_done(dve)
        dve.wait_ge(W["in"], W["in_n"])
        dve.memset(rowT[KH:KH + 1], 1.0)
        dve.memset(back[:, SHARE_T], 0.0).then_inc(rows_set, 1)
        c = Chain(dve, route, ROUTE_MARKS)
        c.begin(0)
        dve.wait_ge(W["logits_mm"], NC)
        c.did(dve.tensor_tensor(logits[:, :, :], psum[:, 2, 0:TT * EXPERTS].rearrange("p (t e) -> p t e", t=TT),
                                W["gate_b"][:, None, :].to_broadcast([P, TT, EXPERTS]), ALU.add))
        c.wait()
        for t in range(TT):
            last = dve.max(top[:, t, :], logits[:, t, :])
        c.did(last)
        c.wait()
        c.did(dve.tensor_tensor(e21[:, :], top[:, :, 1], top[:, :, 0], ALU.subtract))
        for t in range(TT):
            last = dve.max_index(topi[:, t, :], top[:, t, :], logits[:, t, :])
        c.did(last)
        c.wait()
        c.did(dve.tensor_copy(topf[:, :, :], topi[:, :, 0:TOPK]))
        c.wait()
        for k in range(TOPK):
            last = dve.tensor_tensor(pick[:, k], W["iota"][:, None, 0:EXPERTS].to_broadcast([P, TT, EXPERTS]),
                                     topf[:, :, k, None].to_broadcast([P, TT, EXPERTS]), ALU.is_equal)
        c.did(last)
        c.wait()
        c.did(dve.tensor_tensor(both[:, 0:TT, :], pick[:, 0], pick[:, 1], ALU.add))
        c.wait()
        dve.memset(both[:, TT, :], 0.0)
        dve.memset(both[TAIL:P, SHARE_T, :], 0.0).then_inc(counted, 1)
        dve.wait_ge(e_done, 1)
        c.did(dve.tensor_scalar(den[:, :], e21[:, :], 1.0, None, ALU.add))
        c.wait()
        c.did(dve.reciprocal(share[:, :, 0], den[:, :]))
        c.wait()
        c.did(dve.tensor_tensor(share[:, :, 1], e21[:, :], share[:, :, 0], ALU.mult))
        dve.wait_ge(route_mm, 1)
        c.did(dve.tensor_copy(count[:, :], psum[:, 1, TT * EXPERTS:(TT + 1) * EXPERTS]))
        c.wait()
        c.did(dve.tensor_tensor(over[:, :, :], count[:, :, None].to_broadcast([P, EXPERTS, TT]),
                                W["multiples"][:, None, :].to_broadcast([P, EXPERTS, TT]), ALU.is_gt))
        c.wait()
        c.did(dve.tensor_reduce(tiles[:, :], over[:, :, :], AX_X, ALU.add))
        c.wait()
        c.did(dve.tensor_tensor(upto[:, :, :], tiles[:, None, :].to_broadcast([P, EXPERTS, EXPERTS]), W["not_past"],
                                ALU.mult))
        c.wait()
        c.did(dve.tensor_reduce(end[:, :], upto[:, :, :], AX_X, ALU.add))
        c.wait()
        dve.tensor_tensor(start[:, :], end[:, :], tiles[:, :], ALU.subtract).then_inc(sh, 1)
        dve.tensor_tensor(past[:, :, :], end[0:1, None, :].to_broadcast([1, MT, EXPERTS]),
                          W["iota"][0:1, 0:MT, None].to_broadcast([1, MT, EXPERTS]), ALU.is_le).then_inc(sh, 1)
        dve.wait_ge(sh, 2)
        dve.tensor_reduce(tile_f[:, :], past[:, :, :], AX_X, ALU.add).then_inc(sh, 1)
        dve.scalar_tensor_tensor(out=place[:, :, :], in0=start[:, None, :].to_broadcast([P, TT, EXPERTS]),
                                 scalar=float(P), in1=psum[:, 1, 0:TT * EXPERTS].rearrange("p (t e) -> p t e", t=TT),
                                 op0=ALU.mult, op1=ALU.add).then_inc(sh, 1)
        dve.wait_ge(sh, 4)
        dve.tensor_scalar(tile_f[:, :], tile_f[:, :], float(EXPERTS - 1), None, ALU.min).then_inc(sh, 1)
        for k in range(TOPK):
            dve.tensor_tensor(picked[:, k], pick[:, k], place[:, :, :], ALU.mult).then_inc(sh, 1)
        dve.wait_ge(sh, 5 + TOPK)
        dve.tensor_reduce(slot_f[:, :, :], picked[:, :, :, :], AX_X, ALU.add).then_inc(sh, 1)
        dve.wait_ge(sh, 6 + TOPK)
        c.did(dve.tensor_copy(slot[:, :, :], slot_f[:, :, :]))
        c.wait()
        dve.sem_inc(slot_done, 1)
        dve.tensor_copy(tile_expert[:, :], tile_f[:, :]).then_inc(slot_done, 1)
        c.end()
        for k in range(TOPK):
            dve.tensor_tensor(picked[:, k], pick[:, k], share[:, :, k, None].to_broadcast([P, TT, EXPERTS]),
                              ALU.mult).then_inc(sh, 1)
        dve.wait_ge(sh, 6 + 2 * TOPK)
        dve.tensor_tensor(cw[:, :, :], picked[:, 0], picked[:, 1], ALU.add).then_inc(cw_set, 1)
        for t in range(TT):
            dve.wait_ge(b2_mm, t + 1)
            dve.tensor_tensor(x_all[:, t, :], psum[:, 6 + t % 2, 0:DIM], x_all[:, t, :], ALU.add).then_inc(biased, 1)

        def copy_hT(i, j):
            for m in range(HALVES):
                dve.wait_ge(h_tr, 2 * i + m + 1)
                if m == 0:
                    at_least(dve, y_mm, i - 1)
                dve.tensor_copy(hT[:, j % 2, m * TC:(m + 1) * TC], psum[:, 5 + m, 0:TC]).then_inc(hT_done, 1)

        def copy_y(i, j):
            dve.wait_ge(y_mm, i + 1)
            at_least(dve, y_stored[j], i // 4 * 16)
            dve.tensor_copy(y[:, j, :], psum[:, 7, 0:DIM]).then_inc(y_done, 1)

        by_tiles(dve, [(3, copy_y), (2, copy_hT)])

        for c in range(NC + 1):
            if c < NC:
                for t in range(c * 3, c * 3 + 3):
                    dve.wait_ge(gathered[t], 16 * TOPK)
                    for k in range(TOPK):
                        dve.scalar_tensor_tensor(out=x_all[:, t, :], in0=back[:, t, k, :], scalar=share[:, t, k:k + 1],
                                                 in1=x_all[:, t, :], op0=ALU.mult, op1=ALU.add).then_inc(summed, 1)
                        dve.wait_ge(summed, t * TOPK + k + 1)
                statistics(dve, c, x_all, st, mv, stat)
            if c >= 1:
                normalise(dve, c - 1, x_all, mv, normed, powed, final)

    sh = S("sh")
    return program_sync, program_pool, program_tensor, program_scalar, program_vector


INPUTS = ["dft", "rank_row", "ring_pos", "cls_pos", "masks", "identity", "own", "before", "all_ones", "iota",
          "multiples", "not_past", "x", "cls", "w_tok", "b_tok",
          "wqk0", "wv0", "bqk0", "bv0", "wp0", "bp0", "wqk1", "wv1", "wp1", "bp1",
          "g1", "be1", "g2", "be2", "gate", "gate_b", "w1", "b1", "w2", "b2"]


def build(nc, a, out):
    dram = lambda name, rows, cols: nc.dram_tensor(name, (rows, cols), F32, kind="Internal").ap()
    table = dram("power_table", ROWS, IMGS)
    raw = dram("ring_tokens", TOKENS, DIM)
    xs = dram("expert_inputs", MT * P, DIM)
    ys = dram("expert_outputs", MT * P, DIM)
    with ExitStack() as ctx:
        sem = lambda name: ctx.enter_context(nc.semaphore(name))
        with ExitStack() as first:
            *spec, stored, root_done = spectrum(nc, first, sem, a["x"], table, a["dft"])

        def spectrum_done(eng):
            eng.wait_ge(root_done, GROUPS)
            for s in stored[:-1]:
                eng.wait_ge(s, STORES)
            eng.wait_ge(stored[-1], 32)

        sb = lambda n, shape, dt=F32: ctx.enter_context(nc.sbuf_tensor(n, shape, dt))
        psum = ctx.enter_context(nc.psum_tensor("psum", [P, 8, 512], F32))
        minus_half = sb("minus_half", [P, 1])
        zeros = sb("zeros", [P, DIM])
        x_all = sb("x_all", [P, TT, DIM])
        half_set, ones_set, zeros_set, pad_set, v_pad_set, loaded, xs_set = (
            sem("half_set"), sem("ones_set"), sem("zeros_set"), sem("pad_set"), sem("v_pad_set"), sem("loaded"), sem("xs_set"))
        shared = {"psum": psum, "minus_half": minus_half[:, :], "half_set": half_set, "ones_set": ones_set,
                  "pad_set": pad_set, "v_pad_set": v_pad_set, "in": loaded,
                  "tT": sb("tT", [KH, 2, TPAD]), "normed": sb("normed", [P, TT, DIM]), "z": sb("z", [P, TT, DIM])}
        loads = []

        def constant(name, shape, *, source=None, broadcast=False):
            buf = sb(f"c_{name}", shape)
            src = a[source or name]
            loads.append((buf[:], src.to_broadcast(shape) if broadcast else src))
            return buf[:]

        for name, shape in (("identity", [P, P]), ("own", [KH, HPH]), ("before", [P, P]), ("all_ones", [P, P]),
                            ("iota", [P, MT]), ("multiples", [P, TT]), ("not_past", [P, EXPERTS, EXPERTS])):
            shared[name] = constant(name, shape)
        masks = constant("masks", [TG, 2, TG])
        layers = []
        for l in range(2):
            w = dict(shared, mask=masks[:, l, :])
            for n, rows, cols in (("wqk", KH, 2 * DIM), ("wv", KH, DIM), ("wp", KH + 1, DIM)):
                w[n] = sb(f"c_{n}{l}", [rows, 2, cols])[:]
                loads.append((w[n][0:KH], a[f"{n}{l}"].rearrange("(h p) e -> p h e", h=2)))
            loads.append((w["wp"][KH:KH + 1, 1, :], a[f"bp{l}"]))
            layers.append(w)
        layers[0]["bqk"] = constant("bqk0", [KH, 4])
        layers[0]["bv"] = constant("bv0", [TG, DIM], broadcast=True)
        for key, name in (("g1", "g1"), ("b1", "be1"), ("g2", "g2"), ("b2", "be2")):
            layers[1][key] = constant(name, [KH, 2])
        gate = sb("c_gate", [KH, 2, EXPERTS])[:]
        loads.append((gate, a["gate"].rearrange("(h p) e -> p h e", h=2)))
        w1_buf = sb("c_w1", [KH + 1, EXPERTS, 2, HIDDEN])
        for e in range(EXPERTS):
            loads.append((w1_buf[0:KH, e], a["w1"][e * 2:(e + 1) * 2].rearrange("h p n -> p h n")))
        loads.append((w1_buf[KH:KH + 1, :, 1, :], a["b1"]))
        layers[1]["gate"], shared["logits_mm"] = gate, sem("logits_mm")
        layers[1]["logits_mm"] = shared["logits_mm"]
        moe = dict(shared, gate_b=constant("gate_b", [P, EXPERTS], broadcast=True), w1_buf=w1_buf,
                   b2=constant("b2", [EXPERTS, DIM]), g2=layers[1]["g2"], be2=layers[1]["b2"],
                   w2=a["w2"], xs_set=xs_set)
        for w in layers + [moe]:
            w["in_n"] = 16 * len(loads)

        with ExitStack() as second:
            rings = tokens_of_rings(nc, second, sem, a, table, raw, psum, spectrum_done)
        rings_done, rings_in = rings[-2:]
        with ExitStack() as third:
            bufs = attention_buffers(lambda n, shape: third.enter_context(nc.sbuf_tensor(n, shape, F32)))
        att0 = attention(sem, "a0", layers[0], bufs, 0, raw, x_all, rings_done)
        att1 = attention(sem, "a1", layers[1], bufs, 1, raw, x_all, att0[-1])
        moe_p = experts(nc, ctx, sem, moe, x_all, xs, ys, out, att1[-1])
        block = ctx.enter_context(nc.Block())

        @block.sync
        def _(sp):
            spec[0](sp)
            rings[0](sp)
            att0[0](sp)
            moe_p[0](sp)

        @block.gpsimd
        def _(pool):
            spec[1](pool)
            rings[1](pool)
            rings_done(pool)
            att0[1](pool)
            att0[-1](pool)
            att1[1](pool)
            moe_p[1](pool)

        @block.tensor
        def _(pe):
            spec[2](pe)
            spectrum_done(pe)
            rings[2](pe)
            rings_done(pe)
            att0[2](pe)
            att0[-1](pe)
            att1[2](pe)
            moe_p[2](pe)

        @block.scalar
        def _(act):
            spec[3](act)
            spectrum_done(act)
            act.wait_ge(rings_in, 16 * CHANNELS)
            for dst, src in loads:
                act.dma_start(dst, src).then_inc(loaded, 16)
            act.wait_ge(zeros_set, 1)
            act.dma_start(xs.rearrange("(t p) e -> p t e", p=P), zeros[:, None, :].to_broadcast([P, MT, DIM])
                          ).then_inc(xs_set, 16)
            rings_done(act)
            att0[3](act)
            att0[-1](act)
            att1[3](act)
            moe_p[3](act)

        @block.vector
        def _(dve):
            spec[4](dve)
            spectrum_done(dve)
            dve.memset(zeros[:, :], 0.0).then_inc(zeros_set, 1)
            dve.memset(minus_half[:, :], -0.5).then_inc(half_set, 1)
            dve.memset(x_all[TAIL:P, TT - 1, :], 0.0).then_inc(pad_set, 1)
            rings[3](dve)
            rings_done(dve)
            dve.memset(bufs["xT"][KH:KH + 1], 1.0).then_inc(ones_set, 1)
            dve.memset(bufs["v"][:], 0.0).then_inc(v_pad_set, 1)
            dve.wait_ge(v_pad_set, 1)
            att0[4](dve)
            att0[-1](dve)
            att1[4](dve)
            moe_p[4](dve)


def kernel(**inputs):
    import concourse.bacc as _bacc
    from concourse.bass_utils import run_bass_kernel_spmd as _run
    i = {n: np.asarray(v) for n, v in inputs.items()}
    x = np.roll(i["x"], (BATCH // 2, CHANNELS // 2), axis=(0, 1))
    x = x.transpose(2, 0, 1, 3).reshape(SIDE, IMGS, SIDE)
    x = np.concatenate([x[:, :, :HALF], x[:, :, :HALF - 1:-1]], 2)
    wa, wf, ba = i["L0_attn_W_attn"], i["L0_ffn_qkv_w"].T, i["L0_attn_b_attn"]
    arrays = dict(
        constants(),
        x=np.stack([x[:HALF], x[:HALF - 1:-1]]).reshape(2, HALF, IMGS * SIDE),
        cls=i["L0_tok_cls_token"].reshape(1, DIM), w_tok=i["L0_tok_W"].T, b_tok=i["L0_tok_b"][None],
        wqk0=wa[:, :2 * DIM], wv0=wa[:, 2 * DIM:], bqk0=ba[:2 * DIM].reshape(4, KH).T, bv0=ba[None, 2 * DIM:],
        wp0=i["L0_attn_W_proj"], bp0=i["L0_attn_b_proj"][None],
        wqk1=wf[:, :2 * DIM], wv1=wf[:, 2 * DIM:], wp1=i["L0_ffn_proj_w"].T, bp1=i["L0_ffn_proj_b"][None],
        g1=i["L0_ffn_ln1_g"].reshape(2, KH).T, be1=i["L0_ffn_ln1_b"].reshape(2, KH).T,
        g2=i["L0_ffn_ln2_g"].reshape(2, KH).T, be2=i["L0_ffn_ln2_b"].reshape(2, KH).T,
        gate=i["L0_ffn_gate_w"].T, gate_b=i["L0_ffn_gate_b"][None],
        w1=i["L0_ffn_w1"].transpose(0, 2, 1).reshape(EXPERTS * 2, KH, HIDDEN),
        b1=i["L0_ffn_b1"][None],
        w2=i["L0_ffn_w2"].transpose(0, 2, 1).reshape(EXPERTS * HT, P, DIM), b2=i["L0_ffn_b2"])
    nc = _bacc.Bacc("TRN2", target_bir_lowering=False, num_devices=1)
    feed, aps = {}, {}
    for n in INPUTS:
        v = np.ascontiguousarray(arrays[n])
        feed[f"in_{n}"] = v
        aps[n] = nc.dram_tensor(f"in_{n}", v.shape, mybir.dt.from_np(v.dtype), kind="ExternalInput").ap()
    out = nc.dram_tensor("out_0", (BATCH, SEQ, DIM), F32, kind="ExternalOutput").ap()
    build(nc, aps, out)
    return _run(nc, [feed], core_ids=[0]).results[0]["out_0"]
```

```python
from contextlib import ExitStack

import numpy as np
import concourse.bass as bass
from concourse import mybir

F32 = mybir.dt.float32
I32 = mybir.dt.int32
ALU = mybir.AluOpType
ACT = mybir.ActivationFunctionType
AX_X = mybir.AxisListType.X

P = 128
BATCH, CHANNELS, SIDE = 64, 3, 224
IMGS = BATCH * CHANNELS
HALF = SIDE // 2
CROP = 192
FREQ = CROP // 2 + 1
PAIR = 2 * FREQ
BINS = 16
BIN = CROP * CROP // BINS
CHUNKS = BIN // P
DIM = 192
SEQ = BINS + 1
ROWS = FREQ * PAIR
EPS = 1e-5
TOKENS = BATCH * SEQ
TG_IMGS = 6
TG = TG_IMGS * SEQ
TGROUPS = -(-BATCH // TG_IMGS)
HEADS, HEAD = 12, 16
SLOT = 32
KH = DIM // 2
SCALE = HEAD ** -0.5
EXPERTS, HIDDEN, TOPK = 8, 768, 2
HT = HIDDEN // P
TT = -(-TOKENS // P)
TPAD = TT * P
TC = 3 * P
NC = TT // 3
MT = TOKENS * TOPK // P + EXPERTS - 1
SHARE_T = TT - 1
TAIL = TOKENS - SHARE_T * P


def constants():
    y = np.arange(HALF)[:, None] + 0.5
    k = np.arange(FREQ)[None, :]
    angle = 2.0 * np.pi * ((2 * y * k) % (2 * SIDE)) / (2 * SIDE)
    dft = np.concatenate([np.cos(angle), np.sin(angle)], 1).astype(np.float32)
    gy, gx = np.meshgrid(np.arange(CROP), np.arange(CROP), indexing="ij")
    dist = np.sqrt((gx - CROP / 2.0) ** 2 + (gy - CROP / 2.0) ** 2).reshape(-1)
    order = np.argsort(dist, kind="stable")
    ky, kx = (gy - CROP // 2).reshape(-1)[order], (gx - CROP // 2).reshape(-1)[order]
    sign = (ky * kx < 0).astype(np.int64)
    row = (np.abs(kx) * 2 + sign) * FREQ + np.abs(ky)
    rank_row = np.ascontiguousarray(row.reshape(BINS * CHUNKS, P).T.astype(np.int32))
    pos = np.arange(SEQ)[:, None].astype(np.float32)
    div = np.exp(np.arange(0, DIM, 2).astype(np.float32) * (-np.log(10000.0) / DIM))
    pe = np.zeros((SEQ, DIM), np.float32)
    pe[:, 0::2] = np.sin(pos * div)
    pe[:, 1::2] = np.cos(pos * div)
    tok = np.arange(TG)
    own = tok[:, None] // SEQ == tok[None, :] // SEQ
    causal = own & (tok[:, None] >= tok[None, :])
    masks = np.stack([np.where(m, 0.0, -1e30) for m in (causal, own)], 1).astype(np.float32)
    n = np.arange(P)
    e = np.arange(EXPERTS)
    return {"dft": dft, "rank_row": rank_row, "masks": masks, "identity": np.eye(P, dtype=np.float32),
            "ring_pos": pe[1:].reshape(BINS // 2, 2, 1, DIM).repeat(BATCH, 2).transpose(1, 2, 0, 3).reshape(
                P, BINS // 2, DIM),
            "cls_pos": pe[None, 0],
            "own": (np.arange(KH)[:, None] // HEAD == np.arange(HPH)).astype(np.float32),
            "before": (n[:, None] < n[None, :]).astype(np.float32), "all_ones": np.ones((P, P), np.float32),
            "iota": np.tile(np.arange(MT, dtype=np.float32), (P, 1)),
            "multiples": np.tile(P * np.arange(TT, dtype=np.float32), (P, 1)),
            "not_past": np.tile((e[None, :] <= e[:, None]).astype(np.float32), (P, 1, 1))}


def at_least(eng, sem, n):
    if not (isinstance(n, int) and n <= 0):
        eng.wait_ge(sem, n)


def pipeline(eng, step, first, loops, end):
    for t in range(first):
        step(t, t)
    for start, stop, unroll in loops:
        with eng.Fori(start // unroll, stop // unroll) as body:
            for j in range(unroll):
                step(body * unroll + j, start + j)
        first = stop
    for t in range(first, end):
        step(t, t)


G_IMGS = 4
GROUPS = IMGS // G_IMGS
UNITS = IMGS // 2
PASSES = 3
PASS_ENDS = [20, 36, 48]
R_GROUPS = PASS_ENDS[1]
UPG = G_IMGS // 2
PIECES = 8
PIECE = PAIR // PIECES
STORES = 16 * (PIECES + 2)
Y_RING, FOLD_RING, A_RING, UV_RING, SS_RING = 4, 2, 4, 2, 2
BODY_G = 4
BODY_U = BODY_G * UPG
S2_LAG = 2
SQ_LAG = 2


def spectrum(nc, ctx, sem, xh, table, dft_in):
    sb = lambda name, shape, dt=F32: ctx.enter_context(nc.sbuf_tensor(name, shape, dt))
    R = sb("power", [FREQ, PAIR, R_GROUPS * G_IMGS])
    img = sb("img", [HALF, Y_RING, 2, G_IMGS * SIDE])
    fold = sb("fold", [HALF, FOLD_RING, 2, G_IMGS * SIDE])
    dft = sb("dft", [HALF, PAIR])
    far = sb("far", [HALF, 2, 2, PAIR])
    folded = sb("folded", [HALF, A_RING, 2, 2, PAIR])
    odd = sb("odd", [FREQ, 2, 2, PAIR])
    uv = sb("uv", [FREQ, UV_RING, 2, G_IMGS, PAIR])
    ss = sb("ss", [FREQ, SS_RING, 2, G_IMGS, FREQ])
    ps1 = ctx.enter_context(nc.psum_tensor("ps1", [P, 2, 2, 512], F32))
    ps2 = ctx.enter_context(nc.psum_tensor("ps2", [P, 2, 2, 512], F32))

    img_in = [sem(f"img_in{i}") for i in range(Y_RING)]
    dft_in_s = sem("dft_in_s")
    fold_done = sem("fold_done")
    odd_fold = sem("odd_fold")
    dft1_done = sem("dft1_done")
    far_done = sem("far_done")
    folded_done = sem("folded_done")
    dft2_done = sem("dft2_done")
    odd_done = sem("odd_done")
    uv_done = sem("uv_done")
    sq_done = sem("sq_done")
    ss_done = sem("ss_done")
    root_done = sem("root_done")
    root_room = sem("root_room")
    stored = [sem(f"stored{p}") for p in range(PASSES)]

    def program_sync(sp):
        sp.dma_start(dft[:, :], dft_in).then_inc(dft_in_s, 16)
        sp.sem_inc(root_room, R_GROUPS)

        def load(g, j):
            at_least(sp, fold_done, g - Y_RING + 1)
            at_least(sp, odd_fold, g - Y_RING + 1)
            sp.dma_start(img[:, j % Y_RING, :, :].rearrange("p h n -> p h n"),
                         xh[:, :, bass.ds(g * G_IMGS * SIDE, G_IMGS * SIDE)].rearrange("h p n -> p h n")
                         ).then_inc(img_in[j % Y_RING], 16)

        def part_of(p, lo, n, rows):
            images = slice(G_IMGS * ([0] + PASS_ENDS)[p], G_IMGS * PASS_ENDS[p])
            offset = R_GROUPS * G_IMGS if p == PASSES - 1 else 0
            held = slice(images.start - offset, images.stop - offset)
            dst = table.rearrange("(l r) i -> l r i", l=FREQ)[:, :, images]
            sp.dma_start(dst[rows, bass.ds(lo, n)], R[:, :, held][rows, bass.ds(lo, n)]).then_inc(stored[p], 16)

        all_but_one, last_row = slice(0, FREQ - 1), slice(FREQ - 1, FREQ)
        AHEAD = 2 * BODY_G

        for g in range(Y_RING):
            load(g, g)
        at = Y_RING
        for p in range(PASSES - 1):
            first = PASS_ENDS[p] + AHEAD
            with sp.Fori(at // BODY_G, first // BODY_G) as body:
                for j in range(BODY_G):
                    load(body * BODY_G + j, j)
            sp.wait_ge(root_done, PASS_ENDS[p])
            at = min(first + PIECES, GROUPS)
            per_load = PIECES // (at - first)
            with sp.Fori(first // BODY_G, at // BODY_G) as body:
                for j in range(BODY_G):
                    load(body * BODY_G + j, j)
                    for n in range(per_load):
                        part_of(p, ((body * BODY_G + j - first) * per_load + n) * PIECE, PIECE, all_but_one)
            part_of(p, PIECES * PIECE, PAIR - PIECES * PIECE, all_but_one)
            part_of(p, 0, PAIR, last_row)
            if p == 0:
                sp.wait_ge(stored[0], STORES)
                sp.sem_inc(root_room, GROUPS - R_GROUPS)
        sp.wait_ge(root_done, GROUPS)
        part_of(PASSES - 1, 0, PAIR, all_but_one)
        part_of(PASSES - 1, 0, PAIR, last_row)

    def program_pool(pool):
        def fold_group(g, j):
            pool.wait_ge(img_in[j % Y_RING], g // Y_RING * 16 + 16)
            at_least(pool, dft1_done, (g - FOLD_RING + 1) * UPG)
            pool.tensor_tensor(fold[:, j % FOLD_RING, 0], img[:, j % Y_RING, 0], img[:, j % Y_RING, 1], ALU.add
                               ).then_inc(fold_done, 1)

        def sum_group(g, j):
            pool.wait_ge(sq_done, UPG * (g + 1))
            at_least(pool, root_done, g - SS_RING + 1)
            for s in range(2):
                last = pool.tensor_tensor(ss[:, j % SS_RING, s], uv[:, j % UV_RING, s, :, 0:FREQ],
                                          uv[:, j % UV_RING, 1 - s, :, FREQ:PAIR], ALU.add)
            last.then_inc(ss_done, UPG)

        def step(t, j):
            if not isinstance(t, int) or t < GROUPS:
                fold_group(t, j)
            if not isinstance(t, int) or t >= SUM_LAG:
                sum_group(t - SUM_LAG, j - SUM_LAG)

        SUM_LAG = 3
        pipeline(pool, step, BODY_G, [(BODY_G, GROUPS, BODY_G)], GROUPS + SUM_LAG)

    def program_tensor(pe):
        pe.wait_ge(dft_in_s, 16)

        def first_dft(u, j):
            if j % UPG == 0:
                pe.wait_ge(fold_done, u // UPG + 1)
                pe.wait_ge(odd_fold, u // UPG + 1)
            at_least(pe, folded_done, u - 1)
            for i in range(2):
                for chunk in range(2):
                    for part in range(2):
                        x0 = ((j % UPG) * 2 + i) * SIDE + chunk * HALF
                        col = chunk * PAIR + part * FREQ
                        last = pe.matmul(ps1[0:HALF, j % 2, i, col:col + FREQ],
                                         fold[:, j // UPG % FOLD_RING, part, x0:x0 + HALF],
                                         dft[:, part * FREQ:(part + 1) * FREQ], start=True, stop=True)
            last.then_inc(dft1_done, 1)

        def second_dft(u, j):
            pe.wait_ge(folded_done, u + 1)
            at_least(pe, uv_done, u - 1)
            src = folded[:, j % A_RING]
            pe.matmul(ps2[0:FREQ, j % 2, 0, 0:2 * PAIR], dft[:, 0:FREQ], src[:, 0], start=True, stop=True)
            out = ps2[0:FREQ, j % 2, 1, 0:2 * PAIR].rearrange("p (i c) -> p i c", i=2)
            for part in range(2):
                last = pe.matmul(out[:, :, part * FREQ:(part + 1) * FREQ], dft[:, FREQ:PAIR],
                                 src[:, 1, :, (1 - part) * FREQ:(2 - part) * FREQ], start=True, stop=True)
            last.then_inc(dft2_done, 1)

        def step(t, j):
            if not isinstance(t, int) or t < UNITS:
                first_dft(t, j)
            if not isinstance(t, int) or t >= S2_LAG:
                second_dft(t - S2_LAG, j - S2_LAG)

        pipeline(pe, step, BODY_U, [(BODY_U, UNITS, BODY_U)], UNITS + S2_LAG)

    def program_scalar(act):
        def far_copy(u, j):
            act.wait_ge(dft1_done, u + 1)
            at_least(act, folded_done, u - 1)
            act.activation(far[:, j % 2], ps1[0:HALF, j % 2, :, PAIR:2 * PAIR], ACT.Copy).then_inc(far_done, 1)

        def odd_copy(u, j):
            act.wait_ge(dft2_done, u + 1)
            at_least(act, uv_done, u - 1)
            act.activation(odd[:, j % 2], ps2[0:FREQ, j % 2, 1, 0:2 * PAIR].rearrange("p (i c) -> p i c", i=2),
                           ACT.Copy).then_inc(odd_done, 1)

        def square(u, j):
            act.wait_ge(uv_done, u + 1)
            i0 = (j % UPG) * 2
            v = uv[:, j // UPG % UV_RING, :, i0:i0 + 2, :]
            act.activation(v, v, ACT.Square).then_inc(sq_done, 1)

        def root(g, j):
            act.wait_ge(ss_done, UPG * (g + 1))
            act.wait_ge(root_room, g + 1)
            col = (g * G_IMGS) % (R_GROUPS * G_IMGS)
            out = R[:, :, bass.ds(col, G_IMGS)].rearrange("p (s k) i -> p s i k", s=2)
            act.activation(out, ss[:, j % SS_RING], ACT.Sqrt).then_inc(root_done, 1)

        ODD = S2_LAG
        SQ = ODD + SQ_LAG
        RT = SQ + 3

        def step(t, j):
            dyn = not isinstance(t, int)
            if dyn or t < UNITS:
                far_copy(t, j)
            if dyn or ODD <= t < UNITS + ODD:
                odd_copy(t - ODD, j - ODD)
            if dyn or SQ <= t < UNITS + SQ:
                square(t - SQ, j - SQ)
            if (j - RT) % UPG == 0 and (dyn or t >= RT):
                root((t - RT) // UPG, (j - RT) // UPG)

        pipeline(act, step, BODY_U, [(BODY_U, UNITS, BODY_U)], UNITS + RT)

    def program_vector(dve):
        def fold_columns(u, j):
            dve.wait_ge(far_done, u + 1)
            at_least(dve, dft2_done, u - A_RING + 1)
            near = ps1[0:HALF, j % 2, :, 0:PAIR]
            for part, op in ((0, ALU.add), (1, ALU.subtract)):
                last = dve.tensor_tensor(folded[:, j % A_RING, part], near, far[:, j % 2], op)
            last.then_inc(folded_done, 1)

        def fold_odd(g, j):
            dve.wait_ge(img_in[j % Y_RING], g // Y_RING * 16 + 16)
            at_least(dve, dft1_done, (g - FOLD_RING + 1) * UPG)
            dve.tensor_tensor(fold[:, j % FOLD_RING, 1], img[:, j % Y_RING, 0], img[:, j % Y_RING, 1], ALU.subtract
                              ).then_inc(odd_fold, 1)

        def combine(u, j):
            dve.wait_ge(odd_done, u + 1)
            if j % UPG == 0:
                at_least(dve, ss_done, u - (UV_RING - 1) * UPG)
            even = ps2[0:FREQ, j % 2, 0, 0:2 * PAIR].rearrange("p (i c) -> p i c", i=2)
            i0 = (j % UPG) * 2
            for part, op in ((0, ALU.subtract), (1, ALU.add)):
                last = dve.tensor_tensor(uv[:, j // UPG % UV_RING, part, i0:i0 + 2, :], even, odd[:, j % 2], op)
            last.then_inc(uv_done, 1)

        ODD = S2_LAG

        def step(t, j):
            if j % UPG == 0 and (not isinstance(t, int) or t + UPG < UNITS):
                fold_odd(t // UPG + 1, j // UPG + 1)
            if not isinstance(t, int) or t < UNITS:
                fold_columns(t, j)
            if not isinstance(t, int) or t >= ODD:
                combine(t - ODD, j - ODD)

        fold_odd(0, 0)
        pipeline(dve, step, BODY_U, [(BODY_U, UNITS - BODY_U, BODY_U)], UNITS + ODD)

    return program_sync, program_pool, program_tensor, program_scalar, program_vector, stored, root_done




def tokens_of_rings(nc, ctx, sem, rank_row, index_in, a, table, raw, W, xT, qk, spectrum_done):
    ps = W["psum"]
    sb = lambda name, shape, dt=F32: ctx.enter_context(nc.sbuf_tensor(name, shape, dt))
    RING = 12
    wt = sb("w_tok", [P, CHANNELS, CHUNKS, DIM])
    rows = sb("rows", [P, RING, 2, IMGS])
    tok = sb("tok", [P, 2, DIM])
    batchT = sb("batchT", [KH, 2, 2, P])
    ring_pos = sb("ring_pos", [P, BINS // 2, DIM])
    b_tok = sb("b_tok", [P, DIM])
    cls = sb("cls", [BATCH, DIM])
    cls_pos = sb("cls_pos", [BATCH, DIM])
    wt_in = sem("wt_in")
    gathered = [sem(f"gathered{i}") for i in range(RING)]
    rows_used, tok_done, tok_out = sem("rows_used"), sem("tok_done"), sem("tok_out")
    tok_stored = [sem(f"tok_stored{i}") for i in range(2)]
    adds_in, adds_set, cls_set, cls_stored, gate = (
        sem("adds_in"), sem("adds_set"), sem("cls_set"), sem("cls_stored"), sem("gather_gate"))
    turned, batch_set, batch_mm, qk_out = sem("turned"), sem("batch_set"), sem("batch_mm"), W["qk_out"]
    PAIRS = BINS // 2
    STEPS = PAIRS * CHUNKS
    UNROLL = 2 * CHUNKS

    def program_sync(sp):
        spectrum_done(sp)
        def load_index(q, j):
            at_least(sp, rows_used, (q - 1) * CHUNKS)
            sp.dma_start(rank_row[:, j % 2, :], a["rank_row"][:, bass.ds(q * 2 * CHUNKS, 2 * CHUNKS)]
                         ).then_inc(index_in[j % 2], 16)

        for c in range(CHANNELS):
            sp.dma_start(wt[:, c], a["w_tok"][c * BIN:(c + 1) * BIN, :].rearrange("(j p) e -> p j e", p=P)
                         ).then_inc(wt_in, 16)
        for dst, src in ((ring_pos[:, :, :], a["ring_pos"]), (b_tok[:, :], a["b_tok"].to_broadcast([P, DIM])),
                         (cls[:, :], a["cls"].to_broadcast([BATCH, DIM])),
                         (cls_pos[:, :], a["cls_pos"].to_broadcast([BATCH, DIM]))):
            sp.dma_start(dst, src).then_inc(adds_in, 16)
        sp.wait_ge(cls_set, 1)
        sp.dma_start(raw.rearrange("(b s) e -> b s e", s=SEQ)[:, 0, :], cls[:, :]).then_inc(cls_stored, 16)

        def store(q, j):
            sp.wait_ge(tok_out, q + 1)
            for half in range(2):
                sp.dma_start(raw.rearrange("(b s) e -> b s e", s=SEQ)[:, bass.ds(2 * q + half + 1, 1), :],
                             tok[half * BATCH:(half + 1) * BATCH, j % 2, None, :]).then_inc(tok_stored[j % 2], 16)

        def step(q, j):
            if not isinstance(q, int) or q >= 2:
                load_index(q, j)
                store(q - 2, j - 2)

        pipeline(sp, step, 2, [(2, PAIRS, 2)], PAIRS)
        for q in range(PAIRS - 2, PAIRS):
            store(q, q)
        sp.wait_ge(cls_stored, 16)
        for s in tok_stored:
            sp.wait_ge(s, 32 * PAIRS // 2)

    def program_pool(pool):
        spectrum_done(pool)

        def step(n, j):
            at_least(pool, rows_used, n - RING + 1)
            q, chunk = j // CHUNKS % 2, j % CHUNKS
            if chunk == 0:
                pool.wait_ge(index_in[q], n // UNROLL * 16 + 16)
            pool.sem_inc(gate, 1)
            for half in range(2):
                pool.indirect_dma_start(
                    out=rows[:, j % RING, half, :], out_offset=None, in_=table,
                    in_offset=bass.IndirectOffsetOnAxis(
                        ap=rank_row[:, q, half * CHUNKS + chunk, None], axis=0)
                ).then_inc(gathered[j % RING], 16)

        pipeline(pool, step, UNROLL, [(UNROLL, STEPS, UNROLL)], STEPS)

    def by_position(buf, first, count):
        return buf[0:KH, :, 0:TOKENS].rearrange("p h (b s) -> p h s b", s=SEQ)[:, :, bass.ds(first, count), :]

    def program_tensor(pe):
        pe.wait_ge(wt_in, 16 * CHANNELS)

        def turn(b, j):
            if isinstance(b, int) and b == 0:
                pe.wait_ge(W["in"], W["in_n"])
                pe.wait_ge(cls_set, 1)
                source, rows_of = cls, BATCH
            else:
                pe.wait_ge(tok_out, b)
                pe.wait_ge(batch_set, b)
                source, rows_of = tok[:, (j + 1) % 2], P
            for h in range(2):
                last = pe.transpose(ps[0:KH, 2, h * P:h * P + rows_of], source[:, h * KH:(h + 1) * KH],
                                    W["identity"][0:rows_of, 0:rows_of])
            last.then_inc(turned, 1)

        def project(b, j):
            pe.wait_ge(batch_set, b + 1)
            at_least(pe, qk_out, b)
            n = BATCH if isinstance(b, int) and b == 0 else P
            for t in range(4):
                for h in range(2):
                    last = pe.matmul(ps[0:KH, 3, t * P:t * P + n], W["wqk"][:, h, t * KH:(t + 1) * KH],
                                     batchT[:, j % 2, h, 0:n], start=(h == 0), stop=(h == 1))
            last.then_inc(batch_mm, 1)

        def step(n, j):
            q, chunk = j // CHUNKS, j % CHUNKS
            turns, projects = ({6: 0, 12: 1}, {9: 0, 15: 1}) if q == 1 else ({6: q}, {9: q}) if q else ({}, {})
            if chunk in turns:
                turn(turns[chunk] if q == 1 else n // CHUNKS, turns[chunk])
            if chunk in projects:
                project(projects[chunk] if q == 1 else n // CHUNKS, projects[chunk])
            if chunk == 0:
                at_least(pe, tok_out, (n - CHUNKS) // CHUNKS)
            pe.wait_ge(gathered[j % RING], n // RING * 32 + 32)
            for c in range(CHANNELS):
                pair = rows[:, j % RING].rearrange("p h (b c) -> p c (h b)", c=CHANNELS)
                last = pe.matmul(ps[:, q % 2, 0:DIM], pair[:, c, :],
                                 wt[:, c, chunk, :], start=(chunk == 0 and c == 0),
                                 stop=(chunk == CHUNKS - 1 and c == CHANNELS - 1))
            last.then_inc(rows_used, 1)

        pipeline(pe, step, UNROLL, [(UNROLL, STEPS, UNROLL)], STEPS)
        turn(PAIRS, PAIRS)
        project(PAIRS, PAIRS)

    def program_scalar(act):
        act.wait_ge(W["in"], W["in_n"])

        def batch(b, j):
            cls_batch = isinstance(b, int) and b == 0
            first, count = (0, 1) if cls_batch else (2 * b - 1, 2)
            n = count * BATCH
            act.wait_ge(turned, b + 1)
            part = ps[0:KH, 2, 0:2 * P].rearrange("p (h n) -> p h n", h=2)[:, :, 0:n]
            act.activation(by_position(xT, first, count), part.rearrange("p h (s b) -> p h s b", b=BATCH), ACT.Copy)
            at_least(act, batch_mm, b - 1)
            act.activation(batchT[:, j % 2, :, 0:n], part, ACT.Copy).then_inc(batch_set, 1)
            act.wait_ge(batch_mm, b + 1)
            for t in range(4):
                last = act.activation(by_position(qk, first, count)[:, t], ps[0:KH, 3, t * P:t * P + n].rearrange(
                    "p (s b) -> p s b", b=BATCH), ACT.Identity, bias=W["bqk"][:, t:t + 1])
            last.then_inc(qk_out, 1)

        pipeline(act, batch, 2, [(2, PAIRS, 2)], PAIRS + 1)

    def program_vector(dve):
        spectrum_done(dve)
        dve.wait_ge(adds_in, 64)
        dve.tensor_tensor(cls[:, :], cls[:, :], cls_pos[:, :], ALU.add).then_inc(cls_set, 1)
        dve.tensor_tensor(ring_pos[:, :, :], ring_pos[:, :, :], b_tok[:, None, :].to_broadcast([P, BINS // 2, DIM]),
                          ALU.add).then_inc(adds_set, 1)
        dve.wait_ge(adds_set, 1)

        def step(q, j):
            dve.wait_ge(rows_used, (q + 1) * CHUNKS)
            at_least(dve, tok_stored[j % 2], q // 2 * 32)
            if not isinstance(q, int) or q >= 2:
                dve.wait_ge(turned, q)
            dve.tensor_tensor(tok[:, j % 2, None, :], ps[:, j % 2, None, 0:DIM], ring_pos[:, bass.ds(q, 1), :], ALU.add
                              ).then_inc(tok_out, 1)

        pipeline(dve, step, 2, [(2, PAIRS, 2)], PAIRS)

    def done(eng):
        eng.wait_ge(cls_stored, 16)
        for s in tok_stored:
            eng.wait_ge(s, 32 * PAIRS // 2)

    return program_sync, program_pool, program_tensor, program_scalar, program_vector, done, wt_in


class Chain:

    def __init__(self, eng, sem, per):
        self.eng, self.sem, self.per = eng, sem, per

    def begin(self, item):
        self.base, self.n = item * self.per, 0

    def did(self, ins):
        self.n += 1
        return ins.then_inc(self.sem, 1)

    def wait(self):
        self.eng.wait_ge(self.sem, self.base + self.n)

    def end(self):
        assert self.n == self.per, self.n


HPH = HEADS // 2
SLOTS = KH // SLOT


def attention_buffers(sb):
    return {
        "k_own": sb("k_own", [KH, 2, 2, HPH, TG]),
        "v": sb("v", [TG, TGROUPS, HEADS, SLOT]),
        "s": sb("s", [TG, 4, HEADS, TG]),
        "mx": sb("mx", [TG, 4, HEADS]),
        "rs": sb("rs", [TG, 4, HEADS]),
        "pT": sb("pT", [TG, 2, HEADS, TG]),
        "st": sb("st", [P, TT, 6]),
        "mv": sb("mv", [P, TT, 2]),
        "st_next": sb("st_next", [P, TT, 6]),
        "mv_next": sb("mv_next", [P, TT, 2]),
    }


def inverse_root(pool, W, var, sem, done_before):
    pool.tensor_scalar(var, var, EPS, None, ALU.add).then_inc(sem, 1)
    pool.wait_ge(sem, done_before + 1)
    pool.tensor_tensor(var, var, W["minus_half"][:, :, None].to_broadcast([P, var.shape[1], 1]), ALU.pow
                       ).then_inc(sem, 1)


def statistics(dve, c, x, st, mv, sem):
    for t in range(c * 3, c * 3 + 3):
        last = dve.bn_stats(st[:, t, :], x[:, t, :])
    last.then_inc(sem, 1)
    dve.wait_ge(sem, 2 * c + 1)
    for t in range(c * 3, c * 3 + 3):
        last = dve.bn_aggr(mv[:, t, :], st[:, t, :])
    last.then_inc(sem, 1)


def normalise(dve, c, x, mv, out, powed, sem):
    dve.wait_ge(powed, 2 * (c + 1))
    for t in range(c * 3, c * 3 + 3):
        last = dve.tensor_scalar(out[:, t, :], x[:, t, :], mv[:, t, 0:1], mv[:, t, 1:2], ALU.subtract, ALU.mult)
    last.then_inc(sem, 1)


def attention(sem, name, W, B, layer, raw, x_all, ready):
    S = lambda n: sem(f"{name}_{n}")
    psum = W["psum"]
    xT, qk, k_own, v, s, mx, rs = W["xT"], W["qk"], B["k_own"], B["v"], B["s"], B["mx"], B["rs"]
    pT, st, mv = B["pT"], B["st"], B["mv"]
    L1 = layer == 1
    xin = W["normed"] if L1 else x_all
    z = W["z"] if L1 else x_all
    G = TGROUPS
    QK_BANKS = 4
    scores_psum = psum[0:TG, 0:4, 0:HEADS // 4 * TG]
    probs_psum = psum[0:TG, 4:7, 0:HEADS // 3 * TG]

    raw_in = [S(f"raw_in{c}") for c in range(NC)] if not L1 else None
    x_tr, xT_done, qk_mm, qk_done = [S(n) if L1 else None for n in ("x_tr", "xT", "qk_mm", "qk")]
    v_mm, v_done = S("v_mm"), S("v")
    t_tr, tT_done, twice = [S(n) if L1 else None for n in ("t_tr", "tT", "twice")]
    stat0, pow0 = [S(n) if not L1 else None for n in ("stat0", "pow0")]
    xin_done = W["xin_done"]
    k_ready, sc_mm, masked, maxed, less, exped, summed, shared_out = (
        S("k_ready"), S("sc"), S("masked"), S("maxed"), S("less"), S("exp"), S("sum"), S("shared_out"))
    p_tr, pT_done, av, oT_done = S("p_tr"), S("pT"), S("av"), S("oT")
    proj, z_done, stat1, pow1, normed = S("proj"), S("z"), S("stat1"), S("pow1"), S("normed")

    def qk_complete(eng):
        if L1:
            eng.wait_ge(qk_done, NC * 4)
        else:
            eng.wait_ge(W["qk_out"], BINS // 2 + 1)

    def by_groups(parts, tile_part=None):
        tiles = 0
        for t in range(G + max(lag for lag, _ in parts)):
            for lag, f in parts:
                if lag <= t < G + lag:
                    f(t - lag)
            if tile_part and t >= G + 2:
                while tiles < TT and (t == G + 5 or (output_groups(tiles) <= t - 6 and tiles < 3 * (t - G - 1))):
                    tile_part(tiles)
                    tiles += 1

    def output_groups(t):
        return min(G, -(-(t + 1) * P // TG))

    def program_sync(sp):
        if not L1:
            ready(sp)
            for c in range(NC):
                full = min((c + 1) * 3, TOKENS // P)
                sp.dma_start(x_all[:, c * 3:full, :],
                             raw[c * TC:full * P, :].rearrange("(t p) e -> p t e", p=P)).then_inc(raw_in[c], 16)
            sp.dma_start(x_all[0:TAIL, TT - 1, :], raw[SHARE_T * P:TOKENS, :]).then_inc(raw_in[NC - 1], 16)

    def program_pool(pool):
        pool.wait_ge(W["in"], W["in_n"])
        pool.wait_ge(W["half_set"], 1)
        def subtract_max(g):
            pool.wait_ge(maxed, g + 1)
            pool.tensor_tensor(s[:, g % 4], s[:, g % 4], mx[:, g % 4, :, None].to_broadcast([TG, HEADS, TG]),
                               ALU.subtract).then_inc(less, 1)

        def share_out(g):
            pool.wait_ge(summed, 2 * (g + 1))
            pool.tensor_tensor(s[:, g % 4], s[:, g % 4], rs[:, g % 4, :, None].to_broadcast([TG, HEADS, TG]),
                               ALU.mult).then_inc(shared_out, 1)

        by_groups([(4, share_out), (2, subtract_max)])
        for c in range(NC if L1 else NC + 1):
            if c < NC:
                pool.wait_ge(stat1, 2 * (c + 1))
                inverse_root(pool, W, mv[:, c * 3:c * 3 + 3, 1:2], pow1, 2 * c)
            if not L1 and c >= 1:
                pool.wait_ge(stat0, 2 * c)
                inverse_root(pool, W, B["mv_next"][:, c * 3 - 3:c * 3, 1:2], pow0, 2 * (c - 1))
            if L1:
                pool.wait_ge(z_done, 3 * (c + 1))
                part = slice(c * 3, c * 3 + 3)
                pool.tensor_tensor(x_all[:, part, :], z[:, part, :], x_all[:, part, :], ALU.add).then_inc(twice, 1)

    def program_tensor(pe):
        pe.wait_ge(W["in"], W["in_n"])

        def x_transposes(c):
            pe.wait_ge(xin_done, c + 1)
            at_least(pe, xT_done, 2 * c)
            for h in range(2):
                for i in range(3):
                    last = pe.transpose(psum[0:KH, h, i * P:(i + 1) * P], xin[:, c * 3 + i, h * KH:(h + 1) * KH],
                                        W["identity"])
            last.then_inc(x_tr, 1)

        def projections(c):
            pe.wait_ge(xT_done, 2 * (c + 1))
            for t in range(4):
                n = c * 4 + t
                at_least(pe, qk_done, n - QK_BANKS + 1)
                for h in range(2):
                    last = pe.matmul(psum[0:KH, 2 + n % QK_BANKS, 0:TC], W["wqk"][:, h, t * KH:(t + 1) * KH],
                                     xT[0:KH, h, c * TC:(c + 1) * TC], start=(h == 0), stop=(h == 1))
                last.then_inc(qk_mm, 1)

        def project_v(g):
            at_least(pe, v_done, g - 1)
            for h in range(2):
                last = pe.matmul(psum[0:TG, 6 + g % 2, 0:DIM], xT[0:KH, h, g * TG:(g + 1) * TG],
                                 W["wv"][:, h, :], start=(h == 0), stop=(h == 1))
            last.then_inc(v_mm, 1)

        if L1:
            x_transposes(0)
            for c in range(NC):
                if c + 1 < NC:
                    x_transposes(c + 1)
                projections(c)
        else:
            pe.wait_ge(W["pad_set"], 1)
        qk_complete(pe)
        for g in range(G):
            project_v(g)

        def scores(g):
            pe.wait_ge(k_ready, g + 1)
            at_least(pe, masked, g)
            for n in range(4):
                last = pe.matmul(scores_psum[:, n, :], qk[:, n // 2, g * TG:(g + 1) * TG],
                                 k_own[:, g % 2, n // 2, n % 2 * 3:n % 2 * 3 + 3, :].rearrange("p h t -> p (h t)"),
                                 start=True, stop=True)
            last.then_inc(sc_mm, 1)

        def p_transposes(g):
            if g == 0:
                pe.wait_ge(v_done, G)
                pe.wait_ge(W["v_pad_set"], 1)
            pe.wait_ge(shared_out, g + 1)
            at_least(pe, pT_done, g)
            for n in range(HEADS):
                last = pe.transpose(probs_psum[:, n // 4, n % 4 * TG:(n % 4 + 1) * TG], s[:, g % 4, n, :],
                                    W["identity"][0:TG, 0:TG])
            last.then_inc(p_tr, 1)

        def values(g):
            pe.wait_ge(pT_done, g + 1)
            at_least(pe, oT_done, g)
            for n in range(HEADS):
                slot = n % HPH // 2
                last = pe.matmul(psum[slot * SLOT:(slot + 1) * SLOT, 7, n // HPH * TG:(n // HPH + 1) * TG],
                                 v[:, g, n, :], pT[:, g % 2, n, :], start=(n % 2 == 0), stop=(n % 2 == 1))
            last.then_inc(av, 1)

        def out_projection(t):
            if t == 0:
                pe.wait_ge(W["ones_set"], 1)
                pe.wait_ge(masked, G)
            pe.wait_ge(oT_done, output_groups(t))
            at_least(pe, z_done, t - 1)
            for h in range(2):
                last = pe.matmul(psum[:, t % 2, 0:DIM], xT[0:KH + h, h, t * P:(t + 1) * P],
                                 W["wp"][0:KH + h, h, :], start=(h == 0), stop=(h == 1))
            last.then_inc(proj, 1)

        def t_transposes(c):
            pe.wait_ge(normed, c + 1)
            at_least(pe, tT_done, 2 * c)
            for h in range(2):
                for i in range(3):
                    last = pe.transpose(psum[0:KH, 4 + h, i * P:(i + 1) * P],
                                        W["normed"][:, c * 3 + i, h * KH:(h + 1) * KH], W["identity"])
            last.then_inc(t_tr, 1)

        def router_logits(c):
            pe.wait_ge(tT_done, 2 * (c + 1))
            for t in range(c * 3, c * 3 + 3):
                for h in range(2):
                    last = pe.matmul(psum[:, 2, t * EXPERTS:(t + 1) * EXPERTS], W["tT"][:, h, t * P:(t + 1) * P],
                                     W["gate"][:, h, :], start=(h == 0), stop=(h == 1))
            last.then_inc(W["logits_mm"], 1)

        by_groups([(5, p_transposes), (6, values), (1, scores)], out_projection)
        if L1:
            for c in range(NC + 1):
                if c < NC:
                    t_transposes(c)
                if c >= 1:
                    router_logits(c - 1)

    def program_scalar(act):
        act.wait_ge(W["in"], W["in_n"])

        def copy_xT(c):
            act.wait_ge(x_tr, c + 1)
            for h in range(2):
                act.activation(xT[0:KH, h, c * TC:(c + 1) * TC], psum[0:KH, h, 0:TC], ACT.Identity,
                               scale=W["g1"][:, h:h + 1], bias=W["b1"][:, h:h + 1]).then_inc(xT_done, 1)

        def copy_qk(c):
            for t in range(4):
                n = c * 4 + t
                act.wait_ge(qk_mm, n + 1)
                act.activation(qk[:, t, c * TC:(c + 1) * TC], psum[0:KH, 2 + n % QK_BANKS, 0:TC], ACT.Copy
                               ).then_inc(qk_done, 1)

        def own_rows(g):
            at_least(act, sc_mm, g - 1)
            for n in range(HPH):
                last = act.activation(k_own[:, g % 2, :, n, :], qk[:, 2:4, g * TG:(g + 1) * TG], ACT.Identity,
                                      scale=W["own"][:, n:n + 1])
            last.then_inc(k_ready, 1)

        if L1:
            copy_xT(0)
            for c in range(NC):
                if c + 1 < NC:
                    copy_xT(c + 1)
                if c == NC - 1:
                    act.wait_ge(qk_done, 4)
                    own_rows(0)
                copy_qk(c)
        else:
            qk_complete(act)
            own_rows(0)
        qk_complete(act)

        def later_own_rows(g):
            if g:
                own_rows(g)

        def exponent(g):
            act.wait_ge(less, g + 1)
            act.activation(s[:, g % 4], s[:, g % 4], ACT.Exp, scale=SCALE).then_inc(exped, 1)

        def copy_pT(g):
            act.wait_ge(p_tr, g + 1)
            at_least(act, av, g - 1)
            act.activation(pT[:, g % 2].rearrange("p (b h) t -> p b (h t)", b=3), probs_psum, ACT.Copy
                           ).then_inc(pT_done, 1)

        def copy_oT(g):
            act.wait_ge(av, g + 1)
            act.activation(xT[0:KH, :, g * TG:(g + 1) * TG], psum[0:KH, 7, 0:2 * TG].rearrange("p (h t) -> p h t", h=2),
                           ACT.Copy).then_inc(oT_done, 1)

        by_groups([(3, exponent), (0, later_own_rows), (5, copy_pT), (6, copy_oT)])

        if L1:
            for c in range(NC):
                act.wait_ge(t_tr, c + 1)
                for h in range(2):
                    act.activation(W["tT"][:, h, c * TC:(c + 1) * TC], psum[0:KH, 4 + h, 0:TC], ACT.Identity,
                                   scale=W["g2"][:, h:h + 1], bias=W["b2"][:, h:h + 1]).then_inc(tT_done, 1)

    def program_vector(dve):
        dve.wait_ge(W["in"], W["in_n"])
        for g in range(G):
            dve.wait_ge(v_mm, g + 1)
            for odd in range(2):
                out = v[:, g, :, odd * HEAD:(odd + 1) * HEAD].rearrange("p (n o) d -> p n o d", o=2)[:, :, odd, :]
                part = psum[0:TG, 6 + g % 2, 0:DIM].rearrange("p (n o d) -> p n o d", o=2, d=HEAD)[:, :, odd, :]
                if L1:
                    last = dve.tensor_copy(out, part)
                else:
                    bias = W["bv"].rearrange("p (n o d) -> p n o d", o=2, d=HEAD)[:, :, odd, :]
                    last = dve.tensor_tensor(out, part, bias, ALU.add)
            last.then_inc(v_done, 1)

        def mask_and_max(g):
            dve.wait_ge(sc_mm, g + 1)
            at_least(dve, p_tr, g - 3)
            dve.tensor_tensor(s[:, g % 4].rearrange("p (b h) t -> p b h t", b=4),
                              scores_psum.rearrange("p b (h t) -> p b h t", t=TG),
                              W["mask"][:, None, None, :].to_broadcast([TG, 4, HEADS // 4, TG]), ALU.add
                              ).then_inc(masked, 1)
            dve.wait_ge(masked, g + 1)
            at_least(dve, less, g - 3)
            dve.tensor_reduce(mx[:, g % 4, :], s[:, g % 4], AX_X, ALU.max).then_inc(maxed, 1)

        def sums(g):
            dve.wait_ge(exped, g + 1)
            at_least(dve, shared_out, g - 3)
            dve.tensor_reduce(rs[:, g % 4, :], s[:, g % 4], AX_X, ALU.add).then_inc(summed, 1)
            dve.wait_ge(summed, 2 * g + 1)
            dve.reciprocal(rs[:, g % 4, :], rs[:, g % 4, :]).then_inc(summed, 1)

        by_groups([(2, mask_and_max), (3, sums)])

        for c in range(NC + 1 if L1 else NC + 2):
            if c < NC:
                if not L1:
                    dve.wait_ge(raw_in[c], 32 if c == NC - 1 else 16)
                for t in range(c * 3, c * 3 + 3):
                    dve.wait_ge(proj, t + 1)
                    dve.tensor_tensor(z[:, t, :], psum[:, t % 2, 0:DIM], x_all[:, t, :], ALU.add
                                      ).then_inc(z_done, 1)
                dve.wait_ge(z_done, 3 * (c + 1))
                statistics(dve, c, z, st, mv, stat1)
            if 1 <= c <= NC:
                normalise(dve, c - 1, z, mv, W["normed"] if L1 else x_all, pow1, normed)
                if not L1:
                    dve.wait_ge(normed, c)
                    statistics(dve, c - 1, x_all, B["st_next"], B["mv_next"], stat0)
            if not L1 and c >= 2:
                normalise(dve, c - 2, x_all, B["mv_next"], W["normed"], pow0, xin_done)
        dve.wait_ge(normed, NC)

    def done(eng):
        eng.wait_ge(normed, NC)
        if L1:
            eng.wait_ge(tT_done, 2 * NC)
            eng.wait_ge(twice, NC)

    return program_sync, program_pool, program_tensor, program_scalar, program_vector, done


def experts(nc, ctx, sem, W, x_all, xs, ys, out, attention_done):
    sb = lambda n, shape, dt=F32: ctx.enter_context(nc.sbuf_tensor(f"moe_{n}", shape, dt))
    S = lambda n: sem(f"moe_{n}")
    w1, normed = W["w1_buf"], W["normed"]
    w2 = sb("w2", [P, EXPERTS, HT, DIM])
    rowin = sb("rowin", [P, 4, DIM])
    rowT = sb("rowT", [KH + 1, 2, 2, P])
    w1_now = sb("w1_now", [KH + 1, 2, 2, HIDDEN])
    hT = sb("hT", [P, 2, HIDDEN])
    y = sb("y", [P, 4, DIM])
    back = sb("back", [P, TT, TOPK, DIM])
    logits = sb("logits", [P, TT, EXPERTS])
    top = sb("top", [P, TT, 8])
    topi = sb("topi", [P, TT, 8], mybir.dt.uint32)
    topf = sb("topf", [P, TT, TOPK])
    e21 = sb("e21", [P, TT])
    den = sb("den", [P, TT])
    share = sb("share", [P, TT, TOPK])
    pick = sb("pick", [P, TOPK, TT, EXPERTS])
    cw = sb("cw", [P, TT, EXPERTS])
    cwT = sb("cwT", [EXPERTS, TPAD])
    both = sb("both", [P, TT + 1, EXPERTS])
    count = sb("count", [P, EXPERTS])
    over = sb("over", [P, EXPERTS, TT])
    tiles = sb("tiles", [P, EXPERTS])
    upto = sb("upto", [P, EXPERTS, EXPERTS])
    end = sb("end", [P, EXPERTS])
    start = sb("start", [P, EXPERTS])
    place = sb("place", [P, TT, EXPERTS])
    picked = sb("picked", [P, TOPK, TT, EXPERTS])
    slot_f = sb("slot_f", [P, TOPK, TT])
    slot = sb("slot", [P, TOPK, TT], I32)
    past = sb("past", [1, MT, EXPERTS])
    tile_f = sb("tile_f", [1, MT])
    tile_expert = sb("tile_expert", [1, MT], I32)
    st = sb("st", [P, TT, 6])
    mv = sb("mv", [P, TT, 2])
    psum = W["psum"]
    w2_in, route_mm, route, e_done, counted, slot_done = (
        S("w2_in"), S("route_mm"), S("route"), S("e_done"), S("counted"), S("slot"))
    sent, row_in, x_tr, rowT_done, w1_set, h_mm, g_done, y_mm, y_done = (
        S("sent"), [S(f"row_in{i}") for i in range(4)], S("x_tr"), S("rowT"), S("w1_set"), S("h_mm"), S("g_done"),
        S("y_mm"), S("y"))
    y_stored = [S(f"y_stored{i}") for i in range(4)]
    gathered = [S(f"gathered{t}") for t in range(TT)]
    cw_set, cw_tr, cwT_done, b2_mm, biased = S("cw_set"), S("cw_tr"), S("cwT"), S("b2_mm"), S("biased")
    rows_set, summed, stat, powed, final, out_done = (
        S("rows_set"), S("summed"), S("stat"), S("pow"), S("final"), S("out"))
    U = 4
    ROUTE_MARKS = 16
    HALVES = 2

    def tile_rows(t):
        return P if t < SHARE_T else TAIL

    def by_tiles(eng, parts):
        lags = max(lag for lag, _ in parts)

        def step(n, j):
            for lag, f in parts:
                if not isinstance(n, int) or lag <= n < MT + lag:
                    f(n - lag, (j - lag) % U)
        first = 2 * U
        pipeline(eng, step, first, [(first, MT, U)], MT + lags)

    def expert_of(i, engine):
        return nc.values_load(tile_expert[0:1, bass.ds(i, 1)], engines=[engine], min_val=0, max_val=EXPERTS - 1,
                              skip_runtime_bounds_check_because="the table is clamped to the last expert")

    def program_sync(sp):
        attention_done(sp)
        for e in range(0, EXPERTS, 2):
            sp.dma_start(w2[:, e:e + 2], W["w2"][e * HT:(e + 2) * HT].rearrange("(e m) p n -> p e m n", m=HT)
                         ).then_inc(w2_in, 16)
        sp.wait_ge(sent, 16 * TOPK * TT)

        def load(i, j):
            at_least(sp, x_tr, i - 3)
            sp.dma_start(rowin[:, j, :], xs[bass.ds(i * P, P), :]).then_inc(row_in[j], 16)

        def store(i, j):
            sp.wait_ge(y_done, i + 1)
            sp.dma_start(ys[bass.ds(i * P, P), :], y[:, j, :]).then_inc(y_stored[j], 16)

        by_tiles(sp, [(0, load), (3, store)])
        flat = out.rearrange("b s e -> (b s) e")
        for c in range(NC):
            sp.wait_ge(final, c + 1)
            full = min((c + 1) * 3, SHARE_T)
            sp.dma_start(flat[c * TC:full * P, :].rearrange("(t p) e -> p t e", p=P), normed[:, c * 3:full, :]
                         ).then_inc(out_done, 16)
        sp.dma_start(flat[SHARE_T * P:TOKENS, :], normed[0:TAIL, SHARE_T, :]).then_inc(out_done, 16)
        sp.wait_ge(out_done, 16 * (NC + 1))

    def program_pool(pool):
        pool.wait_ge(W["xs_set"], 16)
        pool.wait_ge(slot_done, 1)
        for t in range(TT):
            for k in range(TOPK):
                n = tile_rows(t)
                pool.indirect_dma_start(out=xs, out_offset=bass.IndirectOffsetOnAxis(ap=slot[0:n, k, t, None], axis=0),
                                        in_=normed[0:n, t, :], in_offset=None).then_inc(sent, 16)
        for j in range(4):
            pool.wait_ge(y_stored[j], 16 * (MT // 4))
        pool.wait_ge(rows_set, 1)
        for t in range(TT):
            for k in range(TOPK):
                n = tile_rows(t)
                pool.indirect_dma_start(out=back[0:n, t, k, :], out_offset=None, in_=ys,
                                        in_offset=bass.IndirectOffsetOnAxis(ap=slot[0:n, k, t, None], axis=0)
                                        ).then_inc(gathered[t], 16)
        for c in range(NC):
            pool.wait_ge(stat, 2 * (c + 1))
            inverse_root(pool, W, mv[:, c * 3:c * 3 + 3, 1:2], powed, 2 * c)

    def program_tensor(pe):
        attention_done(pe)
        pe.wait_ge(W["in"], W["in_n"])
        pe.wait_ge(counted, 1)
        pe.matmul(psum[:, 1, 0:(TT + 1) * EXPERTS], W["before"], both[:, :, :].rearrange("p t e -> p (t e)"),
                  start=True, stop=False)
        for ahead in range(TT):
            later = TT - ahead
            last = pe.matmul(psum[:, 1, (ahead + 1) * EXPERTS:(TT + 1) * EXPERTS].rearrange("p (t e) -> p t e", t=later),
                             W["all_ones"], both[:, ahead, None, :].to_broadcast([P, later, EXPERTS]),
                             start=False, stop=(ahead == TT - 1))
        last.then_inc(route_mm, 1)
        pe.wait_ge(cw_set, 1)
        for t in range(TT):
            last = pe.transpose(psum[0:EXPERTS, 3 + t // 4, t % 4 * P:(t % 4 + 1) * P], cw[:, t, :], W["identity"])
        last.then_inc(cw_tr, 1)
        for t in range(TT):
            if t == 0:
                pe.wait_ge(cwT_done, 3)
            at_least(pe, biased, t - 1)
            pe.matmul(psum[:, 6 + t % 2, 0:DIM], cwT[:, t * P:(t + 1) * P], W["b2"], start=True, stop=True
                      ).then_inc(b2_mm, 1)
        pe.wait_ge(biased, TT)
        pe.wait_ge(w2_in, 16 * EXPERTS // 2)
        pe.wait_ge(slot_done, 2)
        pe.wait_ge(rows_set, 1)

        def row_transposes(i, j):
            pe.wait_ge(row_in[j], i // 4 * 16 + 16)
            at_least(pe, rowT_done, 2 * i)
            for k in range(2):
                last = pe.transpose(psum[0:KH, 0, k * P:(k + 1) * P], rowin[:, j, k * KH:(k + 1) * KH], W["identity"])
            last.then_inc(x_tr, 1)

        def hidden(i, j):
            pe.wait_ge(rowT_done, 2 * (i + 1))
            pe.wait_ge(w1_set, i + 1)
            at_least(pe, g_done, 2 * (i - 1))
            for m in range(HT):
                for k in range(2):
                    last = pe.matmul(psum[:, 1 + j % 2 * 2 + m // 3, m % 3 * P:(m % 3 + 1) * P],
                                     w1_now[0:KH + k, j % 2, k, m * P:(m + 1) * P], rowT[0:KH + k, j % 2, k, :],
                                     start=(k == 0), stop=(k == 1))
                if m % 3 == 2:
                    last.then_inc(h_mm, 1)

        def results(i, j):
            e = expert_of(i, mybir.EngineType.PE)
            pe.wait_ge(g_done, 2 * (i + 1))
            at_least(pe, y_done, i - 1)
            for m in range(HT):
                last = pe.matmul(psum[:, 6 + j % 2, 0:DIM], hT[:, j % 2, m * P:(m + 1) * P],
                                 w2[:, bass.ds(e, 1), m, :].rearrange("p a n -> p (a n)"),
                                 start=(m == 0), stop=(m == HT - 1))
            last.then_inc(y_mm, 1)

        by_tiles(pe, [(0, row_transposes), (1, hidden), (2, results)])

    def program_scalar(act):
        act.wait_ge(route, 3)
        act.activation(e21[:, :], e21[:, :], ACT.Exp).then_inc(e_done, 1)
        act.wait_ge(cw_tr, 1)
        for b in range(3):
            n = min(4, TT - 4 * b) * P
            act.activation(cwT[:, b * 4 * P:b * 4 * P + n], psum[0:EXPERTS, 3 + b, 0:n], ACT.Copy).then_inc(cwT_done, 1)

        def copy_rowT(i, j):
            act.wait_ge(x_tr, i + 1)
            at_least(act, h_mm, 2 * (i - 1))
            for k in range(2):
                act.activation(rowT[0:KH, j % 2, k, :], psum[0:KH, 0, k * P:(k + 1) * P], ACT.Identity,
                               scale=W["g2"][:, k:k + 1], bias=W["be2"][:, k:k + 1]).then_inc(rowT_done, 1)

        def gelu(i, j):
            at_least(act, y_mm, i - 1)
            for m in range(HALVES):
                act.wait_ge(h_mm, 2 * i + m + 1)
                act.activation(hT[:, j % 2, m * TC:(m + 1) * TC], psum[:, 1 + j % 2 * 2 + m, 0:TC], ACT.Gelu
                               ).then_inc(g_done, 1)

        by_tiles(act, [(0, copy_rowT), (1, gelu)])

    def program_vector(dve):
        attention_done(dve)
        dve.wait_ge(W["in"], W["in_n"])
        dve.memset(rowT[KH:KH + 1], 1.0)
        dve.memset(back[:, SHARE_T], 0.0).then_inc(rows_set, 1)
        c = Chain(dve, route, ROUTE_MARKS)
        c.begin(0)
        dve.wait_ge(W["logits_mm"], NC)
        c.did(dve.tensor_tensor(logits[:, :, :], psum[:, 2, 0:TT * EXPERTS].rearrange("p (t e) -> p t e", t=TT),
                                W["gate_b"][:, None, :].to_broadcast([P, TT, EXPERTS]), ALU.add))
        c.wait()
        for t in range(TT):
            last = dve.max(top[:, t, :], logits[:, t, :])
        c.did(last)
        c.wait()
        c.did(dve.tensor_tensor(e21[:, :], top[:, :, 1], top[:, :, 0], ALU.subtract))
        for t in range(TT):
            last = dve.max_index(topi[:, t, :], top[:, t, :], logits[:, t, :])
        c.did(last)
        c.wait()
        c.did(dve.tensor_copy(topf[:, :, :], topi[:, :, 0:TOPK]))
        c.wait()
        for k in range(TOPK):
            last = dve.tensor_tensor(pick[:, k], W["iota"][:, None, 0:EXPERTS].to_broadcast([P, TT, EXPERTS]),
                                     topf[:, :, k, None].to_broadcast([P, TT, EXPERTS]), ALU.is_equal)
        c.did(last)
        c.wait()
        c.did(dve.tensor_tensor(both[:, 0:TT, :], pick[:, 0], pick[:, 1], ALU.add))
        c.wait()
        dve.memset(both[:, TT, :], 0.0)
        dve.memset(both[TAIL:P, SHARE_T, :], 0.0).then_inc(counted, 1)
        dve.wait_ge(e_done, 1)
        c.did(dve.tensor_scalar(den[:, :], e21[:, :], 1.0, None, ALU.add))
        c.wait()
        c.did(dve.reciprocal(share[:, :, 0], den[:, :]))
        c.wait()
        c.did(dve.tensor_tensor(share[:, :, 1], e21[:, :], share[:, :, 0], ALU.mult))
        dve.wait_ge(route_mm, 1)
        c.did(dve.tensor_copy(count[:, :], psum[:, 1, TT * EXPERTS:(TT + 1) * EXPERTS]))
        c.wait()
        c.did(dve.tensor_tensor(over[:, :, :], count[:, :, None].to_broadcast([P, EXPERTS, TT]),
                                W["multiples"][:, None, :].to_broadcast([P, EXPERTS, TT]), ALU.is_gt))
        c.wait()
        c.did(dve.tensor_reduce(tiles[:, :], over[:, :, :], AX_X, ALU.add))
        c.wait()
        c.did(dve.tensor_tensor(upto[:, :, :], tiles[:, None, :].to_broadcast([P, EXPERTS, EXPERTS]), W["not_past"],
                                ALU.mult))
        c.wait()
        c.did(dve.tensor_reduce(end[:, :], upto[:, :, :], AX_X, ALU.add))
        c.wait()
        dve.tensor_tensor(start[:, :], end[:, :], tiles[:, :], ALU.subtract).then_inc(sh, 1)
        dve.tensor_tensor(past[:, :, :], end[0:1, None, :].to_broadcast([1, MT, EXPERTS]),
                          W["iota"][0:1, 0:MT, None].to_broadcast([1, MT, EXPERTS]), ALU.is_le).then_inc(sh, 1)
        dve.wait_ge(sh, 2)
        dve.tensor_reduce(tile_f[:, :], past[:, :, :], AX_X, ALU.add).then_inc(sh, 1)
        dve.scalar_tensor_tensor(out=place[:, :, :], in0=start[:, None, :].to_broadcast([P, TT, EXPERTS]),
                                 scalar=float(P), in1=psum[:, 1, 0:TT * EXPERTS].rearrange("p (t e) -> p t e", t=TT),
                                 op0=ALU.mult, op1=ALU.add).then_inc(sh, 1)
        dve.wait_ge(sh, 4)
        dve.tensor_scalar(tile_f[:, :], tile_f[:, :], float(EXPERTS - 1), None, ALU.min).then_inc(sh, 1)
        for k in range(TOPK):
            dve.tensor_tensor(picked[:, k], pick[:, k], place[:, :, :], ALU.mult).then_inc(sh, 1)
        dve.wait_ge(sh, 5 + TOPK)
        dve.tensor_reduce(slot_f[:, :, :], picked[:, :, :, :], AX_X, ALU.add).then_inc(sh, 1)
        dve.wait_ge(sh, 6 + TOPK)
        c.did(dve.tensor_copy(slot[:, :, :], slot_f[:, :, :]))
        c.wait()
        dve.sem_inc(slot_done, 1)
        dve.tensor_copy(tile_expert[:, :], tile_f[:, :]).then_inc(slot_done, 1)
        c.end()
        for k in range(TOPK):
            dve.tensor_tensor(picked[:, k], pick[:, k], share[:, :, k, None].to_broadcast([P, TT, EXPERTS]),
                              ALU.mult).then_inc(sh, 1)
        dve.wait_ge(sh, 6 + 2 * TOPK)
        dve.tensor_tensor(cw[:, :, :], picked[:, 0], picked[:, 1], ALU.add).then_inc(cw_set, 1)
        for t in range(TT):
            dve.wait_ge(b2_mm, t + 1)
            dve.tensor_tensor(x_all[:, t, :], psum[:, 6 + t % 2, 0:DIM], x_all[:, t, :], ALU.add).then_inc(biased, 1)

        dve.wait_ge(slot_done, 2)

        def place_w1(i, j):
            e = expert_of(i, mybir.EngineType.DVE)
            at_least(dve, h_mm, 2 * (i - 1))
            dve.tensor_copy(w1_now[:, j % 2, None], w1[:, bass.ds(e, 1)]).then_inc(w1_set, 1)

        def copy_y(i, j):
            dve.wait_ge(y_mm, i + 1)
            at_least(dve, y_stored[j], i // 4 * 16)
            dve.tensor_copy(y[:, j, :], psum[:, 6 + j % 2, 0:DIM]).then_inc(y_done, 1)

        by_tiles(dve, [(0, place_w1), (2, copy_y)])

        for c in range(NC + 1):
            if c < NC:
                for t in range(c * 3, c * 3 + 3):
                    dve.wait_ge(gathered[t], 16 * TOPK)
                    for k in range(TOPK):
                        dve.scalar_tensor_tensor(out=x_all[:, t, :], in0=back[:, t, k, :], scalar=share[:, t, k:k + 1],
                                                 in1=x_all[:, t, :], op0=ALU.mult, op1=ALU.add).then_inc(summed, 1)
                        dve.wait_ge(summed, t * TOPK + k + 1)
                statistics(dve, c, x_all, st, mv, stat)
            if c >= 1:
                normalise(dve, c - 1, x_all, mv, normed, powed, final)

    sh = S("sh")
    return program_sync, program_pool, program_tensor, program_scalar, program_vector


INPUTS = ["dft", "rank_row", "ring_pos", "cls_pos", "masks", "identity", "own", "before", "all_ones", "iota",
          "multiples", "not_past", "x", "cls", "w_tok", "b_tok",
          "wqk0", "wv0", "bqk0", "bv0", "wp0", "bp0", "wqk1", "wv1", "wp1", "bp1",
          "g1", "be1", "g2", "be2", "gate", "gate_b", "w1", "b1", "w2", "b2"]


def build(nc, a, out):
    dram = lambda name, rows, cols: nc.dram_tensor(name, (rows, cols), F32, kind="Internal").ap()
    table = dram("power_table", ROWS, IMGS)
    raw = dram("ring_tokens", TOKENS, DIM)
    xs = dram("expert_inputs", MT * P, DIM)
    ys = dram("expert_outputs", MT * P, DIM)
    with ExitStack() as ctx:
        sem = lambda name: ctx.enter_context(nc.semaphore(name))
        rank_row = ctx.enter_context(nc.sbuf_tensor("rank_row", [P, 2, 2 * CHUNKS], I32))
        index_in = [sem(f"index_in{i}") for i in range(2)]
        with ExitStack() as first:
            *spec, stored, root_done = spectrum(nc, first, sem, a["x"], table, a["dft"])

        def spectrum_done(eng):
            eng.wait_ge(root_done, GROUPS)
            for s in stored[:-1]:
                eng.wait_ge(s, STORES)
            eng.wait_ge(stored[-1], 32)

        sb = lambda n, shape, dt=F32: ctx.enter_context(nc.sbuf_tensor(n, shape, dt))
        psum = ctx.enter_context(nc.psum_tensor("psum", [P, 8, 512], F32))
        minus_half = sb("minus_half", [P, 1])
        zeros = sb("zeros", [P, DIM])
        x_all = sb("x_all", [P, TT, DIM])
        half_set, ones_set, zeros_set, pad_set, v_pad_set, loaded, xs_set = (
            sem("half_set"), sem("ones_set"), sem("zeros_set"), sem("pad_set"), sem("v_pad_set"), sem("loaded"), sem("xs_set"))
        shared = {"psum": psum, "minus_half": minus_half[:, :], "half_set": half_set, "ones_set": ones_set,
                  "pad_set": pad_set, "v_pad_set": v_pad_set, "in": loaded,
                  "tT": sb("tT", [KH, 2, TPAD]), "normed": sb("normed", [P, TT, DIM]), "z": sb("z", [P, TT, DIM])}
        xT, qk = sb("xT", [KH + 1, 2, TPAD]), sb("qk", [KH, 4, TPAD])
        shared.update(xT=xT, qk=qk, qk_out=sem("qk_out"))
        loads = []

        def constant(name, shape, *, source=None, broadcast=False):
            buf = sb(f"c_{name}", shape)
            src = a[source or name]
            loads.append((buf[:], src.to_broadcast(shape) if broadcast else src))
            return buf[:]

        for name, shape in (("identity", [P, P]), ("own", [KH, HPH]), ("before", [P, P]), ("all_ones", [P, P]),
                            ("iota", [P, MT]), ("multiples", [P, TT]), ("not_past", [P, EXPERTS, EXPERTS])):
            shared[name] = constant(name, shape)
        masks = constant("masks", [TG, 2, TG])
        layers = []
        for l in range(2):
            w = dict(shared, mask=masks[:, l, :])
            for n, rows, cols in (("wqk", KH, 2 * DIM), ("wv", KH, DIM), ("wp", KH + 1, DIM)):
                w[n] = sb(f"c_{n}{l}", [rows, 2, cols])[:]
                loads.append((w[n][0:KH], a[f"{n}{l}"].rearrange("(h p) e -> p h e", h=2)))
            loads.append((w["wp"][KH:KH + 1, 1, :], a[f"bp{l}"]))
            layers.append(w)
        layers[0]["bqk"] = constant("bqk0", [KH, 4])
        layers[0]["bv"] = constant("bv0", [TG, DIM], broadcast=True)
        for key, name in (("g1", "g1"), ("b1", "be1"), ("g2", "g2"), ("b2", "be2")):
            layers[1][key] = constant(name, [KH, 2])
        gate = sb("c_gate", [KH, 2, EXPERTS])[:]
        loads.append((gate, a["gate"].rearrange("(h p) e -> p h e", h=2)))
        w1_buf = sb("c_w1", [KH + 1, EXPERTS, 2, HIDDEN])
        unused_row = w1_buf[KH:KH + 1, :, 0, :]
        for e in range(EXPERTS):
            loads.append((w1_buf[0:KH, e], a["w1"][e * 2:(e + 1) * 2].rearrange("h p n -> p h n")))
        loads.append((w1_buf[KH:KH + 1, :, 1, :], a["b1"]))
        layers[1]["gate"], shared["logits_mm"] = gate, sem("logits_mm")
        layers[1]["logits_mm"] = shared["logits_mm"]
        layers[0]["xin_done"] = layers[1]["xin_done"] = sem("xin_done")
        moe = dict(shared, gate_b=constant("gate_b", [P, EXPERTS], broadcast=True), w1_buf=w1_buf,
                   b2=constant("b2", [EXPERTS, DIM]), g2=layers[1]["g2"], be2=layers[1]["b2"],
                   w2=a["w2"], xs_set=xs_set)
        for w in layers + [moe]:
            w["in_n"] = 16 * len(loads)

        with ExitStack() as second:
            rings = tokens_of_rings(nc, second, sem, rank_row, index_in, a, table, raw, layers[0], xT, qk, spectrum_done)
        rings_done, rings_in = rings[-2:]
        with ExitStack() as third:
            bufs = attention_buffers(lambda n, shape: third.enter_context(nc.sbuf_tensor(n, shape, F32)))
        att0 = attention(sem, "a0", layers[0], bufs, 0, raw, x_all, rings_done)
        att1 = attention(sem, "a1", layers[1], bufs, 1, raw, x_all, att0[-1])
        moe_p = experts(nc, ctx, sem, moe, x_all, xs, ys, out, att1[-1])
        block = ctx.enter_context(nc.Block())

        @block.sync
        def _(sp):
            for q in range(2):
                sp.dma_start(rank_row[:, q, :], a["rank_row"][:, q * 2 * CHUNKS:(q + 1) * 2 * CHUNKS]
                             ).then_inc(index_in[q], 16)
            spec[0](sp)
            rings[0](sp)
            att0[0](sp)
            moe_p[0](sp)

        @block.gpsimd
        def _(pool):
            spec[1](pool)
            rings[1](pool)
            rings_done(pool)
            att0[1](pool)
            att0[-1](pool)
            att1[1](pool)
            moe_p[1](pool)

        @block.tensor
        def _(pe):
            spec[2](pe)
            spectrum_done(pe)
            rings[2](pe)
            att0[2](pe)
            att0[-1](pe)
            att1[2](pe)
            moe_p[2](pe)

        @block.scalar
        def _(act):
            spec[3](act)
            spectrum_done(act)
            act.wait_ge(rings_in, 16 * CHANNELS)
            for dst, src in loads:
                act.dma_start(dst, src).then_inc(loaded, 16)
            act.wait_ge(zeros_set, 1)
            act.dma_start(xs.rearrange("(t p) e -> p t e", p=P), zeros[:, None, :].to_broadcast([P, MT, DIM])
                          ).then_inc(xs_set, 16)
            rings[3](act)
            rings_done(act)
            att0[3](act)
            att0[-1](act)
            att1[3](act)
            moe_p[3](act)

        @block.vector
        def _(dve):
            spec[4](dve)
            spectrum_done(dve)
            dve.memset(zeros[:, :], 0.0).then_inc(zeros_set, 1)
            dve.memset(minus_half[:, :], -0.5).then_inc(half_set, 1)
            dve.memset(xT[KH:KH + 1], 1.0).then_inc(ones_set, 1)
            dve.memset(unused_row, 0.0)
            dve.memset(xT[0:KH, :, TOKENS:TPAD], 0.0)
            dve.memset(qk[:, :, TOKENS:TPAD], 0.0)
            dve.memset(x_all[TAIL:P, TT - 1, :], 0.0).then_inc(pad_set, 1)
            rings[4](dve)
            rings_done(dve)
            dve.memset(bufs["v"][:], 0.0).then_inc(v_pad_set, 1)
            dve.wait_ge(v_pad_set, 1)
            att0[4](dve)
            att0[-1](dve)
            att1[4](dve)
            moe_p[4](dve)


def kernel(**inputs):
    import concourse.bacc as _bacc
    from concourse.bass_utils import run_bass_kernel_spmd as _run
    i = {n: np.asarray(v) for n, v in inputs.items()}
    x = np.roll(i["x"], (BATCH // 2, CHANNELS // 2), axis=(0, 1))
    x = x.transpose(2, 0, 1, 3).reshape(SIDE, IMGS, SIDE)
    x = np.concatenate([x[:, :, :HALF], x[:, :, :HALF - 1:-1]], 2)
    wa, wf, ba = i["L0_attn_W_attn"], i["L0_ffn_qkv_w"].T, i["L0_attn_b_attn"]
    arrays = dict(
        constants(),
        x=np.stack([x[:HALF], x[:HALF - 1:-1]]).reshape(2, HALF, IMGS * SIDE),
        cls=i["L0_tok_cls_token"].reshape(1, DIM), w_tok=i["L0_tok_W"].T, b_tok=i["L0_tok_b"][None],
        wqk0=wa[:, :2 * DIM], wv0=wa[:, 2 * DIM:], bqk0=ba[:2 * DIM].reshape(4, KH).T, bv0=ba[None, 2 * DIM:],
        wp0=i["L0_attn_W_proj"], bp0=i["L0_attn_b_proj"][None],
        wqk1=wf[:, :2 * DIM], wv1=wf[:, 2 * DIM:], wp1=i["L0_ffn_proj_w"].T, bp1=i["L0_ffn_proj_b"][None],
        g1=i["L0_ffn_ln1_g"].reshape(2, KH).T, be1=i["L0_ffn_ln1_b"].reshape(2, KH).T,
        g2=i["L0_ffn_ln2_g"].reshape(2, KH).T, be2=i["L0_ffn_ln2_b"].reshape(2, KH).T,
        gate=i["L0_ffn_gate_w"].T, gate_b=i["L0_ffn_gate_b"][None],
        w1=i["L0_ffn_w1"].transpose(0, 2, 1).reshape(EXPERTS * 2, KH, HIDDEN),
        b1=i["L0_ffn_b1"][None],
        w2=i["L0_ffn_w2"].transpose(0, 2, 1).reshape(EXPERTS * HT, P, DIM), b2=i["L0_ffn_b2"])
    nc = _bacc.Bacc("TRN2", target_bir_lowering=False, num_devices=1)
    feed, aps = {}, {}
    for n in INPUTS:
        v = np.ascontiguousarray(arrays[n])
        feed[f"in_{n}"] = v
        aps[n] = nc.dram_tensor(f"in_{n}", v.shape, mybir.dt.from_np(v.dtype), kind="ExternalInput").ap()
    out = nc.dram_tensor("out_0", (BATCH, SEQ, DIM), F32, kind="ExternalOutput").ap()
    build(nc, aps, out)
    return _run(nc, [feed], core_ids=[0]).results[0]["out_0"]
```
